# Optimizing a Trainium2 kernel written in Bass

```python
import numpy as np
import jax
import jax.numpy as jnp

def _softmax(x, axis=-1):
    return jax.nn.softmax(x, axis=axis)

def _gelu(x):
    return jax.nn.gelu(x, approximate=True)

def _silu(x):
    return jax.nn.silu(x)

def _sigmoid(x):
    return jax.nn.sigmoid(x)

def _layernorm(x, axis=-1, eps=1e-05):
    m = jnp.mean(x, axis=axis, keepdims=True)
    v = jnp.var(x, axis=axis, keepdims=True)
    return (x - m) / jnp.sqrt(v + eps)

def _scatter_add(tgt, idx, src, axis=0):
    return tgt.at[idx].add(src)

def _segment_sum(src, seg, n):
    return jax.ops.segment_sum(src, seg, n)
kernel_name = 'mk_vit_tower_d1_tok_img768_r4_bcff3e'

def setup_inputs(seed: int=0):
    np.random.seed(seed)
    _w = jnp.asarray

    def _rec_inputs():
        import jax
        import jax.numpy as jnp
        _rk = jax.random.key(seed)
        x = -0.00016672 + 0.999947 * jax.random.normal(jax.random.fold_in(_rk, 1), (128, 3, 224, 224), jnp.float32)
        return x
    x = _rec_inputs()

    def _L0_tok_setup():
        import jax, jax.numpy as jnp
        import numpy as np
        PATCH = (16, 16)
        EPS = 1e-05

        def img2patches(x, ph, pw):
            B, C, H, W = x.shape
            h, w = (H // ph, W // pw)
            x = x.reshape(B, C, h, ph, w, pw)
            x = x.transpose(0, 2, 4, 3, 5, 1)
            return x.reshape(B, h * w, ph * pw * C)

        def layernorm(x, g, b):
            mu = jnp.mean(x, axis=-1, keepdims=True)
            var = jnp.mean(jnp.square(x - mu), axis=-1, keepdims=True)
            return (x - mu) * jax.lax.rsqrt(var + EPS) * g + b
        key = jax.random.key(seed)
        ks = jax.random.split(key, 7)
        B, C, H, W_ = (64, 3, 96, 96)
        patch_dim = PATCH[0] * PATCH[1] * C
        model_dim = 192
        return {'x': jax.random.normal(ks[0], (B, C, H, W_), dtype=jnp.float32), 'ln1_g': jax.random.uniform(ks[1], (patch_dim,), dtype=jnp.float32), 'ln1_b': jax.random.normal(ks[2], (patch_dim,), dtype=jnp.float32) * 0.02, 'W': jax.random.normal(ks[3], (patch_dim, model_dim), dtype=jnp.float32) * (1.0 / np.sqrt(patch_dim)), 'b': jax.random.normal(ks[4], (model_dim,), dtype=jnp.float32) * 0.02, 'ln2_g': jax.random.uniform(ks[5], (model_dim,), dtype=jnp.float32), 'ln2_b': jax.random.normal(ks[6], (model_dim,), dtype=jnp.float32) * 0.02}
    _L0_tok_all = _L0_tok_setup()
    _L0_tok_in = {k: v for k, v in _L0_tok_all.items() if k in ('ln1_g', 'ln1_b', 'W', 'b', 'ln2_g', 'ln2_b')}
    del _L0_tok_all

    def _L0_attn_setup():
        import jax, jax.numpy as jnp
        import numpy as np
        N_HEAD = 12
        key = jax.random.key(seed)
        ks = jax.random.split(key, 6)
        B, T, C = (8, 256, 192)
        x = jax.random.normal(ks[0], (B, T, C), dtype=jnp.float32)
        w_attn = jax.random.normal(ks[1], (C, 3 * C), dtype=jnp.float32) * 0.02
        b_attn = jnp.zeros((3 * C,), dtype=jnp.float32)
        w_proj = jax.random.normal(ks[2], (C, C), dtype=jnp.float32) * 0.02
        b_proj = jnp.zeros((C,), dtype=jnp.float32)
        rel_emb = jax.random.normal(ks[3], (2 * 256 - 1, C // N_HEAD), dtype=jnp.float32) * 0.02
        return {'x': x, 'w_attn': w_attn, 'b_attn': b_attn, 'w_proj': w_proj, 'b_proj': b_proj, 'rel_emb': rel_emb}
    _L0_attn_all = _L0_attn_setup()
    _L0_attn_in = {k: v for k, v in _L0_attn_all.items() if k in ('w_attn', 'b_attn', 'w_proj', 'b_proj', 'rel_emb')}
    del _L0_attn_all

    def _L0_ffn_setup():
        import jax, jax.numpy as jnp
        import numpy as np
        B, L, D, H, F = (4, 512, 192, 12, 768)
        ROUTE_FRAC = 0.15
        LN_EPS = 1e-05

        def _ln(x, g, b):
            m = jnp.mean(x, axis=-1, keepdims=True)
            v = jnp.mean((x - m) ** 2, axis=-1, keepdims=True)
            return (x - m) * jax.lax.rsqrt(v + LN_EPS) * g + b
        key = jax.random.key(seed)
        ks = jax.random.split(key, 20)
        s = 0.02
        return {'hidden_states': jax.random.normal(ks[0], (B, L, D), dtype=jnp.float32), 'g1': jnp.ones((D,), jnp.float32), 'b1': jnp.zeros((D,), jnp.float32), 'g2': jnp.ones((D,), jnp.float32), 'b2': jnp.zeros((D,), jnp.float32), 'Wr': jax.random.normal(ks[1], (D,), jnp.float32) * s, 'br': jnp.zeros((), jnp.float32), 'Wq': jax.random.normal(ks[2], (D, D), jnp.float32) * s, 'bq': jnp.zeros((D,), jnp.float32), 'Wk': jax.random.normal(ks[3], (D, D), jnp.float32) * s, 'bk': jnp.zeros((D,), jnp.float32), 'Wv': jax.random.normal(ks[4], (D, D), jnp.float32) * s, 'bv': jnp.zeros((D,), jnp.float32), 'Wo': jax.random.normal(ks[5], (D, D), jnp.float32) * s, 'bo': jnp.zeros((D,), jnp.float32), 'Wm': jax.random.normal(ks[6], (D, D), jnp.float32) * s, 'bm': jnp.zeros((D,), jnp.float32), 'W1': jax.random.normal(ks[7], (D, F), jnp.float32) * s, 'bf1': jnp.zeros((F,), jnp.float32), 'W2': jax.random.normal(ks[8], (F, D), jnp.float32) * s, 'bf2': jnp.zeros((D,), jnp.float32)}
    _L0_ffn_all = _L0_ffn_setup()
    _L0_ffn_in = {k: v for k, v in _L0_ffn_all.items() if k in ('g1', 'b1', 'g2', 'b2', 'Wr', 'br', 'Wq', 'bq', 'Wk', 'bk', 'Wv', 'bv', 'Wo', 'bo', 'Wm', 'bm', 'W1', 'bf1', 'W2', 'bf2')}
    del _L0_ffn_all
    return {'x': x, 'L0_tok_ln1_g': _L0_tok_in['ln1_g'], 'L0_tok_ln1_b': _L0_tok_in['ln1_b'], 'L0_tok_W': _L0_tok_in['W'], 'L0_tok_b': _L0_tok_in['b'], 'L0_tok_ln2_g': _L0_tok_in['ln2_g'], 'L0_tok_ln2_b': _L0_tok_in['ln2_b'], 'L0_attn_w_attn': _L0_attn_in['w_attn'], 'L0_attn_b_attn': _L0_attn_in['b_attn'], 'L0_attn_w_proj': _L0_attn_in['w_proj'], 'L0_attn_b_proj': _L0_attn_in['b_proj'], 'L0_attn_rel_emb': _L0_attn_in['rel_emb'], 'L0_ffn_g1': _L0_ffn_in['g1'], 'L0_ffn_b1': _L0_ffn_in['b1'], 'L0_ffn_g2': _L0_ffn_in['g2'], 'L0_ffn_b2': _L0_ffn_in['b2'], 'L0_ffn_Wr': _L0_ffn_in['Wr'], 'L0_ffn_br': _L0_ffn_in['br'], 'L0_ffn_Wq': _L0_ffn_in['Wq'], 'L0_ffn_bq': _L0_ffn_in['bq'], 'L0_ffn_Wk': _L0_ffn_in['Wk'], 'L0_ffn_bk': _L0_ffn_in['bk'], 'L0_ffn_Wv': _L0_ffn_in['Wv'], 'L0_ffn_bv': _L0_ffn_in['bv'], 'L0_ffn_Wo': _L0_ffn_in['Wo'], 'L0_ffn_bo': _L0_ffn_in['bo'], 'L0_ffn_Wm': _L0_ffn_in['Wm'], 'L0_ffn_bm': _L0_ffn_in['bm'], 'L0_ffn_W1': _L0_ffn_in['W1'], 'L0_ffn_bf1': _L0_ffn_in['bf1'], 'L0_ffn_W2': _L0_ffn_in['W2'], 'L0_ffn_bf2': _L0_ffn_in['bf2']}

def reference(x, L0_tok_ln1_g, L0_tok_ln1_b, L0_tok_W, L0_tok_b, L0_tok_ln2_g, L0_tok_ln2_b, L0_attn_w_attn, L0_attn_b_attn, L0_attn_w_proj, L0_attn_b_proj, L0_attn_rel_emb, L0_ffn_g1, L0_ffn_b1, L0_ffn_g2, L0_ffn_b2, L0_ffn_Wr, L0_ffn_br, L0_ffn_Wq, L0_ffn_bq, L0_ffn_Wk, L0_ffn_bk, L0_ffn_Wv, L0_ffn_bv, L0_ffn_Wo, L0_ffn_bo, L0_ffn_Wm, L0_ffn_bm, L0_ffn_W1, L0_ffn_bf1, L0_ffn_W2, L0_ffn_bf2):
    import jax
    import jax.numpy as jnp

    def _L0_tok_ref(x, ln1_g, ln1_b, W, b, ln2_g, ln2_b):
        import jax, jax.numpy as jnp
        import numpy as np
        PATCH = (16, 16)
        EPS = 1e-05

        def img2patches(x, ph, pw):
            B, C, H, W = x.shape
            h, w = (H // ph, W // pw)
            x = x.reshape(B, C, h, ph, w, pw)
            x = x.transpose(0, 2, 4, 3, 5, 1)
            return x.reshape(B, h * w, ph * pw * C)

        def layernorm(x, g, b):
            mu = jnp.mean(x, axis=-1, keepdims=True)
            var = jnp.mean(jnp.square(x - mu), axis=-1, keepdims=True)
            return (x - mu) * jax.lax.rsqrt(var + EPS) * g + b
        p = img2patches(x, PATCH[0], PATCH[1])
        h = layernorm(p, ln1_g, ln1_b)
        h = jnp.einsum('bsd,dm->bsm', h, W) + b
        return layernorm(h, ln2_g, ln2_b)

    def _L0_attn_ref(x, w_attn, b_attn, w_proj, b_proj, rel_emb):
        import jax, jax.numpy as jnp
        import numpy as np
        N_HEAD = 12
        b, t, c = x.shape
        h = N_HEAD
        d = c // h
        scale = d ** (-0.5)
        qkv = x @ w_attn + b_attn
        q, k, v = jnp.split(qkv, 3, axis=-1)
        split_heads = lambda z: z.reshape(b, t, h, d).transpose(0, 2, 1, 3)
        q, k, v = map(split_heads, (q, k, v))
        q = q * scale
        scores = jnp.einsum('bhid,bhjd->bhij', q, k)
        rel = rel_emb[:t]
        rel = jnp.concatenate([jnp.zeros_like(rel[:1]), rel], axis=0)[:-1]
        scores = scores + jnp.einsum('bhid,jd->bhij', q, rel)
        causal = jnp.tril(jnp.ones((t, t), dtype=bool))
        scores = jnp.where(causal, scores, -jnp.inf)
        probs = jax.nn.softmax(scores, axis=-1)
        y = jnp.einsum('bhij,bhjd->bhid', probs, v)
        y = y.transpose(0, 2, 1, 3).reshape(b, t, c)
        return y @ w_proj + b_proj

    def _L0_ffn_ref(hidden_states, g1, b1, g2, b2, Wr, br, Wq, bq, Wk, bk, Wv, bv, Wo, bo, Wm, bm, W1, bf1, W2, bf2):
        import jax, jax.numpy as jnp
        import numpy as np
        B, L, D, H, F = (4, 512, 192, 12, 768)
        ROUTE_FRAC = 0.15
        LN_EPS = 1e-05

        def _ln(x, g, b):
            m = jnp.mean(x, axis=-1, keepdims=True)
            v = jnp.mean((x - m) ** 2, axis=-1, keepdims=True)
            return (x - m) * jax.lax.rsqrt(v + LN_EPS) * g + b
        b, l, d = hidden_states.shape
        dh = d // H
        normed = _ln(hidden_states, g1, b1)
        scores = jax.nn.sigmoid(jnp.einsum('bld,d->bl', normed, Wr) + br)
        k = max(1, int(round(ROUTE_FRAC * l)))
        _, idx = jax.lax.top_k(-scores, k)
        attn_mask = jnp.zeros((b, l), bool).at[jnp.arange(b)[:, None], idx].set(True)
        q = (normed @ Wq + bq).reshape(b, l, H, dh)
        kk = (normed @ Wk + bk).reshape(b, l, H, dh)
        v = (normed @ Wv + bv).reshape(b, l, H, dh)
        logits = jnp.einsum('blhd,bmhd->bhlm', q, kk) / jnp.sqrt(jnp.float32(dh))
        probs = jax.nn.softmax(logits, axis=-1)
        ctx = jnp.einsum('bhlm,bmhd->blhd', probs, v).reshape(b, l, d)
        attn_out = ctx @ Wo + bo
        w = scores / (jnp.sum(scores, axis=1, keepdims=True) + 1e-06)
        pooled = jnp.einsum('bl,bld->bd', w, normed)
        mix_out = (normed + scores[..., None] * pooled[:, None, :]) @ Wm + bm
        merged = jnp.where(attn_mask[..., None], attn_out, mix_out)
        h = hidden_states + merged
        n2 = _ln(h, g2, b2)
        ffn = jax.nn.gelu(n2 @ W1 + bf1, approximate=False) @ W2 + bf2
        return h + ffn
    h = _L0_tok_ref(x, L0_tok_ln1_g, L0_tok_ln1_b, L0_tok_W, L0_tok_b, L0_tok_ln2_g, L0_tok_ln2_b)
    h = h + _L0_attn_ref(_layernorm(h, axis=-1), L0_attn_w_attn, L0_attn_b_attn, L0_attn_w_proj, L0_attn_b_proj, L0_attn_rel_emb)
    h = h + _L0_ffn_ref(_layernorm(h, axis=-1), L0_ffn_g1, L0_ffn_b1, L0_ffn_g2, L0_ffn_b2, L0_ffn_Wr, L0_ffn_br, L0_ffn_Wq, L0_ffn_bq, L0_ffn_Wk, L0_ffn_bk, L0_ffn_Wv, L0_ffn_bv, L0_ffn_Wo, L0_ffn_bo, L0_ffn_Wm, L0_ffn_bm, L0_ffn_W1, L0_ffn_bf1, L0_ffn_W2, L0_ffn_bf2)
    return h

_drawn_inputs = setup_inputs


def setup_inputs(seed=0):
    import zlib

    import numpy as np

    out = dict(_drawn_inputs(seed))
    spreads = {'L0_attn_b_attn': (0.0, 0.1),
     'L0_attn_b_proj': (0.0, 0.1),
     'L0_ffn_g1': (1.0, 0.2),
     'L0_ffn_b1': (0.0, 0.341),
     'L0_ffn_g2': (1.0, 0.6),
     'L0_ffn_b2': (0.0, 0.8),
     'L0_ffn_bq': (0.0, 0.8),
     'L0_ffn_bk': (0.0, 2.0),
     'L0_ffn_bv': (0.0, 0.8),
     'L0_ffn_bo': (0.0, 0.328),
     'L0_ffn_bm': (0.0, 0.1),
     'L0_ffn_bf1': (0.0, 0.418),
     'L0_ffn_bf2': (0.0, 0.1)}
    factors = {'L0_attn_rel_emb': 27.947,
     'L0_ffn_Wq': 8.0,
     'L0_ffn_Wk': 8.0,
     'L0_ffn_Wv': 8.0,
     'L0_ffn_Wo': 8.0}
    for name, (base, spread) in spreads.items():
        noise = np.random.default_rng([zlib.crc32(name.encode()), seed]).standard_normal(out[name].shape)
        drawn = base * np.exp(spread * noise) if base else spread * noise
        out[name] = jnp.asarray(drawn.astype(out[name].dtype))
    for name, factor in factors.items():
        out[name] = (out[name] * factor).astype(out[name].dtype)
    return out
```

```python
from contextlib import ExitStack

import concourse.bass as bass
from concourse import mybir

F32 = mybir.dt.float32
BF16 = mybir.dt.bfloat16
ALU = mybir.AluOpType
ACT = mybir.ActivationFunctionType
AX = mybir.AxisListType

B, C, IMG = 128, 3, 224
PS = 16
GR = IMG // PS
T = GR * GR
HT = T // 2
PD = PS * PS * C
D = 192
NH, DH = 12, 16
F = 768
NSEL = max(1, int(round(0.15 * T)))
SELP = 32
EPS = 1e-5
QH = PS // 2
KX = 2 * C * PS
NEG = -1e30
KC = ((0, 128), (128, 192))
NG = 3
QSCALE = DH ** -0.5
TOPZ = 16.635532
ORDER = ["S0", "S1", "S2", "S3", "S4", "A0", "S5", "A1", "S6", "A2", "B0", "S7", "A3", "B1", "A4",
         "A5", "B2"]
NITEM = len(ORDER)

SEMS = dict(
    x_in=2 * C * 16, out_done=16,
    tok_mm=1, zT_mm=1, score_mm=1, kk_mm=1, vv_mm=1, aT_mm=1, q_mm=1, k_mm=1, v_mm=1,
    s_mm=8, p_T=9, y_mm=1, den_mm=1, proj_mm=1,
    gather_mm=1, qsel_mm=1, s2_mm=1, p2_T=1, ctx_mm=1, ctxT_mm=1, ao_mm=1, mix_mm=1,
    scat_mm=1, z3_T=1, up_mm=3, down_mm=1,
    sqsum_sb=1, tok_var=1, tok_y=1, y_stat=1, y_norm=1, h1_stat=1, a_sb=1, kT_sb=1, rowmax=8,
    pT_dve=5, yn_sb=1, h2_sb=1,
    h2_stat=1, z0_sb=1, f0_sb=1, z_sb=1, sel_sb=1, mT_sb=1, qb_sb=1, max2=1, ctx_sb=1, ctxT_sb=1, ao_sb=1,
    h3_sb=1, h3_stat=1, z3_sb=1, out_sb=1,
    sq_sb=1, aT_sb=1, qT_sb=1, v_sb=1, probs=8, pT_act=4, yT_sb=1,
    nT_sb=1, expz=1, kk_sb=1, vv_sb=1, nsel_sb=1, qs_sb=1, probs2=1, p2T_sb=1, n2T_sb=1, gelu_sb=3,
    tok_rstd=1, y_rstd=1, h1_sb=1, h1b_sb=1, h1_rstd=1, h2_rstd=1, res_sb=1, h3_rstd=1,
)


def s_unit(u):
    s, second = divmod(u, 2)
    if second:
        return s, [(0, 1, 0), (1, 1, T)]
    return s, [(0, 0, 0), (1, 0, HT), (2, 0, 2 * HT), (2, 1, 3 * HT)]


def build(nc, ins, out):
    W = dict(ins)
    with ExitStack() as ctx:
        ctx.enter_context(nc.allow_non_contiguous_dma(reason="small weights, once"))
        def sb(name, shape, dt=F32):
            return ctx.enter_context(nc.sbuf_tensor(name, shape, dt))

        sem = {name: ctx.enter_context(nc.semaphore(name)) for name in SEMS}
        one = {name: ctx.enter_context(nc.semaphore(name)) for name in
               ("w_in", "consts_made", "zeroed", "w_scaled", "w_sums", "w_ready")}
        bank = [ctx.enter_context(nc.psum_tensor(f"bank{i}", [128, 512], F32)) for i in range(8)]

        ident = sb("ident", [128, 128])
        identh = sb("identh", [HT, HT], BF16)
        tri = sb("tri", [HT, HT], BF16)
        before = sb("before", [HT, 2, T])
        notbefore = sb("notbefore", [HT, 2, T])
        slot_of = sb("slot_of", [128, 8])
        diag_of = sb("diag_of", [128, 4, DH])
        stack32 = sb("stack32", [128, SELP])
        den_sel = sb("den_sel", [128, 4, 32])
        iota32 = sb("iota32", [HT, SELP])
        ones = sb("ones", [128, 128])
        epsc = sb("epsc", [HT, 2])
        nhalf = sb("nhalf", [HT, 2])
        tokraw = sb("tokraw", [KX, QH, D])
        tokw = sb("tokw", [KX, QH, D + 1])
        tok_g = sb("tok_g", [KX, QH])
        tok_bb = sb("tok_bb", [KX, QH])
        tok_brep = sb("tok_brep", [KX, QH, HT])
        tok_bias = sb("tok_bias", [HT, D])
        tok_brow = sb("tok_brow", [HT, D])
        ln2g = sb("ln2g", [HT, D])
        ln2b = sb("ln2b", [HT, D])
        wq = sb("wq", [128, 2, NG * 128])
        wk = sb("wk", [128, 2, NG * 128])
        wv = sb("wv", [128, 2, D])
        bq = sb("bq", [128, NG])
        bqs = sb("bqs", [128, NG])
        bk = sb("bk", [128, NG])
        bv = sb("bv", [128, NG])
        bvrep = sb("bvrep", [128, NG, HT])
        relk = sb("relk", [128, NG, T])
        rel4 = sb("rel4", [HT, 2, 128])
        wp = sb("wp", [128, NG, D])
        bprow = sb("bprow", [HT, D])
        bp = sb("bp", [HT, D])
        g1 = sb("g1", [128, 2])
        b1 = sb("b1", [128, 2])
        g2 = sb("g2", [128, 2])
        b2 = sb("b2", [128, 2])
        wr = sb("wr", [128, 2])
        wrrep = sb("wrrep", [128, 2, 128])
        br = sb("br", [128, 1])
        fwq = sb("fwq", [128, 2, D])
        fwk = sb("fwk", [128, 2, D])
        fwv = sb("fwv", [128, 2, D])
        fwm = sb("fwm", [128, 2, D])
        fwo = sb("fwo", [128, 2, D])
        fbq = sb("fbq", [128, 2])
        fbqs = sb("fbqs", [128, 2])
        fbk = sb("fbk", [128, 2])
        fbv = sb("fbv", [128, 2])
        fbo = sb("fbo", [SELP, D])
        fbm = sb("fbm", [HT, D])
        w1 = sb("w1", [128, 2, F])
        bf1 = sb("bf1", [128, F // 128])
        w2 = sb("w2", [128, F // 128, D])
        bf2 = sb("bf2", [HT, D])
        x_sb = sb("x_sb", [KX, GR, IMG])
        x_sq = sb("x_sq", [KX, T, QH])
        sqsum = sb("sqsum", [KX, T])
        mean1 = sb("mean1", [HT, 2])
        msq1 = sb("msq1", [HT, 2])
        var1 = sb("var1", [HT, 2])
        ve1 = sb("ve1", [HT, 2])
        rstd1 = sb("rstd1", [HT, 2])
        y_row = sb("y_row", [HT, 2, D])
        bn_y = sb("bn_y", [HT, 2, 6])
        mv_y = sb("mv_y", [HT, 2, 2])
        ve2 = sb("ve2", [HT, 2])
        rstd2 = sb("rstd2", [HT, 2])
        yn_row = sb("yn_row", [HT, 2, D])
        h1g = sb("h1g", [HT, 2, D])
        h1 = sb("h1", [HT, 2, D])
        h1b = sb("h1b", [HT, 2, D])
        bn_a = sb("bn_a", [HT, 2, 6])
        mv_a = sb("mv_a", [HT, 2, 2])
        ve3 = sb("ve3", [HT, 2])
        rstd3 = sb("rstd3", [HT, 2])
        a_row = sb("a_row", [HT, 2, D])
        aT = sb("aT", [128, 2, T])
        qT = sb("qT", [128, NG, T])
        kT = sb("kT", [128, NG, T])
        v_sb = sb("v_sb", [HT, 2, NH, 32])
        negmax = sb("negmax", [HT, 2, NH])
        p0 = sb("p0", [HT, NH, HT])
        p1 = sb("p1", [HT, NH, T])
        pT0 = sb("pT0", [HT, NH, T])
        pT1 = sb("pT1", [HT, NH, HT])
        yT = sb("yT", [128, NG, T])
        rden = sb("rden", [128, NG, T])
        ynT = sb("ynT", [128, NG, T])
        h2 = sb("h2", [HT, 2, D])
        h2b = sb("h2b", [HT, 2, D])
        bn_f = sb("bn_f", [HT, 2, 6])
        mv_f = sb("mv_f", [HT, 2, 2])
        vf = sb("vf", [HT, 6, 2])
        f0 = sb("f0", [HT, 2, D])
        z0 = sb("z0", [HT, 2, D])
        nT = sb("nT", [128, 2, T])
        zrow = sb("zrow", [128, T])
        zclip = sb("zclip", [128, T])
        zi = sb("zi", [HT, 2])
        scr = sb("scr", [HT, 4, T])
        cnt = sb("cnt", [HT, 2, 2])
        rank = sb("rank", [HT, 2])
        keep = sb("keep", [HT, 2])
        sel = sb("sel", [HT, 2, SELP])
        ez = sb("ez", [128, T])
        ez1 = sb("ez1", [128, T])
        sig = sb("sig", [128, T])
        scr2 = sb("scr2", [128, 3, T])
        ssum = sb("ssum", [128, 1])
        sse = sb("sse", [128, 1])
        rss = sb("rss", [128, 1])
        pool_raw = sb("pool_raw", [128, 2])
        pooled = sb("pooled", [128, 2])
        mT = sb("mT", [128, 2, T])
        kk = sb("kk", [128, 2, T])
        vv = sb("vv", [HT, 2, D])
        nsel = sb("nsel", [128, 2, SELP])
        selT = sb("selT", [SELP, T])
        qs = sb("qs", [128, 2, SELP])
        qb0 = sb("qb0", [128, 8, SELP])
        qb1 = sb("qb1", [64, 4, SELP])
        negmax2 = sb("negmax2", [128, NG])
        probs2 = sb("probs2_", [128, NG, T])
        den2 = sb("den2", [128, NG])
        rden2 = sb("rden2", [128, NG])
        p2T = sb("p2T", [HT, 2, NG * 128])
        ctxm = sb("ctxm", [128, NG, 64])
        ctxT = sb("ctxT", [128, 2, SELP])
        ao = sb("ao", [SELP, D])
        mixb = sb("mixb", [HT, 2, D])
        f1 = sb("f1", [HT, 2, D])
        h3 = sb("h3", [HT, 2, D])
        res = sb("res", [HT, 2, D])
        bn_3 = sb("bn_3", [HT, 2, 6])
        mv_3 = sb("mv_3", [HT, 2, 2])
        ve5 = sb("ve5", [HT, 2])
        rstd5 = sb("rstd5", [HT, 2])
        z3 = sb("z3", [HT, 2, D])
        n2T = sb("n2T", [128, 2, T])
        gT = sb("gT", [128, F // 128, T])
        out_row = sb("out_row", [HT, 2, D])

        def cols(t, chunk):
            lo, hi = KC[chunk]
            return t[0:hi - lo, chunk]

        def after(name, image, j=None):
            k = SEMS[name]
            return image * k + (k if j is None else j)

        def all_before(name, image):
            return image * SEMS[name]

        def steps(eng, step):
            step(-1, 0, True, False, False)
            step(0, 1, True, True, False)
            with eng.Fori(1, B - 1) as m:
                step(m, m + 1, True, True, True)
            step(B - 1, B, False, True, True)

        def pt_done(i):
            k = sum(o[0] != "S" for o in ORDER[:i])
            return ("pT_dve", k // 2 + 1) if k % 2 == 0 else ("pT_act", k // 2 + 1)

        def pt_dst(kind, k):
            if kind == "A":
                return pT0[:, 2 * k:2 * k + 2].rearrange("p h t -> p (h t)")
            return pT1[:, 4 * k:4 * k + 4].rearrange("p h t -> p (h t)")

        block = ctx.enter_context(nc.Block())

        loads = []

        def load(dst, src):
            loads.append((dst, src))

        xh = W["x"].rearrange("b c (h p) w -> b c p h w", p=PS)

        def load_x(eng, image):
            for s in range(2):
                for c in range(C):
                    part = (s * C + c) * PS
                    eng.dma_start(x_sb[part:part + PS, :, 0:IMG - QH * s],
                                  xh[image, c, :, :, QH * s:IMG]).then_inc(sem["x_in"], 16)

        tw = W["L0_tok_W"].rearrange("(p s q c) m -> s c p q m", p=PS, s=2, q=QH)
        tg = W["L0_tok_ln1_g"].rearrange("(p s q c) -> s c p q", p=PS, s=2, q=QH)
        tb = W["L0_tok_ln1_b"].rearrange("(p s q c) -> s c p q", p=PS, s=2, q=QH)
        for s in range(2):
            for c in range(C):
                part = (s * C + c) * PS
                load(tokraw[part:part + PS], tw[s, c])
                load(tok_g[part:part + PS], tg[s, c])
                load(tok_bb[part:part + PS], tb[s, c])
        for dst, name, n in ((tok_brow, "L0_tok_b", HT), (ln2g, "L0_tok_ln2_g", HT),
                             (ln2b, "L0_tok_ln2_b", HT), (bprow, "L0_attn_b_proj", HT),
                             (fbo, "L0_ffn_bo", SELP), (fbm, "L0_ffn_bm", HT),
                             (bf2, "L0_ffn_bf2", HT)):
            load(dst[:], W[name].partition_broadcast(n))
        wa = W["L0_attn_w_attn"]
        for chunk, (lo, hi) in enumerate(KC):
            size = hi - lo
            for j, dst in enumerate((wq, wk)):
                load(dst[0:size, chunk].rearrange("p (h e) -> p h e", e=32)[:, :, 0:DH],
                     wa[lo:hi, j * D:(j + 1) * D].rearrange("p (h e) -> p h e", e=DH))
            load(wv[0:size, chunk], wa[lo:hi, 2 * D:3 * D])
            for dst, name in ((fwq, "Wq"), (fwk, "Wk"), (fwv, "Wv"), (fwm, "Wm"),
                              (fwo, "Wo"), (w1, "W1")):
                load(dst[0:size, chunk], W["L0_ffn_" + name][lo:hi])
            for dst, name in ((g1, "g1"), (b1, "b1"), (g2, "g2"), (b2, "b2"), (wr, "Wr"),
                              (fbq, "bq"), (fbk, "bk"), (fbv, "bv")):
                load(dst[0:size, chunk:chunk + 1], W["L0_ffn_" + name][lo:hi].unsqueeze(1))
        ba = W["L0_attn_b_attn"].rearrange("(j g s e) -> j s e g", j=3, g=NG, s=4)
        wpr = W["L0_attn_w_proj"].rearrange("(g s e) m -> s e g m", g=NG, s=4)
        for s in range(4):
            for j, dst in enumerate((bq, bk, bv)):
                load(dst[32 * s:32 * s + DH], ba[j, s])
            load(wp[32 * s:32 * s + DH], wpr[s])
            rel = W["L0_attn_rel_emb"]
            load(rel4[1:HT, 0, 32 * s:32 * s + DH], rel[0:HT - 1])
            load(rel4[0:HT, 1, 32 * s:32 * s + DH], rel[HT - 1:T - 1])
        load(br[:], W["L0_ffn_br"].unsqueeze(0).partition_broadcast(128))
        load(bf1[:], W["L0_ffn_bf1"].rearrange("(k p) -> p k", p=128))
        load(w2[:], W["L0_ffn_W2"].rearrange("(k p) m -> p k m", p=128))
        all_loaded = 16 * len(loads)

        @block.sync
        def _(sp):
            load_x(sp, 0)
            sp.wait_ge(one["zeroed"], 1)
            for dst, src in loads:
                sp.dma_start(dst, src).then_inc(one["w_in"], 16)

            def prefetch(j, image):
                sp.wait_ge(sem["tok_mm"], after("tok_mm", j))
                sp.wait_ge(sem["sq_sb"], after("sq_sb", j))
                load_x(sp, image)

            def store(j):
                sp.wait_ge(sem["out_sb"], after("out_sb", j))
                sp.dma_start(out[j].rearrange("(t p) d -> p t d", p=HT),
                             out_row[:]).then_inc(sem["out_done"], 16)

            prefetch(0, 1)
            with sp.Fori(0, B - 2) as j:
                prefetch(j + 1, j + 2)
                store(j)
            store(B - 2)
            store(B - 1)
            sp.wait_ge(sem["out_done"], 16 * B)

        @block.gpsimd
        def _(gp):
            for t in (wq, wk, bq, bk, bv, wp, rel4):
                gp.memset(t[:], 0.0)
            gp.drain().then_inc(one["zeroed"], 1)
            gp.memset(ident[:], 0.0)
            gp.memset(identh[:], 0.0)
            gp.memset(tri[:], 0.0)
            gp.memset(before[:], 1.0)
            gp.memset(notbefore[:], 1.0)
            gp.memset(slot_of[:], 1.0)
            gp.memset(diag_of[:], 1.0)
            gp.memset(stack32[:], 0.0)
            gp.memset(den_sel[:], 0.0)
            gp.memset(ones[:], 1.0)
            gp.memset(epsc[:], EPS)
            gp.memset(nhalf[:], -0.5)
            gp.memset(v_sb[:], 0.0)
            gp.memset(tokw[:], 1.0)
            gp.iota(iota32[:], [[1, SELP]], base=0, channel_multiplier=0,
                    allow_small_or_imprecise_dtypes=True)
            gp.drain()

            def select(t, op, fill, base, mult, pattern):
                gp.affine_select(out=t, in_=t, compare_op=op, fill=fill, base=base,
                                 pattern=pattern, channel_multiplier=mult)

            select(ident[:], ALU.not_equal, 1.0, 0, 1, [[-1, 128]])
            select(identh[:], ALU.not_equal, 1.0, 0, 1, [[-1, HT]])
            select(tri[:], ALU.is_ge, NEG, 0, 1, [[-1, HT]])
            for t in range(2):
                select(before[:, t], ALU.is_ge, 0.0, HT * t - 1, 1, [[-1, T]])
                select(notbefore[:, t], ALU.is_ge, 0.0, -HT * t, -1, [[1, T]])
            select(slot_of[:], ALU.is_ge, 0.0, 0, 1, [[-DH, 8]])
            select(diag_of[:], ALU.is_ge, 0.0, 0, 1, [[-32, 4], [0, DH]])
            select(den_sel[:], ALU.not_equal, 1.0, -DH, 1, [[-32, 4], [0, 32]])
            gp.memset(v_sb[:, :, :, DH:DH + 1], 1.0)
            for r in range(4):
                gp.drain()
                select(stack32[:], ALU.not_equal, 1.0, -32 * r, 1, [[-1, SELP]])
            select(slot_of[:], ALU.is_ge, 0.0, DH - 1, -1, [[DH, 8]])
            select(diag_of[:], ALU.is_ge, 0.0, 31, -1, [[32, 4], [0, DH]])
            gp.drain().then_inc(one["consts_made"], 1)
            gp.wait_ge(one["w_ready"], 1)

            def rstd(var, ve, r, name):
                gp.tensor_tensor(ve, var, epsc[:], ALU.add)
                gp.drain()
                gp.tensor_tensor(r, ve, nhalf[:], ALU.pow).then_inc(sem[name], 1)

            def both(t):
                return t[:].unsqueeze(1).broadcast_to([HT, 2, D])

            def step(m, n, front, back, again):
                if back:
                    gp.wait_ge(sem["h2_stat"], after("h2_stat", m))
                    v = mv_f[:, :, 1]
                    ve, r, rr, vr, vn, r2 = (vf[:, i, :] for i in range(6))
                    gp.tensor_tensor(ve, v, epsc[:], ALU.add)
                    gp.drain()
                    gp.tensor_tensor(r, ve, nhalf[:], ALU.pow)
                    gp.drain()
                    gp.tensor_tensor(rr, r, r, ALU.mult)
                    gp.drain()
                    gp.tensor_tensor(vr, rr, v, ALU.mult)
                    gp.drain()
                    gp.tensor_tensor(vn, vr, epsc[:], ALU.add)
                    gp.drain()
                    gp.tensor_tensor(vr, vn, nhalf[:], ALU.pow)
                    gp.drain()
                    gp.tensor_tensor(r2, r, vr, ALU.mult).then_inc(sem["h2_rstd"], 1)
                if front:
                    gp.wait_ge(sem["tok_var"], after("tok_var", n))
                    rstd(var1[:], ve1[:], rstd1[:], "tok_rstd")
                    gp.wait_ge(sem["y_stat"], after("y_stat", n))
                    rstd(mv_y[:, :, 1], ve2[:], rstd2[:], "y_rstd")
                if back:
                    gp.tensor_tensor(h2b[:], h2[:], both(bf2), ALU.add)
                if front:
                    gp.wait_ge(sem["y_norm"], after("y_norm", n))
                    gp.tensor_tensor(h1g[:], yn_row[:], both(ln2g), ALU.mult)
                    gp.drain()
                    gp.tensor_tensor(h1[:], h1g[:], both(ln2b), ALU.add).then_inc(sem["h1_sb"], 1)
                    gp.wait_ge(sem["h1_stat"], after("h1_stat", n))
                    rstd(mv_a[:, :, 1], ve3[:], rstd3[:], "h1_rstd")
                    gp.drain()
                    gp.tensor_tensor(h1b[:], h1[:], both(bp), ALU.add).then_inc(sem["h1b_sb"], 1)
                if back:
                    gp.wait_ge(sem["h3_stat"], after("h3_stat", m))
                    rstd(mv_3[:, :, 1], ve5[:], rstd5[:], "h3_rstd")
                    gp.tensor_tensor(res[:], h2b[:], h3[:], ALU.add).then_inc(sem["res_sb"], 1)

            steps(gp, step)

        @block.tensor
        def _(pe):
            mm = pe.matmul
            pe.wait_ge(one["w_in"], all_loaded)
            pe.wait_ge(one["consts_made"], 1)
            pe.wait_ge(one["w_scaled"], 1)
            for q in range(QH):
                mm(bank[0][0:KX, 0:D], ones[0:KX, 0:KX], tokw[:, q, 0:D], start=q == 0,
                   stop=q == QH - 1)
            for q in range(QH):
                mm(bank[1][0:HT, 0:D], tok_brep[:, q], tokraw[:, q], start=q == 0, stop=q == QH - 1)
            for g in range(NG):
                mm(bank[2][0:HT, 0:D], bvrep[:, g], wp[:, g], start=g == 0, stop=g == NG - 1)
            for t in range(2):
                last = pe.transpose(bank[3][0:128, HT * t:HT * t + HT], rel4[:, t],
                                    ident[0:HT, 0:HT])
            last.then_inc(one["w_sums"], 1)
            pe.wait_ge(one["w_ready"], 1)

            def rows_to_cols(b, src, name):
                for chunk, (lo, hi) in enumerate(KC):
                    for t in range(2):
                        c0 = chunk * T + t * HT
                        last = pe.transpose(bank[b][0:hi - lo, c0:c0 + HT], src[:, t, lo:hi],
                                            ident[0:HT, 0:HT])
                last.then_inc(sem[name], 1)

            def cols_to_rows(b, src, w, name):
                for t in range(2):
                    for chunk, (lo, hi) in enumerate(KC):
                        last = mm(bank[b][0:HT, t * D:(t + 1) * D],
                                  src[0:hi - lo, chunk, HT * t:HT * t + HT], w[0:hi - lo, chunk],
                                  start=chunk == 0, stop=chunk == 1)
                last.then_inc(sem[name], 1)

            def group_cols(b0, w, name):
                for g in range(NG):
                    o = bank[b0 + g // 2][:, (g % 2) * T:(g % 2) * T + T]
                    for chunk, (lo, hi) in enumerate(KC):
                        last = mm(o, w[0:hi - lo, chunk, 128 * g:128 * g + 128],
                                  aT[0:hi - lo, chunk], start=chunk == 0, stop=chunk == 1)
                last.then_inc(sem[name], 1)

            def step(m, n, front, back, again):
                xf = x_sb[:].rearrange("p h w -> p (h w)")
                if front:
                    pe.wait_ge(sem["x_in"], after("x_in", n))
                    if again:
                        pe.wait_ge(sem["gelu_sb"], all_before("gelu_sb", m))
                    for t in range(2):
                        for q in range(QH):
                            a = t * HT * PS + q
                            mm(bank[4][0:HT, t * (D + 1):(t + 1) * (D + 1)],
                               xf[:, a:a + (HT - 1) * PS + 1:PS], tokw[:, q],
                               start=q == 0, stop=q == QH - 1)
                    pe.wait_ge(sem["sqsum_sb"], after("sqsum_sb", n))
                    for t in range(2):
                        last = mm(bank[4][0:HT, 2 * D + 2 + t:2 * D + 3 + t],
                                  sqsum[:, HT * t:HT * t + HT], ones[0:KX, 0:1], start=True,
                                  stop=True)
                    last.then_inc(sem["tok_mm"], 1)
                if back:
                    if again:
                        pe.wait_ge(sem["gelu_sb"], all_before("gelu_sb", m))
                    pe.wait_ge(sem["z0_sb"], after("z0_sb", m))
                    rows_to_cols(5, z0, "zT_mm")
                    pe.wait_ge(sem["nT_sb"], after("nT_sb", m))
                    if again:
                        pe.wait_ge(sem["out_sb"], all_before("out_sb", m))
                    for chunk, (lo, hi) in enumerate(KC):
                        last = mm(bank[6][:, 0:T], wrrep[0:hi - lo, chunk], cols(nT, chunk),
                                  start=chunk == 0, stop=chunk == 1)
                    last.then_inc(sem["score_mm"], 1)
                    for mt, (mlo, mhi) in enumerate(KC):
                        for chunk, (lo, hi) in enumerate(KC):
                            last = mm(bank[7][0:mhi - mlo, mt * T:mt * T + T],
                                      fwk[0:hi - lo, chunk, mlo:mhi], cols(nT, chunk),
                                      start=chunk == 0, stop=chunk == 1)
                    last.then_inc(sem["kk_mm"], 1)
                    cols_to_rows(5, nT, fwv, "vv_mm")
                if front:
                    pe.wait_ge(sem["a_sb"], after("a_sb", n))
                    rows_to_cols(4, a_row, "aT_mm")
                    pe.wait_ge(sem["aT_sb"], after("aT_sb", n))
                    if back:
                        pe.wait_ge(sem["yn_sb"], all_before("yn_sb", n))
                    group_cols(0, wq, "q_mm")
                    if back:
                        pe.wait_ge(sem["h2_sb"], all_before("h2_sb", n))
                    group_cols(2, wk, "k_mm")
                    cols_to_rows(4, aT, wv, "v_mm")

                def scores(u, b):
                    s, heads = s_unit(u)
                    for n, (c0, cn, w) in enumerate([(0, 2, T)] if u % 2 else
                                                    [(0, 3, HT), (3 * HT, 1, T)]):
                        o = bank[b][0:HT, c0:c0 + cn * w].rearrange("p (h w) -> p h w", w=w)
                        mm(o[:, :, w - HT:w], identh[:],
                           tri[:].unsqueeze(1).broadcast_to([HT, cn, HT]), start=n == 0,
                           stop=False, skip_group_check=True)
                    for i, (g, t, c0) in enumerate(heads):
                        w = T if t else HT
                        last = mm(bank[b][0:HT, c0:c0 + w],
                                  qT[32 * s:32 * s + 32, g, HT * t:HT * t + HT],
                                  kT[32 * s:32 * s + 32, g, 0:w], start=False,
                                  stop=i == len(heads) - 1, skip_group_check=True)
                    last.then_inc(sem["s_mm"], 1)

                def transposes(kind, k, b):
                    if kind == "A":
                        blocks = [(2 * k + i, t, 0) for i in range(2) for t in range(2)]
                    else:
                        blocks = [(4 * k + i, 1, 1) for i in range(4)]
                    for i, (h, t, u) in enumerate(blocks):
                        src = p1[:, h, HT * u:HT * u + HT] if t else p0[:, h]
                        last = pe.transpose(bank[b][0:HT, HT * i:HT * i + HT], src,
                                            ident[0:HT, 0:HT])
                    last.then_inc(sem["p_T"], 1)

                def item(i):
                    kind, k = ORDER[i][0], int(ORDER[i][1:])
                    b = i % 4
                    if i < 2:
                        pe.wait_ge(sem["qT_sb"], after("qT_sb", n))
                    elif i < 4:
                        pe.wait_ge(sem["kT_sb"], after("kT_sb", n))
                    elif ORDER[i - 4][0] == "S":
                        pe.wait_ge(sem["probs"], after("probs", n, int(ORDER[i - 4][1:]) + 1))
                    else:
                        name, c = pt_done(i - 4)
                        pe.wait_ge(sem[name], after(name, n, c))
                    if kind == "S":
                        if i == 0:
                            pe.wait_ge(sem["kT_sb"], after("kT_sb", n))
                        scores(k, b)
                    else:
                        need = 2 * ((2 * k + 1 if kind == "A" else 4 * k + 3) // 3) + 1
                        pe.wait_ge(sem["probs"], after("probs", n, need + 1))
                        transposes(kind, k, b)

                def gather():
                    pe.wait_ge(sem["sel_sb"], after("sel_sb", m))
                    for chunk, (lo, hi) in enumerate(KC):
                        for t in range(2):
                            mm(bank[6][0:hi - lo, chunk * SELP:(chunk + 1) * SELP],
                               z0[:, t, lo:hi], sel[:, t], start=t == 0, stop=t == 1)
                    for t in range(2):
                        last = pe.transpose(bank[6][0:SELP, 64 + HT * t:64 + HT * t + HT],
                                            sel[:, t], ident[0:HT, 0:HT])
                    last.then_inc(sem["gather_mm"], 1)

                def qsel():
                    pe.wait_ge(sem["nsel_sb"], after("nsel_sb", m))
                    for mt, (mlo, mhi) in enumerate(KC):
                        for chunk, (lo, hi) in enumerate(KC):
                            last = mm(bank[7][0:mhi - mlo, mt * SELP:(mt + 1) * SELP],
                                      fwq[0:hi - lo, chunk, mlo:mhi], cols(nsel, chunk),
                                      start=chunk == 0, stop=chunk == 1)
                    last.then_inc(sem["qsel_mm"], 1)

                def scores2():
                    pe.wait_ge(sem["qb_sb"], after("qb_sb", m))
                    if front:
                        pe.wait_ge(sem["v_sb"], after("v_sb", n))
                    mm(bank[5][:, 0:T], qb0[:, 0:4], kk[:, 0], start=True, stop=True)
                    mm(bank[5][:, T:2 * T], qb0[:, 4:8], kk[:, 0], start=True, stop=True)
                    mm(bank[4][:, 0:T], qb1[:], kk[0:64, 1], start=True,
                       stop=True).then_inc(sem["s2_mm"], 1)

                def transposes2():
                    pe.wait_ge(sem["probs2"], after("probs2", m))
                    for t in range(2):
                        for g in range(NG):
                            last = pe.transpose(bank[6 + t][0:HT, 128 * g:128 * g + 128],
                                                probs2[:, g, HT * t:HT * t + HT], ident[:])
                    last.then_inc(sem["p2_T"], 1)

                def context2():
                    pe.wait_ge(sem["p2T_sb"], after("p2T_sb", m))
                    for g in range(NG):
                        for t in range(2):
                            last = mm(bank[5][:, 64 * g:64 * g + 64],
                                      p2T[:, t, 128 * g:128 * g + 128],
                                      vv[:, t, 64 * g:64 * g + 64], start=t == 0, stop=t == 1)
                    last.then_inc(sem["ctx_mm"], 1)

                def mix():
                    pe.wait_ge(sem["mT_sb"], after("mT_sb", m))
                    cols_to_rows(7, mT, fwm, "mix_mm")

                def context2_cols():
                    pe.wait_ge(sem["ctx_sb"], after("ctx_sb", m))
                    mm(bank[4][:, 0:SELP], ctxm[:, 0:2], stack32[:], start=True, stop=True)
                    last = mm(bank[4][0:64, SELP:2 * SELP], ctxm[:, 2], stack32[:], start=True,
                              stop=True)
                    last.then_inc(sem["ctxT_mm"], 1)

                def attn_out():
                    pe.wait_ge(sem["ctxT_sb"], after("ctxT_sb", m))
                    for chunk in range(2):
                        last = mm(bank[6][0:SELP, 0:D], cols(ctxT, chunk), cols(fwo, chunk),
                                  start=chunk == 0, stop=chunk == 1)
                    last.then_inc(sem["ao_mm"], 1)

                def scatter():
                    pe.wait_ge(sem["ao_sb"], after("ao_sb", m))
                    for t in range(2):
                        last = mm(bank[5][0:HT, t * D:(t + 1) * D],
                                  selT[0:NSEL, HT * t:HT * t + HT], ao[0:NSEL], start=True,
                                  stop=True)
                    last.then_inc(sem["scat_mm"], 1)

                between = {0: gather, 2: qsel, 4: scores2, 6: transposes2, 8: context2, 9: mix,
                           10: context2_cols, 12: attn_out, 14: scatter}
                for i in range(NITEM):
                    if front:
                        item(i)
                    if back and i in between:
                        between[i]()
                if front:
                    pe.wait_ge(sem["pT_dve"], after("pT_dve", n))
                    pe.wait_ge(sem["pT_act"], after("pT_act", n))
                    for g in range(NG):
                        o = bank[2 + g // 2][:, (g % 2) * T:(g % 2) * T + T]
                        for s in range(4):
                            mm(o[32 * s:32 * s + 32], v_sb[:, 0, 4 * g + s], pT0[:, 3 * s + g],
                               start=True, stop=False)
                        for s in range(4):
                            last = mm(o[32 * s:32 * s + 32, HT:T], v_sb[:, 1, 4 * g + s],
                                      pT1[:, 3 * s + g], start=False, stop=True)
                    last.then_inc(sem["y_mm"], 1)
                if back:
                    pe.wait_ge(sem["z3_sb"], after("z3_sb", m))
                    rows_to_cols(6, z3, "z3_T")
                if front:
                    pe.wait_ge(sem["yT_sb"], after("yT_sb", n))
                    for g in range(NG):
                        last = mm(bank[g // 2][:, (g % 2) * T:(g % 2) * T + T],
                                  den_sel[:], yT[:, g], start=True, stop=True)
                    last.then_inc(sem["den_mm"], 1)
                if back:
                    pe.wait_ge(sem["n2T_sb"], after("n2T_sb", m))
                    for j in range(3):
                        for i in range(2):
                            f = 2 * j + i
                            for chunk, (lo, hi) in enumerate(KC):
                                last = mm(bank[(4, 5, 7)[j]][:, T * i:T * i + T],
                                          w1[0:hi - lo, chunk, 128 * f:128 * f + 128],
                                          cols(n2T, chunk), start=chunk == 0, stop=chunk == 1)
                        last.then_inc(sem["up_mm"], 1)
                if front:
                    pe.wait_ge(sem["yn_sb"], after("yn_sb", n))
                    for t in range(2):
                        for g in range(NG):
                            last = mm(bank[2][0:HT, t * D:(t + 1) * D],
                                      ynT[:, g, HT * t:HT * t + HT], wp[:, g], start=g == 0,
                                      stop=g == NG - 1)
                    last.then_inc(sem["proj_mm"], 1)
                if back:
                    pe.wait_ge(sem["gelu_sb"], after("gelu_sb", m))
                    for t in range(2):
                        for f in range(F // 128):
                            last = mm(bank[6][0:HT, t * D:(t + 1) * D],
                                      gT[:, f, HT * t:HT * t + HT], w2[:, f], start=f == 0,
                                      stop=f == F // 128 - 1)
                    last.then_inc(sem["down_mm"], 1)

            steps(pe, step)

        @block.vector
        def _(ve):
            ve.wait_ge(one["w_in"], all_loaded)
            ve.wait_ge(one["consts_made"], 1)
            for q in range(QH):
                ve.tensor_scalar(tokw[:, q, 0:D], tokraw[:, q], tok_g[:, q:q + 1], None, ALU.mult)
            ve.tensor_copy(tok_brep[:], tok_bb[:].unsqueeze(2).broadcast_to([KX, QH, HT]))
            ve.tensor_copy(bvrep[:], bv[:].unsqueeze(2).broadcast_to([128, NG, HT]))
            for chunk, (lo, hi) in enumerate(KC):
                size = hi - lo
                ve.tensor_copy(wrrep[0:size, chunk],
                               wr[0:size, chunk:chunk + 1].broadcast_to([size, 128]))
                ve.tensor_scalar(fbqs[0:size, chunk:chunk + 1], fbq[0:size, chunk:chunk + 1], QSCALE,
                                 None, ALU.mult)
            ve.tensor_scalar(bqs[:], bq[:], QSCALE, None, ALU.mult)
            ve.drain().then_inc(one["w_scaled"], 1)
            ve.wait_ge(one["w_sums"], 1)
            for q in range(QH):
                ve.scalar_tensor_tensor(tokw[:, q, 0:D], bank[0][0:KX, 0:D], -1.0 / PD,
                                        tokw[:, q, 0:D], ALU.mult, ALU.add)
            ve.tensor_tensor(tok_bias[:], bank[1][0:HT, 0:D], tok_brow[:], ALU.add)
            ve.tensor_tensor(bp[:], bank[2][0:HT, 0:D], bprow[:], ALU.add)
            for g in range(NG):
                ve.tensor_scalar(relk[:, g], bank[3][:, 0:T], bk[:, g:g + 1], None, ALU.add)
            ve.drain().then_inc(one["w_ready"], 1)

            def stats(src, bn, mv, name):
                for t in range(2):
                    ve.bn_stats(bn[:, t], src[:, t])
                ve.drain()
                for t in range(2):
                    last = ve.bn_aggr(mv[:, t], bn[:, t])
                last.then_inc(sem[name], 1)

            def normalise(dst, src, mv, r, name):
                for t in range(2):
                    last = ve.tensor_scalar(dst[:, t], src[:, t], mv[:, t, 0:1], r[:, t:t + 1],
                                            ALU.subtract, ALU.mult)
                last.then_inc(sem[name], 1)

            def rows(b):
                return bank[b][0:HT, 0:2 * D].rearrange("p (t d) -> p t d", t=2)

            def step(m, n, front, back, again):
                if back:
                    ve.drain()
                    stats(h2, bn_f, mv_f, "h2_stat")
                if front:
                    ve.wait_ge(sem["sq_sb"], after("sq_sb", n))
                    ve.tensor_reduce(sqsum[:], x_sq[:], AX.X, ALU.add).then_inc(sem["sqsum_sb"], 1)
                if back:
                    ve.wait_ge(sem["h2_rstd"], after("h2_rstd", m))
                    normalise(z0, h2, mv_f, vf[:, 5], "z0_sb")
                    normalise(f0, h2, mv_f, vf[:, 1], "f0_sb")
                if front:
                    ve.wait_ge(sem["tok_mm"], after("tok_mm", n))
                    tok = bank[4][0:HT, 0:2 * (D + 1)].rearrange("p (t d) -> p t d", t=2)
                    ve.tensor_scalar(mean1[:], tok[:, :, D], 1.0 / PD, None, ALU.mult)
                    ve.drain()
                    ve.tensor_tensor(msq1[:], mean1[:], mean1[:], ALU.mult)
                    ve.drain()
                    ve.scalar_tensor_tensor(var1[:], bank[4][0:HT, 2 * D + 2:2 * D + 4], 1.0 / PD,
                                            msq1[:], ALU.mult,
                                            ALU.subtract).then_inc(sem["tok_var"], 1)
                    ve.wait_ge(sem["tok_rstd"], after("tok_rstd", n))
                    for t in range(2):
                        last = ve.scalar_tensor_tensor(y_row[:, t], tok[:, t, 0:D],
                                                       rstd1[:, t:t + 1], tok_bias[:], ALU.mult,
                                                       ALU.add)
                    last.then_inc(sem["tok_y"], 1)
                    ve.drain()
                    stats(y_row, bn_y, mv_y, "y_stat")
                    ve.wait_ge(sem["y_rstd"], after("y_rstd", n))
                    normalise(yn_row, y_row, mv_y, rstd2, "y_norm")
                if back:
                    ve.wait_ge(sem["score_mm"], after("score_mm", m))
                    ve.tensor_scalar(zrow[:], bank[6][:, 0:T], br[:], None,
                                     ALU.add).then_inc(sem["z_sb"], 1)
                    ve.drain()
                    ve.tensor_scalar(zclip[:], zrow[:], TOPZ, -88.0, ALU.min, ALU.max)
                    ve.drain()
                    for t in range(2):
                        ve.tensor_tensor_reduce(scr[:, t, 0:HT], zclip[0:HT, HT * t:HT * t + HT],
                                                ident[0:HT, 0:HT], 1.0, 0.0, ALU.mult, ALU.add,
                                                zi[:, t:t + 1])
                    ve.drain()
                    for t in range(2):
                        ve.scalar_tensor_tensor(scr[:, t], zclip[0:HT], zi[:, t:t + 1],
                                                before[:, t], ALU.is_le, ALU.mult,
                                                accum_out=cnt[:, 0, t:t + 1])
                        ve.scalar_tensor_tensor(scr[:, 2 + t], zclip[0:HT], zi[:, t:t + 1],
                                                notbefore[:, t], ALU.is_lt, ALU.mult,
                                                accum_out=cnt[:, 1, t:t + 1])
                    ve.drain()
                    ve.tensor_tensor(rank[:], cnt[:, 0], cnt[:, 1], ALU.add)
                    ve.drain()
                    ve.tensor_scalar(keep[:], rank[:], NSEL - 0.5, None, ALU.is_ge)
                    for t in range(2):
                        last = ve.tensor_scalar(sel[:, t], iota32[:], rank[:, t:t + 1], None,
                                                ALU.is_equal)
                    last.then_inc(sem["sel_sb"], 1)
                if front:
                    ve.wait_ge(sem["h1_sb"], after("h1_sb", n))
                    stats(h1, bn_a, mv_a, "h1_stat")
                if back:
                    ve.wait_ge(sem["expz"], after("expz", m))
                    ve.tensor_scalar(ez1[:], ez[:], 1.0, None, ALU.add)
                    ve.drain()
                    ve.reciprocal(sig[:], ez1[:])
                    ve.drain()
                if front:
                    ve.wait_ge(sem["h1_rstd"], after("h1_rstd", n))
                    normalise(a_row, h1, mv_a, rstd3, "a_sb")
                if back:
                    ve.tensor_scalar(scr2[:, 2], sig[:], 1.0, None, ALU.mult, ALU.add,
                                     accum_out=ssum[:])
                    for chunk, (lo, hi) in enumerate(KC):
                        size = hi - lo
                        ve.tensor_tensor_reduce(scr2[0:size, chunk], nT[0:size, chunk], sig[0:size], 1.0,
                                                0.0, ALU.mult, ALU.add,
                                                pool_raw[0:size, chunk:chunk + 1])
                    ve.drain()
                    ve.tensor_scalar(sse[:], ssum[:], 1e-6, None, ALU.add)
                    ve.drain()
                    ve.reciprocal(rss[:], sse[:])
                    ve.drain()
                    for chunk, (lo, hi) in enumerate(KC):
                        size = hi - lo
                        ve.tensor_scalar(pooled[0:size, chunk:chunk + 1],
                                         pool_raw[0:size, chunk:chunk + 1], rss[0:size], None, ALU.mult)
                    ve.drain()
                    for chunk, (lo, hi) in enumerate(KC):
                        size = hi - lo
                        last = ve.scalar_tensor_tensor(mT[0:size, chunk], sig[0:size],
                                                       pooled[0:size, chunk:chunk + 1],
                                                       nT[0:size, chunk], ALU.mult, ALU.add)
                    last.then_inc(sem["mT_sb"], 1)
                if front:
                    ve.wait_ge(sem["k_mm"], after("k_mm", n))
                    ve.tensor_tensor(kT[:, 0:2].rearrange("p g t -> p (g t)"), bank[2][:, 0:2 * T],
                                     relk[:, 0:2].rearrange("p g t -> p (g t)"), ALU.add)
                    ve.tensor_tensor(kT[:, 2], bank[3][:, 0:T], relk[:, 2],
                                     ALU.add).then_inc(sem["kT_sb"], 1)

                def item(i):
                    kind, k = ORDER[i][0], int(ORDER[i][1:])
                    if kind == "S":
                        ve.wait_ge(sem["s_mm"], after("s_mm", n, k + 1))
                        s = 3 * (k // 2)
                        parts = ([(1, s, 2, 0, T)] if k % 2 else
                                 [(0, s, 3, 0, HT), (1, s + 2, 1, 3 * HT, T)])
                        for t, h, hn, c0, w in parts:
                            last = ve.tensor_reduce(
                                negmax[:, t, h:h + hn],
                                bank[i % 4][0:HT, c0:c0 + w * hn].rearrange("p (h w) -> p h w",
                                                                            w=w),
                                AX.X, ALU.max, negate=True)
                        last.then_inc(sem["rowmax"], 1)
                    elif pt_done(i)[0] == "pT_dve":
                        made = sum(o[0] != "S" for o in ORDER[:i + 1])
                        ve.wait_ge(sem["p_T"], after("p_T", n, made))
                        ve.tensor_copy(pt_dst(kind, k),
                                       bank[i % 4][0:HT, 0:4 * HT]).then_inc(sem["pT_dve"], 1)

                def q_blocks():
                    ve.wait_ge(sem["qs_sb"], after("qs_sb", m))
                    ve.tensor_tensor(qb0[:], qs[:, 0:1].broadcast_to([128, 8, SELP]),
                                     slot_of[:].unsqueeze(2).broadcast_to([128, 8, SELP]),
                                     ALU.mult)
                    ve.tensor_tensor(qb1[:], qs[0:64, 1:2].broadcast_to([64, 4, SELP]),
                                     slot_of[0:64, 0:4].unsqueeze(2).broadcast_to([64, 4, SELP]),
                                     ALU.mult).then_inc(sem["qb_sb"], 1)

                def max2():
                    ve.wait_ge(sem["s2_mm"], after("s2_mm", m))
                    ve.tensor_reduce(negmax2[:, 0:2],
                                     bank[5][:, 0:2 * T].rearrange("p (g t) -> p g t", g=2), AX.X,
                                     ALU.max, negate=True)
                    ve.tensor_reduce(negmax2[:, 2:3], bank[4][:, 0:T], AX.X, ALU.max,
                                     negate=True).then_inc(sem["max2"], 1)

                def context2():
                    ve.wait_ge(sem["probs2"], after("probs2", m))
                    ve.reciprocal(rden2[:], den2[:])
                    ve.drain()
                    ve.wait_ge(sem["ctx_mm"], after("ctx_mm", m))
                    for g in range(NG):
                        last = ve.scalar_tensor_tensor(
                            ctxm[:, g], bank[5][:, 64 * g:64 * g + 64], rden2[:, g:g + 1],
                            diag_of[:].rearrange("p h e -> p (h e)"), ALU.mult, ALU.mult)
                    last.then_inc(sem["ctx_sb"], 1)

                def context2_cols():
                    ve.wait_ge(sem["ctxT_mm"], after("ctxT_mm", m))
                    for chunk, (lo, hi) in enumerate(KC):
                        size = hi - lo
                        last = ve.tensor_scalar(ctxT[0:size, chunk],
                                                bank[4][0:size, SELP * chunk:SELP * (chunk + 1)],
                                                fbv[0:size, chunk:chunk + 1], None, ALU.add)
                    last.then_inc(sem["ctxT_sb"], 1)

                def attn_out():
                    ve.wait_ge(sem["ao_mm"], after("ao_mm", m))
                    ve.tensor_tensor(ao[:], bank[6][0:SELP, 0:D], fbo[:],
                                     ALU.add).then_inc(sem["ao_sb"], 1)

                def mix():
                    ve.wait_ge(sem["mix_mm"], after("mix_mm", m))
                    ve.tensor_tensor(mixb[:], rows(7), fbm[:].unsqueeze(1).broadcast_to([HT, 2, D]),
                                     ALU.add)
                    ve.drain()
                    for t in range(2):
                        ve.scalar_tensor_tensor(f1[:, t], mixb[:, t], keep[:, t:t + 1], f0[:, t],
                                                ALU.mult, ALU.add)

                def merge():
                    ve.drain()
                    ve.wait_ge(sem["scat_mm"], after("scat_mm", m))
                    ve.tensor_tensor(h3[:], rows(5), f1[:], ALU.add).then_inc(sem["h3_sb"], 1)
                    ve.drain()
                    stats(h3, bn_3, mv_3, "h3_stat")

                between = {3: q_blocks, 5: max2, 9: context2, 11: context2_cols, 12: mix,
                           13: attn_out, 15: merge}
                for i in range(NITEM):
                    if front:
                        item(i)
                    if back and i in between:
                        between[i]()
                if back:
                    ve.wait_ge(sem["h3_rstd"], after("h3_rstd", m))
                    normalise(z3, h3, mv_3, rstd5, "z3_sb")
                if front:
                    ve.wait_ge(sem["den_mm"], after("den_mm", n))
                    ve.reciprocal(rden[:, 0:2].rearrange("p g t -> p (g t)"), bank[0][:, 0:2 * T])
                    ve.reciprocal(rden[:, 2], bank[1][:, 0:T])
                    ve.drain()
                    ve.tensor_tensor(ynT[:], yT[:], rden[:], ALU.mult).then_inc(sem["yn_sb"], 1)
                    ve.wait_ge(sem["proj_mm"], after("proj_mm", n))
                    ve.wait_ge(sem["h1b_sb"], after("h1b_sb", n))
                    if back:
                        ve.wait_ge(sem["res_sb"], all_before("res_sb", n))
                    ve.tensor_tensor(h2[:], rows(2), h1b[:], ALU.add).then_inc(sem["h2_sb"], 1)
                if back:
                    ve.wait_ge(sem["down_mm"], after("down_mm", m))
                    ve.wait_ge(sem["res_sb"], after("res_sb", m))
                    if again:
                        ve.wait_ge(sem["out_done"], all_before("out_done", m))
                    ve.tensor_tensor(out_row[:], rows(6), res[:], ALU.add).then_inc(sem["out_sb"], 1)

            steps(ve, step)

        @block.scalar
        def _(sc):
            sc.wait_ge(one["w_ready"], 1)

            def affine_cols(dst, b, name, scale=None, bias=None, width=T):
                for chunk, (lo, hi) in enumerate(KC):
                    size = hi - lo
                    src = bank[b][0:size, chunk * width:(chunk + 1) * width]
                    if bias is None:
                        last = sc.copy(dst[0:size, chunk], src)
                    else:
                        last = sc.activation(
                            dst[0:size, chunk], src, ACT.Identity, bias=bias[0:size, chunk:chunk + 1],
                            scale=scale[0:size, chunk:chunk + 1] if not isinstance(scale, float)
                            else scale)
                if name:
                    last.then_inc(sem[name], 1)

            def step(m, n, front, back, again):
                if front:
                    sc.wait_ge(sem["x_in"], after("x_in", n))
                    if back:
                        sc.wait_ge(sem["sqsum_sb"], all_before("sqsum_sb", n))
                    xv = x_sb[:].rearrange("p h (w q) -> p (h w) q", q=PS)
                    sc.activation(x_sq[:], xv[:, :, 0:QH], ACT.Square).then_inc(sem["sq_sb"], 1)
                if back:
                    sc.wait_ge(sem["zT_mm"], after("zT_mm", m))
                    affine_cols(nT, 5, "nT_sb", g1, b1)
                    sc.wait_ge(sem["z_sb"], after("z_sb", m))
                    sc.activation(ez[:], zrow[:], ACT.Exp, scale=-1.0).then_inc(sem["expz"], 1)
                    sc.wait_ge(sem["kk_mm"], after("kk_mm", m))
                    affine_cols(kk, 7, "kk_sb", 1.0, fbk)
                    sc.wait_ge(sem["vv_mm"], after("vv_mm", m))
                    sc.copy(vv[:].rearrange("p t d -> p (t d)"),
                            bank[5][0:HT, 0:2 * D]).then_inc(sem["vv_sb"], 1)
                if front:
                    sc.wait_ge(sem["aT_mm"], after("aT_mm", n))
                    affine_cols(aT, 4, "aT_sb")
                    sc.wait_ge(sem["q_mm"], after("q_mm", n))
                    for g in range(NG):
                        last = sc.activation(qT[:, g],
                                             bank[g // 2][:, (g % 2) * T:(g % 2) * T + T],
                                             ACT.Identity, bias=bqs[:, g:g + 1], scale=QSCALE)
                    last.then_inc(sem["qT_sb"], 1)
                    sc.wait_ge(sem["v_mm"], after("v_mm", n))
                    sc.copy(v_sb[:, :, :, 0:DH].rearrange("p t h e -> p (t h) e"),
                            bank[4][0:HT, 0:2 * D].rearrange("p (h e) -> p h e", e=DH)
                            ).then_inc(sem["v_sb"], 1)

                def item(i):
                    kind, k = ORDER[i][0], int(ORDER[i][1:])
                    if kind == "S":
                        sc.wait_ge(sem["rowmax"], after("rowmax", n, k + 1))
                        s, heads = s_unit(k)
                        for g, t, c0 in heads:
                            h = 3 * s + g
                            last = sc.activation((p1 if t else p0)[:, h],
                                                 bank[i % 4][0:HT, c0:c0 + (T if t else HT)],
                                                 ACT.Exp, bias=negmax[:, t, h:h + 1])
                        last.then_inc(sem["probs"], 1)
                    elif pt_done(i)[0] == "pT_act":
                        made = sum(o[0] != "S" for o in ORDER[:i + 1])
                        sc.wait_ge(sem["p_T"], after("p_T", n, made))
                        sc.copy(pt_dst(kind, k),
                                bank[i % 4][0:HT, 0:4 * HT]).then_inc(sem["pT_act"], 1)

                def gathered():
                    sc.wait_ge(sem["gather_mm"], after("gather_mm", m))
                    affine_cols(nsel, 6, None, g1, b1, SELP)
                    sc.copy(selT[:], bank[6][0:SELP, 64:64 + T]).then_inc(sem["nsel_sb"], 1)

                def queries2():
                    sc.wait_ge(sem["qsel_mm"], after("qsel_mm", m))
                    affine_cols(qs, 7, "qs_sb", QSCALE, fbqs, SELP)

                def softmax2():
                    sc.wait_ge(sem["max2"], after("max2", m))
                    for g in range(NG):
                        src = bank[5][:, T * g:T * g + T] if g < 2 else bank[4][:, 0:T]
                        last = sc.activation(probs2[:, g], src, ACT.Exp, bias=negmax2[:, g:g + 1],
                                             accum_out=den2[:, g:g + 1])
                    sc.drain().then_inc(sem["probs2"], 1)

                def transposed2():
                    sc.wait_ge(sem["p2_T"], after("p2_T", m))
                    for t in range(2):
                        last = sc.copy(p2T[:, t], bank[6 + t][0:HT, 0:NG * 128])
                    last.then_inc(sem["p2T_sb"], 1)

                between = {1: gathered, 3: queries2, 5: softmax2, 7: transposed2}
                for i in range(NITEM):
                    if front:
                        item(i)
                    if back and i in between:
                        between[i]()
                if front:
                    sc.wait_ge(sem["y_mm"], after("y_mm", n))
                    sc.copy(yT[:, 0:2].rearrange("p g t -> p (g t)"), bank[2][:, 0:2 * T])
                    sc.copy(yT[:, 2], bank[3][:, 0:T]).then_inc(sem["yT_sb"], 1)
                if back:
                    sc.wait_ge(sem["z3_T"], after("z3_T", m))
                    affine_cols(n2T, 6, "n2T_sb", g2, b2)
                    for j in range(3):
                        sc.wait_ge(sem["up_mm"], after("up_mm", m, j + 1))
                        for i in range(2):
                            f = 2 * j + i
                            last = sc.activation(gT[:, f], bank[(4, 5, 7)[j]][:, T * i:T * i + T],
                                                 ACT.Gelu, bias=bf1[:, f:f + 1])
                        last.then_inc(sem["gelu_sb"], 1)

            steps(sc, step)


def kernel(**inputs):
    import numpy as _np
    import concourse.bacc as _bacc
    from concourse import mybir as _mybir
    from concourse.bass_utils import run_bass_kernel_spmd as _run

    nc = _bacc.Bacc("TRN2", target_bir_lowering=False, num_devices=1)
    arrays, args = {}, {}
    for name, a in inputs.items():
        a = _np.ascontiguousarray(a)
        if a.ndim == 0:
            a = a.reshape(1)
        arrays[f"in_{name}"] = a
        args[name] = nc.dram_tensor(f"in_{name}", a.shape, _mybir.dt.from_np(a.dtype),
                                    kind="ExternalInput").ap()
    y = nc.dram_tensor("out_0", (B, T, D), _mybir.dt.float32, kind="ExternalOutput").ap()
    build(nc, args, y)
    r = _run(nc, [arrays], core_ids=[0])
    return r.results[0]["out_0"]
```

```python
from contextlib import ExitStack

import concourse.bass as bass
from concourse import mybir

F32 = mybir.dt.float32
F32R = mybir.dt.float32r
BF16 = mybir.dt.bfloat16
ALU = mybir.AluOpType
ACT = mybir.ActivationFunctionType
AX = mybir.AxisListType

B, C, IMG = 128, 3, 224
PS = 16
GR = IMG // PS
T = GR * GR
HT = T // 2
PD = PS * PS * C
D = 192
NH, DH = 12, 16
F = 768
NSEL = max(1, int(round(0.15 * T)))
SELP = 32
EPS = 1e-5
QH = PS // 2
KX = 2 * C * PS
NEG = -1e30
KC = ((0, 128), (128, 192))
NG = 3
QSCALE = DH ** -0.5
TOPZ = 16.635532
RING = dict(S0=0, S1=1, S2=2, T0=3, S3=0, S4=1, S5=2, S6=0, S7=1, A0=2, A1=3, A2=0, B0=1, A3=2,
            B1=3, A4=0, A5=1, B2=2)
ORDER = list(RING)
PT = [name for name in ORDER if name[0] in "AB"]
PT_ACT = ("A1", "B0", "B1", "A5", "B2")
PAIRS = ((0, 0), (0, 1), (1, 0), (2, 2), (2, 3))

SEMS = dict(
    x_in=2 * C * 16, out_done=16,
    tok_mm=1, zT_mm=1, score_mm=1, kk_mm=1, vv_mm=1, aT_mm=1, q_mm=1, k_mm=1, v_mm=1,
    s_mm=8, p_T=len(PT), y_mm=1, proj_mm=1,
    gather_mm=1, qsel_mm=1, s2_mm=1, p2_T=1, ctx_mm=1, ctxT_mm=1, ao_mm=1, mix_mm=1,
    scat_mm=1, z3_T=1, up_mm=3, down_mm=1,
    tok_var=1, tok_y=1, y_stat=1, y_norm=1, h1_stat=1, a_sb=1, aTs_sb=1, klo_sb=1,
    qparts_sb=1, qz_sb=2, rowmax=8, rden_sb=4, pT_dve=len(PT) - len(PT_ACT), h2_sb=1,
    h2_stat=1, z0_sb=1, f0_sb=1, nTs_sb=1, n2Ts_sb=1, z_sb=1, sel_sb=1, mT_sb=1, f1_sb=1, qb_sb=1, max2=1, ctx_sb=1, ctxT_sb=1, ao_sb=1,
    h3_sb=1, h3_stat=1, z3_sb=1, out_sb=1,
    sq_sb=1, aT_sb=1, qhi_sb=1, khi_sb=1, v_sb=1, probs=8, pT_act=len(PT_ACT), yT_sb=1,
    nT_sb=1, expz=1, kk_sb=1, vv_sb=1, nsel_sb=1, qs_sb=1, probs2=1, p2T_sb=1, n2T_sb=1, gelu_sb=3,
    qz2_sb=2, sqsum_sb=1, tok_rstd=1, y_rstd=1, h1_sb=1, h1b_sb=1, diag_sb=4, h1_rstd=1, h2_rstd=1, res_sb=1, h3_rstd=1,
)


def s_unit(u):
    s, second = divmod(u, 2)
    if second:
        return s, [(0, 1, 0), (1, 1, T)]
    return s, [(0, 0, 0), (1, 0, HT), (2, 0, 2 * HT), (2, 1, 3 * HT)]


def build(nc, ins, out):
    W = dict(ins)
    with ExitStack() as ctx:
        ctx.enter_context(nc.allow_non_contiguous_dma(reason="small weights, once"))
        def sb(name, shape, dt=F32):
            return ctx.enter_context(nc.sbuf_tensor(name, shape, dt))

        sem = {name: ctx.enter_context(nc.semaphore(name)) for name in SEMS}
        one = {name: ctx.enter_context(nc.semaphore(name)) for name in
               ("w_in", "consts_made", "zeroed", "w_scaled", "w_sums", "w_ready", "p1_zeroed")}
        bank = [ctx.enter_context(nc.psum_tensor(f"bank{i}", [128, 512], F32)) for i in range(8)]

        ident = sb("ident", [128, 128])
        identh = sb("identh", [HT, HT], BF16)
        tri = sb("tri", [HT, HT], BF16)
        before = sb("before", [HT, 2, T])
        notbefore = sb("notbefore", [HT, 2, T])
        slot_of = sb("slot_of", [128, 8])
        diag_of = sb("diag_of", [128, 4, DH])
        stack32 = sb("stack32", [128, SELP])
        lo_rows = sb("lo_rows", [128, 1])
        hi_half = sb("hi_half", [128, 1])
        iota32 = sb("iota32", [HT, SELP])
        ones = sb("ones", [128, 128])
        epsc = sb("epsc", [HT, 2])
        nhalf = sb("nhalf", [HT, 2])
        tokw = sb("tokw", [128, QH, D + 1])
        tok_g = sb("tok_g", [KX, QH])
        tok_bb = sb("tok_bb", [KX, QH])
        tok_bias = sb("tok_bias", [HT, D])
        ln2g = sb("ln2g", [HT, D])
        ln2b = sb("ln2b", [HT, D])
        widths = dict(wq=NG * 128, wk=NG * 128, wv=D, fwk=D, fwv=D, wr=128, w1=F)
        split = {name: sb(name + "_split", [128, 4, width], F32R)
                 for name, width in widths.items()}
        bk = sb("bk", [128, NG])
        bv = sb("bv", [128, NG])
        relk = sb("relk", [128, 2, NG, T], F32R)
        identr = sb("identr", [128, 128], F32R)
        onesr = sb("onesr", [64, T], F32R)
        bqparts = sb("bqparts", [64, NG * 128], F32R)
        wp = sb("wp", [128, NG, D])
        bp = sb("bp", [HT, D])
        g1 = sb("g1", [128, 2])
        b1 = sb("b1", [128, 2])
        g2 = sb("g2", [128, 2])
        b2 = sb("b2", [128, 2])
        wr = sb("wr", [128, 2])
        br = sb("br", [128, 1])
        fwq = sb("fwq", [128, 2, D])
        fwm = sb("fwm", [128, 2, D])
        fwo = sb("fwo", [128, 2, D])
        fbq = sb("fbq", [128, 2])
        fbqs = sb("fbqs", [128, 2])
        fbk = sb("fbk", [128, 2])
        fbv = sb("fbv", [128, 2])
        fbo = sb("fbo", [SELP, D])
        fbm = sb("fbm", [HT, D])
        bf1 = sb("bf1", [128, F // 128])
        w2 = sb("w2", [128, F // 128, D])
        bf2 = sb("bf2", [HT, D])
        x_sb = sb("x_sb", [128, GR, IMG])
        x_store = sb("x_store", [128, T * QH])
        x_sq = x_store[0:KX].rearrange("p (t q) -> p t q", q=QH)
        sqsum = sb("sqsum", [KX, T])
        mean1 = sb("mean1", [HT, 2])
        msq1 = sb("msq1", [HT, 2])
        var1 = sb("var1", [HT, 2])
        ve1 = sb("ve1", [HT, 2])
        rstd1 = sb("rstd1", [HT, 2])
        y_row = sb("y_row", [HT, 2, D])
        bn_y = sb("bn_y", [HT, 2, 6])
        mv_y = sb("mv_y", [HT, 2, 2])
        ve2 = sb("ve2", [HT, 2])
        rstd2 = sb("rstd2", [HT, 2])
        h1 = sb("h1", [HT, 2, D])
        h1b = sb("h1b", [HT, 2, D])
        bn_a = sb("bn_a", [HT, 2, 6])
        mv_a = sb("mv_a", [HT, 2, 2])
        ve3 = sb("ve3", [HT, 2])
        rstd3 = sb("rstd3", [HT, 2])
        a_row = sb("a_row", [HT, 2, D])
        aT = sb("aT", [128, 3, T], F32R)
        qparts = sb("qparts", [128, NG, T], F32R)
        probs2 = sb("probs2_", [128, NG, T])
        qhi = sb("qhi", [128, NG, T], F32R)
        table_out = sb("table_out", [1, 1])
        qz = sb("qz", [128, 4, NG, T], F32R)
        khi = sb("khi", [128, NG, T], F32R)
        klo = sb("klo", [128, NG, T], F32R)
        v_sb = sb("v_sb", [128, 2, NH, 32])
        negmax = sb("negmax", [HT, 4, 2, NG])
        den = sb("den", [HT, 4, 2, NG])
        rden = sb("rden", [HT, 4, 2, NG])
        diag = sb("diag", [128, 4, 2, NG, HT])
        p0 = sb("p0", [128, NH, HT])
        p1 = sb("p1", [128, NH, T])
        pT0 = sb("pT0", [128, NH, T])
        pT1 = sb("pT1", [128, NH, HT])
        yT = sb("yT", [128, NG, T])
        h2 = sb("h2", [HT, 2, D])
        h2b = sb("h2b", [HT, 2, D])
        bn_f = sb("bn_f", [HT, 2, 6])
        mv_f = sb("mv_f", [HT, 2, 2])
        vf = sb("vf", [HT, 6, 2])
        f0 = sb("f0", [HT, 2, D])
        z0 = sb("z0", [HT, 2, D])
        nT = sb("nT", [128, 2, T])
        nTs = sb("nTs", [128, 3, T], F32R)
        zrow = sb("zrow", [128, T])
        zclip = sb("zclip", [128, T])
        zi = sb("zi", [HT, 2])
        scr = sb("scr", [HT, 4, T])
        cnt = sb("cnt", [HT, 2, 2])
        rank = sb("rank", [HT, 2])
        keep = sb("keep", [HT, 2])
        sel = sb("sel", [HT, 2, SELP])
        ez = sb("ez", [128, T])
        sig = sb("sig", [128, T])
        scr2 = sb("scr2", [128, 3, T])
        ssum = sb("ssum", [128, 1])
        sse = sb("sse", [128, 1])
        rss = sb("rss", [128, 1])
        pool_raw = sb("pool_raw", [128, 2])
        pooled = sb("pooled", [128, 2])
        mT = sb("mT", [128, 2, T])
        kk = sb("kk", [128, 2, T])
        vv = sb("vv", [HT, 2, D])
        nsel = sb("nsel", [128, 2, SELP])
        selT = sb("selT", [SELP, T])
        qs = sb("qs", [128, 2, SELP])
        qb0 = sb("qb0", [128, 8, SELP])
        qb1 = sb("qb1", [64, 4, SELP])
        negmax2 = sb("negmax2", [128, NG])
        den2 = sb("den2", [128, NG])
        rden2 = sb("rden2", [128, NG])
        p2T = sb("p2T", [HT, 2, NG * 128])
        ctxm = sb("ctxm", [128, NG, 64])
        ctxT = sb("ctxT", [128, 2, SELP])
        ao = sb("ao", [SELP, D])
        f1 = sb("f1", [HT, 2, D])
        h3 = sb("h3", [HT, 2, D])
        res = sb("res", [HT, 2, D])
        bn_3 = sb("bn_3", [HT, 2, 6])
        mv_3 = sb("mv_3", [HT, 2, 2])
        ve5 = sb("ve5", [HT, 2])
        rstd5 = sb("rstd5", [HT, 2])
        z3 = sb("z3", [HT, 2, D])
        n2T, n2Ts = nT, nTs
        gstore = sb("gstore", [128, 2 * F])
        gT = gstore[:, 0:F // 128 * T].rearrange("p (f t) -> p f t", t=T)
        out_row = sb("out_row", [HT, 2, D])

        tokraw = x_store[0:KX, 0:QH * D].rearrange(
            "p (q d) -> p q d", d=D)
        tok_brep = scr[0:KX].rearrange("p a t -> p (a t)").rearrange("p (q i) -> p q i", i=HT)
        flat = p1[:].rearrange("p h t -> p (h t)")
        relb = flat[:, 2 * F:2 * F + NG * T].rearrange("p (g t) -> p g t", g=NG)
        bvrep = scr2[:].rearrange("p a t -> p (a t)")[:, 0:NG * HT].rearrange(
            "p (g i) -> p g i", g=NG)
        tok_brow, bprow = h3[:, 0], h3[:, 1]
        rel4 = out_row[:, :, 0:128]
        bqrow = p0[0:64].rearrange("p h t -> p (h t)")[:, 0:NG * 128]
        raw = dict(w1=gstore[:].rearrange("p (c w) -> p c w", c=2),
                   wr=qb0[:].rearrange("p h i -> p (h i)").rearrange("p (c w) -> p c w", c=2))
        for i, name in enumerate(("wq", "wk")):
            size = 2 * widths[name]
            raw[name] = flat[:, i * size:(i + 1) * size].rearrange("p (c w) -> p c w", c=2)
        for name, place in (("wv", nT), ("fwk", mT), ("fwv", kk)):
            raw[name] = place[:].rearrange("p c t -> p (c t)")[:, 0:2 * D].rearrange(
                "p (c w) -> p c w", c=2)

        def cols(t, chunk):
            lo, hi = KC[chunk]
            return t[0:hi - lo, chunk]

        def after(name, image, j=None):
            k = SEMS[name]
            return image * k + (k if j is None else j)

        def all_before(name, image):
            return image * SEMS[name]

        def steps(eng, step):
            step(-2, -1, 0, True, False, False, False)
            step(-1, 0, 1, True, True, False, False)
            step(0, 1, 2, True, True, True, False)
            with eng.Fori(1, B - 2) as m:
                step(m, m + 1, m + 2, True, True, True, True)
            step(B - 2, B - 1, B, False, True, True, True)
            step(B - 1, B, B + 1, False, False, True, True)

        def evacuation(name):
            act = name in PT_ACT
            return ("pT_act" if act else "pT_dve",
                    sum((o in PT_ACT) == act for o in PT[:PT.index(name) + 1]))

        def pt_dst(kind, k):
            if kind == "A":
                return pT0[0:HT, 2 * k:2 * k + 2].rearrange("p h t -> p (h t)")
            return pT1[0:HT, 4 * k:4 * k + 4].rearrange("p h t -> p (h t)")

        block = ctx.enter_context(nc.Block())

        loads = []

        def load(dst, src):
            loads.append((dst, src))

        xh = W["x"].rearrange("b c (h p) w -> b c p h w", p=PS)

        def load_x(eng, image):
            for s in range(2):
                for c in range(C):
                    part = (s * C + c) * PS
                    eng.dma_start(x_sb[part:part + PS, :, 0:IMG - QH * s],
                                  xh[image, c, :, :, QH * s:IMG]).then_inc(sem["x_in"], 16)

        tw = W["L0_tok_W"].rearrange("(p s q c) m -> s c p q m", p=PS, s=2, q=QH)
        tg = W["L0_tok_ln1_g"].rearrange("(p s q c) -> s c p q", p=PS, s=2, q=QH)
        tb = W["L0_tok_ln1_b"].rearrange("(p s q c) -> s c p q", p=PS, s=2, q=QH)
        for s in range(2):
            for c in range(C):
                part = (s * C + c) * PS
                load(tokraw[part:part + PS], tw[s, c])
                load(tok_g[part:part + PS], tg[s, c])
                load(tok_bb[part:part + PS], tb[s, c])
        for dst, name, n in ((tok_brow, "L0_tok_b", HT), (ln2g, "L0_tok_ln2_g", HT),
                             (ln2b, "L0_tok_ln2_b", HT), (bprow, "L0_attn_b_proj", HT),
                             (fbo, "L0_ffn_bo", SELP), (fbm, "L0_ffn_bm", HT),
                             (bf2, "L0_ffn_bf2", HT)):
            load(dst[:], W[name].partition_broadcast(n))
        wa = W["L0_attn_w_attn"]
        for chunk, (lo, hi) in enumerate(KC):
            size = hi - lo
            for p in (0,) if chunk == 0 else (0, 64):
                for j, name in enumerate(("wq", "wk")):
                    for r in (0, DH):
                        load(raw[name][p:p + size, chunk].rearrange(
                                 "p (h e) -> p h e", e=32)[:, :, r:r + DH],
                             wa[lo:hi, j * D:(j + 1) * D].rearrange("p (h e) -> p h e", e=DH))
                load(raw["wv"][p:p + size, chunk], wa[lo:hi, 2 * D:3 * D])
                for dst, name in (("fwk", "Wk"), ("fwv", "Wv"), ("w1", "W1")):
                    load(raw[dst][p:p + size, chunk], W["L0_ffn_" + name][lo:hi])
                load(wr[p:p + size, chunk:chunk + 1], W["L0_ffn_Wr"][lo:hi].unsqueeze(1))
            for dst, name in ((fwq, "Wq"), (fwm, "Wm"), (fwo, "Wo")):
                load(dst[0:size, chunk], W["L0_ffn_" + name][lo:hi])
            for dst, name in ((g1, "g1"), (b1, "b1"), (g2, "g2"), (b2, "b2"), (fbq, "bq"),
                              (fbk, "bk"), (fbv, "bv")):
                load(dst[0:size, chunk:chunk + 1], W["L0_ffn_" + name][lo:hi].unsqueeze(1))
        ba = W["L0_attn_b_attn"].rearrange("(j g s e) -> j s e g", j=3, g=NG, s=4)
        wpr = W["L0_attn_w_proj"].rearrange("(g s e) m -> s e g m", g=NG, s=4)
        rel = W["L0_attn_rel_emb"]
        for s in range(4):
            for r in (0, DH):
                at = 32 * s + r
                load(bk[at:at + DH], ba[1, s])
                load(rel4[1:HT, 0, at:at + DH], rel[0:HT - 1])
                load(rel4[0:HT, 1, at:at + DH], rel[HT - 1:T - 1])
            load(bv[32 * s:32 * s + DH], ba[2, s])
            load(wp[32 * s:32 * s + DH], wpr[s])
        for row in (0, 32):
            for r in (0, DH):
                load(bqrow[row:row + 1].rearrange("p (h e) -> p h e", e=32)[:, :, r:r + DH],
                     W["L0_attn_b_attn"][0:D].rearrange("(o h e) -> o h e", o=1, e=DH))
        load(br[:], W["L0_ffn_br"].unsqueeze(0).partition_broadcast(128))
        load(bf1[:], W["L0_ffn_bf1"].rearrange("(k p) -> p k", p=128))
        load(w2[:], W["L0_ffn_W2"].rearrange("(k p) m -> p k m", p=128))
        all_loaded = 16 * len(loads)

        @block.sync
        def _(sp):
            load_x(sp, 0)
            sp.wait_ge(one["zeroed"], 1)
            for dst, src in loads:
                sp.dma_start(dst, src).then_inc(one["w_in"], 16)

            def prefetch(j, image):
                sp.wait_ge(sem["tok_mm"], after("tok_mm", j))
                sp.wait_ge(sem["sq_sb"], after("sq_sb", j))
                load_x(sp, image)

            def store(j):
                sp.wait_ge(sem["out_sb"], after("out_sb", j))
                sp.dma_start(out[j].rearrange("(t p) d -> p t d", p=HT),
                             out_row[:]).then_inc(sem["out_done"], 16)

            prefetch(0, 1)
            prefetch(1, 2)
            with sp.Fori(0, B - 3) as j:
                prefetch(j + 2, j + 3)
                store(j)
            for j in range(B - 3, B):
                store(j)
            sp.wait_ge(sem["out_done"], 16 * B)

        @block.gpsimd
        def _(gp):
            for t in (bv, wp, out_row, p0):
                gp.memset(t[:], 0.0)
            gp.drain().then_inc(one["zeroed"], 1)
            gp.memset(ident[:], 0.0)
            gp.memset(identh[:], 0.0)
            gp.memset(tri[:], 0.0)
            gp.memset(before[:], 1.0)
            gp.memset(notbefore[:], 1.0)
            gp.memset(slot_of[:], 1.0)
            gp.memset(diag_of[:], 1.0)
            gp.memset(stack32[:], 0.0)
            gp.memset(qz[:].bitcast(F32), 0.0)
            gp.memset(ones[:], 1.0)
            gp.memset(epsc[:], EPS)
            gp.memset(nhalf[:], -0.5)
            gp.memset(v_sb[:], 0.0)
            for t in (pT0, pT1, diag, tokw):
                gp.memset(t[:], 0.0)
            gp.drain()
            gp.memset(tokw[0:KX], 1.0)
            gp.drain()
            gp.memset(x_sb[KX:128], 0.0)
            gp.drain()
            gp.iota(iota32[:], [[1, SELP]], base=0, channel_multiplier=0,
                    allow_small_or_imprecise_dtypes=True)
            gp.drain()

            def select(t, op, fill, base, mult, pattern):
                gp.affine_select(out=t, in_=t, compare_op=op, fill=fill, base=base,
                                 pattern=pattern, channel_multiplier=mult)

            select(ident[:], ALU.not_equal, 1.0, 0, 1, [[-1, 128]])
            select(identh[:], ALU.not_equal, 1.0, 0, 1, [[-1, HT]])
            select(tri[:], ALU.is_ge, NEG, 0, 1, [[-1, HT]])
            for t in range(2):
                select(before[:, t], ALU.is_ge, 0.0, HT * t - 1, 1, [[-1, T]])
                select(notbefore[:, t], ALU.is_ge, 0.0, -HT * t, -1, [[1, T]])
            select(slot_of[:], ALU.is_ge, 0.0, 0, 1, [[-DH, 8]])
            select(diag_of[:], ALU.is_ge, 0.0, 0, 1, [[-32, 4], [0, DH]])
            for r in range(4):
                gp.drain()
                select(stack32[:], ALU.not_equal, 1.0, -32 * r, 1, [[-1, SELP]])
            select(slot_of[:], ALU.is_ge, 0.0, DH - 1, -1, [[DH, 8]])
            select(diag_of[:], ALU.is_ge, 0.0, 31, -1, [[32, 4], [0, DH]])
            gp.drain().then_inc(one["consts_made"], 1)
            gp.wait_ge(one["w_ready"], 1)
            gp.memset(p1[:], 0.0)
            gp.drain().then_inc(one["p1_zeroed"], 1)

            def rstd(var, ve, r, name):
                gp.tensor_tensor(ve, var, epsc[:], ALU.add)
                gp.drain()
                gp.tensor_tensor(r, ve, nhalf[:], ALU.pow).then_inc(sem[name], 1)

            def both(t):
                return t[:].unsqueeze(1).broadcast_to([HT, 2, D])

            def step(m, n, l, head, front, back, again):
                def h1_with_bias():
                    if back:
                        gp.wait_ge(sem["h2_sb"], all_before("h2_sb", n))
                    gp.tensor_tensor(h1b[:], h1[:], both(bp), ALU.add).then_inc(sem["h1b_sb"], 1)

                def diagonals(s):
                    gp.wait_ge(sem["rden_sb"], after("rden_sb", n, s + 1))
                    gp.tensor_tensor(
                        diag[0:HT, s].rearrange("p t g i -> p (t g) i"),
                        ident[0:HT, 0:HT].unsqueeze(1).broadcast_to([HT, 2 * NG, HT]),
                        rden[:, s].rearrange("p t g -> p (t g)").unsqueeze(2).broadcast_to(
                            [HT, 2 * NG, HT]), ALU.mult).then_inc(sem["diag_sb"], 1)

                if front:
                    h1_with_bias()
                if back:
                    gp.tensor_tensor(h2b[:], h2[:], both(bf2), ALU.add)
                if front:
                    for i in (2, 3):
                        at = slice(32 * i, 32 * i + 32)
                        gp.drain()
                        if i == 2:
                            gp.wait_ge(sem["qparts_sb"], after("qparts_sb", n))
                        gp.tensor_tensor(qz[at, i], qparts[at].bitcast(F32),
                                         ones[at, 0:1].unsqueeze(2).broadcast_to([32, NG, T]),
                                         ALU.mult).then_inc(sem["qz2_sb"], 1)
                    gp.drain()
                if head:
                    gp.wait_ge(sem["sq_sb"], after("sq_sb", l))
                    gp.tensor_tensor(x_sq[:, :, 0:4], x_sq[:, :, 0:4], x_sq[:, :, 4:8], ALU.add)
                    gp.drain()
                    gp.tensor_tensor(x_sq[:, :, 0:2], x_sq[:, :, 0:2], x_sq[:, :, 2:4], ALU.add)
                    gp.drain()
                    gp.tensor_tensor(sqsum[:].unsqueeze(2), x_sq[:, :, 0:1], x_sq[:, :, 1:2],
                                     ALU.add).then_inc(sem["sqsum_sb"], 1)
                if front:
                    diagonals(0)
                if head:
                    gp.wait_ge(sem["tok_var"], after("tok_var", l))
                    rstd(var1[:], ve1[:], rstd1[:], "tok_rstd")
                if front:
                    diagonals(1)
                if head:
                    gp.wait_ge(sem["y_stat"], after("y_stat", l))
                    rstd(mv_y[:, :, 1], ve2[:], rstd2[:], "y_rstd")
                if front:
                    diagonals(2)
                if head:
                    gp.wait_ge(sem["y_norm"], after("y_norm", l))
                    gp.tensor_tensor(y_row[:], y_row[:], both(ln2g), ALU.mult)
                    gp.drain()
                    gp.tensor_tensor(h1[:], y_row[:], both(ln2b), ALU.add).then_inc(sem["h1_sb"], 1)
                if front:
                    diagonals(3)
                if head:
                    gp.wait_ge(sem["h1_stat"], after("h1_stat", l))
                    rstd(mv_a[:, :, 1], ve3[:], rstd3[:], "h1_rstd")
                if back:
                    gp.wait_ge(sem["h3_stat"], after("h3_stat", m))
                    rstd(mv_3[:, :, 1], ve5[:], rstd5[:], "h3_rstd")
                    gp.tensor_tensor(res[:], h2b[:], h3[:], ALU.add).then_inc(sem["res_sb"], 1)
                if front:
                    gp.wait_ge(sem["h2_stat"], after("h2_stat", n))
                    v = mv_f[:, :, 1]
                    ve, r, rr, vr, vn, r2 = (vf[:, i, :] for i in range(6))
                    gp.tensor_tensor(ve, v, epsc[:], ALU.add)
                    gp.drain()
                    gp.tensor_tensor(r, ve, nhalf[:], ALU.pow)
                    gp.drain()
                    gp.tensor_tensor(rr, r, r, ALU.mult)
                    gp.drain()
                    gp.tensor_tensor(vr, rr, v, ALU.mult)
                    gp.drain()
                    gp.tensor_tensor(vn, vr, epsc[:], ALU.add)
                    gp.drain()
                    gp.tensor_tensor(vr, vn, nhalf[:], ALU.pow)
                    gp.drain()
                    gp.tensor_tensor(r2, r, vr, ALU.mult).then_inc(sem["h2_rstd"], 1)

            steps(gp, step)

        @block.tensor
        def _(pe):
            mm = pe.matmul
            pe.wait_ge(one["w_in"], all_loaded)
            pe.wait_ge(one["consts_made"], 1)
            pe.wait_ge(one["w_scaled"], 1)
            for q in range(QH):
                mm(bank[0][0:KX, 0:D], ones[0:KX, 0:KX], tokw[0:KX, q, 0:D], start=q == 0,
                   stop=q == QH - 1)
            for q in range(QH):
                mm(bank[1][0:HT, 0:D], tok_brep[:, q], tokraw[:, q], start=q == 0, stop=q == QH - 1)
            for g in range(NG):
                mm(bank[2][0:HT, 0:D], bvrep[:, g], wp[:, g], start=g == 0, stop=g == NG - 1)
            for t in range(2):
                last = pe.transpose(bank[3][0:128, HT * t:HT * t + HT], rel4[:, t],
                                    ident[0:HT, 0:HT])
            last.then_inc(one["w_sums"], 1)
            pe.wait_ge(one["w_ready"], 1)

            def rows_to_cols(b, src, name):
                for chunk, (lo, hi) in enumerate(KC):
                    for t in range(2):
                        c0 = chunk * T + t * HT
                        last = pe.transpose(bank[b][0:hi - lo, c0:c0 + HT], src[:, t, lo:hi],
                                            ident[0:HT, 0:HT])
                last.then_inc(sem[name], 1)

            def cols_to_rows(b, src, w, name):
                for t in range(2):
                    for i, (p, wpart) in enumerate(PAIRS):
                        last = mm(bank[b][0:HT, t * D:(t + 1) * D],
                                  src[:, p, HT * t:HT * t + HT], w[:, wpart],
                                  start=i == 0, stop=i == len(PAIRS) - 1)
                last.then_inc(sem[name], 1)

            def cols_to_cols(o, src, w, lo, hi):
                for i, (p, wpart) in enumerate(PAIRS):
                    last = mm(o, w[:, wpart, lo:hi], src[:, p], start=i == 0,
                              stop=i == len(PAIRS) - 1)
                return last

            def group_cols(b0, w, name):
                for g in range(NG):
                    o = bank[b0 + g // 2][:, (g % 2) * T:(g % 2) * T + T]
                    for i, (p, wpart) in enumerate(PAIRS):
                        mm(o, w[:, wpart, 128 * g:128 * g + 128], aT[:, p], start=i == 0,
                           stop=False)
                    if name == "q_mm":
                        last = mm(o, bqparts[:, 128 * g:128 * g + 128], onesr[:], start=False,
                                  stop=True)
                    else:
                        for part in range(2):
                            last = mm(o, identr[:], relk[:, part, g], start=False, stop=part == 1)
                last.then_inc(sem[name], 1)

            def step(m, n, l, head, front, back, again):
                def routed_cols():
                    pe.wait_ge(sem["z0_sb"], after("z0_sb", m))
                    rows_to_cols(5, z0, "zT_mm")

                def queries_keys_values():
                    pe.wait_ge(sem["aTs_sb"], after("aTs_sb", n))
                    if back:
                        pe.wait_ge(sem["h2_sb"], all_before("h2_sb", n))
                    group_cols(0, split["wq"], "q_mm")
                    group_cols(2, split["wk"], "k_mm")
                    cols_to_rows(4, aT, split["wv"], "v_mm")

                def scores(u, b):
                    s, heads = s_unit(u)
                    for i, (c0, cn, w) in enumerate([(0, 2, T)] if u % 2 else
                                                    [(0, 3, HT), (3 * HT, 1, T)]):
                        o = bank[b][0:HT, c0:c0 + cn * w].rearrange("p (h w) -> p h w", w=w)
                        mm(o[:, :, w - HT:w], identh[:],
                           tri[:].unsqueeze(1).broadcast_to([HT, cn, HT]), start=i == 0,
                           stop=False, skip_group_check=True)
                    for i, (g, t, c0) in enumerate(heads):
                        w = T if t else HT
                        for part in (khi, klo):
                            last = mm(bank[b][0:HT, c0:c0 + w],
                                      qz[:, s, g, HT * t:HT * t + HT], part[:, g, 0:w],
                                      start=False, stop=i == len(heads) - 1 and part is klo,
                                      skip_group_check=True)
                    last.then_inc(sem["s_mm"], 1)

                def patches(b, t):
                    xf = x_sb[:].rearrange("p h w -> p (h w)")
                    for q in range(QH):
                        a = t * HT * PS + q
                        mm(bank[b][0:HT, t * (D + 1):(t + 1) * (D + 1)],
                           xf[:, a:a + (HT - 1) * PS + 1:PS], tokw[:, q],
                           start=t == 0 and q == 0, stop=q == QH - 1, skip_group_check=True)

                def square_sums(b):
                    pe.wait_ge(sem["sqsum_sb"], after("sqsum_sb", l))
                    for t in range(2):
                        last = mm(bank[b][0:HT, 2 * D + 2 + t:2 * D + 3 + t],
                                  sqsum[:, HT * t:HT * t + HT], ones[0:KX, 0:1], start=False,
                                  stop=True, skip_group_check=True)
                    last.then_inc(sem["tok_mm"], 1)

                def transposes(kind, k, b):
                    if kind == "A":
                        blocks = [(2 * k + i, t, 0) for i in range(2) for t in range(2)]
                    else:
                        blocks = [(4 * k + i, 1, 1) for i in range(4)]
                    for i, (h, t, u) in enumerate(blocks):
                        src = p1[:, h, HT * u:HT * u + HT] if t else p0[:, h]
                        last = mm(bank[b][0:HT, HT * i:HT * i + HT], src, diag[:, h // 3, t, h % 3],
                                  start=True, stop=True)
                    last.then_inc(sem["p_T"], 1)

                def bank_free(name):
                    i = ORDER.index(name)
                    before_it = [o for o in ORDER[:i] if RING[o] == RING[name]]
                    if not before_it:
                        return
                    o = before_it[-1]
                    if o[0] == "S" and front:
                        pe.wait_ge(sem["probs"], after("probs", n, int(o[1:]) + 1))
                    elif o[0] == "T" and head:
                        pe.wait_ge(sem["tok_y"], after("tok_y", l))
                    elif o[0] in "AB":
                        engine, count = evacuation(o)
                        pe.wait_ge(sem[engine], after(engine, n, count))

                def causal(name):
                    kind, k = name[0], int(name[1:])
                    bank_free(name)
                    if kind == "S":
                        if k == 0:
                            pe.wait_ge(sem["klo_sb"], after("klo_sb", n))
                        if k % 2 == 0:
                            by = "qz_sb" if k < 4 else "qz2_sb"
                            pe.wait_ge(sem[by], after(by, n, k // 2 % 2 + 1))
                        scores(k, RING[name])
                    else:
                        s = (2 * k + 1 if kind == "A" else 4 * k + 3) // 3
                        pe.wait_ge(sem["diag_sb"], after("diag_sb", n, s + 1))
                        transposes(kind, k, RING[name])

                def embed(t):
                    if t == 0:
                        bank_free("T0")
                        pe.wait_ge(sem["x_in"], after("x_in", l))
                    patches(RING["T0"], t)
                    if t == 1:
                        square_sums(RING["T0"])

                def score():
                    pe.wait_ge(sem["nTs_sb"], after("nTs_sb", m))
                    if again:
                        pe.wait_ge(sem["out_sb"], all_before("out_sb", m))
                    cols_to_cols(bank[6][:, 0:T], nTs, split["wr"], 0, 128).then_inc(
                        sem["score_mm"], 1)

                def keys_values2():
                    for mt, (mlo, mhi) in enumerate(KC):
                        last = cols_to_cols(bank[7][0:mhi - mlo, mt * T:mt * T + T], nTs,
                                            split["fwk"], mlo, mhi)
                    last.then_inc(sem["kk_mm"], 1)
                    cols_to_rows(5, nTs, split["fwv"], "vv_mm")

                def gather():
                    pe.wait_ge(sem["sel_sb"], after("sel_sb", m))
                    for chunk, (lo, hi) in enumerate(KC):
                        for t in range(2):
                            mm(bank[6][0:hi - lo, chunk * SELP:(chunk + 1) * SELP],
                               z0[:, t, lo:hi], sel[:, t], start=t == 0, stop=t == 1)
                    for t in range(2):
                        last = pe.transpose(bank[6][0:SELP, 64 + HT * t:64 + HT * t + HT],
                                            sel[:, t], ident[0:HT, 0:HT])
                    last.then_inc(sem["gather_mm"], 1)

                def qsel():
                    pe.wait_ge(sem["nsel_sb"], after("nsel_sb", m))
                    for mt, (mlo, mhi) in enumerate(KC):
                        for chunk, (lo, hi) in enumerate(KC):
                            last = mm(bank[7][0:mhi - mlo, mt * SELP:(mt + 1) * SELP],
                                      fwq[0:hi - lo, chunk, mlo:mhi], cols(nsel, chunk),
                                      start=chunk == 0, stop=chunk == 1)
                    last.then_inc(sem["qsel_mm"], 1)

                def scores2():
                    pe.wait_ge(sem["qb_sb"], after("qb_sb", m))
                    if front:
                        pe.wait_ge(sem["v_sb"], after("v_sb", n))
                    mm(bank[5][:, 0:T], qb0[:, 0:4], kk[:, 0], start=True, stop=True)
                    mm(bank[5][:, T:2 * T], qb0[:, 4:8], kk[:, 0], start=True, stop=True)
                    mm(bank[4][:, 0:T], qb1[:], kk[0:64, 1], start=True,
                       stop=True).then_inc(sem["s2_mm"], 1)

                def transposes2():
                    pe.wait_ge(sem["probs2"], after("probs2", m))
                    pe.wait_ge(sem["f1_sb"], after("f1_sb", m))
                    for t in range(2):
                        for g in range(NG):
                            last = pe.transpose(bank[6 + t][0:HT, 128 * g:128 * g + 128],
                                                probs2[:, g, HT * t:HT * t + HT], ident[:])
                    last.then_inc(sem["p2_T"], 1)

                def context2():
                    pe.wait_ge(sem["p2T_sb"], after("p2T_sb", m))
                    for g in range(NG):
                        for t in range(2):
                            last = mm(bank[5][:, 64 * g:64 * g + 64],
                                      p2T[:, t, 128 * g:128 * g + 128],
                                      vv[:, t, 64 * g:64 * g + 64], start=t == 0, stop=t == 1)
                    last.then_inc(sem["ctx_mm"], 1)

                def mix():
                    pe.wait_ge(sem["mT_sb"], after("mT_sb", m))
                    for t in range(2):
                        for chunk, (lo, hi) in enumerate(KC):
                            last = mm(bank[7][0:HT, t * D:(t + 1) * D],
                                      mT[0:hi - lo, chunk, HT * t:HT * t + HT],
                                      fwm[0:hi - lo, chunk], start=chunk == 0, stop=chunk == 1)
                    last.then_inc(sem["mix_mm"], 1)

                def context2_cols():
                    pe.wait_ge(sem["ctx_sb"], after("ctx_sb", m))
                    mm(bank[4][:, 0:SELP], ctxm[:, 0:2], stack32[:], start=True, stop=True)
                    last = mm(bank[4][0:64, SELP:2 * SELP], ctxm[:, 2], stack32[:], start=True,
                              stop=True)
                    last.then_inc(sem["ctxT_mm"], 1)

                def attn_out():
                    pe.wait_ge(sem["ctxT_sb"], after("ctxT_sb", m))
                    for chunk in range(2):
                        last = mm(bank[6][0:SELP, 0:D], cols(ctxT, chunk), cols(fwo, chunk),
                                  start=chunk == 0, stop=chunk == 1)
                    last.then_inc(sem["ao_mm"], 1)

                def scatter():
                    pe.wait_ge(sem["ao_sb"], after("ao_sb", m))
                    for t in range(2):
                        last = mm(bank[5][0:HT, t * D:(t + 1) * D],
                                  selT[0:NSEL, HT * t:HT * t + HT], ao[0:NSEL], start=True,
                                  stop=True)
                    last.then_inc(sem["scat_mm"], 1)

                def attention():
                    pe.wait_ge(sem["pT_dve"], after("pT_dve", n))
                    pe.wait_ge(sem["pT_act"], after("pT_act", n))
                    for g in range(NG):
                        o = bank[2 + g // 2][:, (g % 2) * T:(g % 2) * T + T]
                        for s in range(4):
                            mm(o[32 * s:32 * s + 32], v_sb[:, 0, 4 * g + s], pT0[:, 3 * s + g],
                               start=True, stop=False)
                        for s in range(4):
                            last = mm(o[32 * s:32 * s + 32, HT:T], v_sb[:, 1, 4 * g + s],
                                      pT1[:, 3 * s + g], start=False, stop=True)
                    last.then_inc(sem["y_mm"], 1)

                def projection():
                    pe.wait_ge(sem["yT_sb"], after("yT_sb", n))
                    for t in range(2):
                        for g in range(NG):
                            last = mm(bank[0][0:HT, t * D:(t + 1) * D],
                                      yT[:, g, HT * t:HT * t + HT], wp[:, g], start=g == 0,
                                      stop=g == NG - 1)
                    last.then_inc(sem["proj_mm"], 1)

                def mlp_cols():
                    pe.wait_ge(sem["z3_sb"], after("z3_sb", m))
                    rows_to_cols(6, z3, "z3_T")

                def up():
                    pe.wait_ge(sem["n2Ts_sb"], after("n2Ts_sb", m))
                    for f in range(F // 128):
                        last = cols_to_cols(bank[(4, 5, 7)[f // 2]][:, T * (f % 2):T * (f % 2) + T],
                                            n2Ts, split["w1"], 128 * f, 128 * f + 128)
                        if f % 2:
                            last.then_inc(sem["up_mm"], 1)

                def down(j):
                    pe.wait_ge(sem["gelu_sb"], after("gelu_sb", m, j + 1))
                    for f in (2 * j, 2 * j + 1):
                        for t in range(2):
                            last = mm(bank[6][0:HT, t * D:(t + 1) * D],
                                      gT[:, f, HT * t:HT * t + HT], w2[:, f],
                                      start=f == 0 and t == 0, stop=f == F // 128 - 1,
                                      skip_group_check=True)
                    if j == 2:
                        last.then_inc(sem["down_mm"], 1)

                def attention_cols():
                    pe.wait_ge(sem["a_sb"], after("a_sb", l))
                    if front and not back:
                        pe.wait_ge(sem["v_sb"], after("v_sb", n))
                    rows_to_cols(4, a_row, "aT_mm")

                if back:
                    routed_cols()
                if front:
                    queries_keys_values()
                if back:
                    score()
                    keys_values2()
                if front:
                    causal("S0")
                    causal("S1")
                    causal("S2")
                if head:
                    embed(0)
                if front:
                    causal("S3")
                    causal("S4")
                if back:
                    gather()
                if front:
                    causal("S5")
                if head:
                    embed(1)
                if back:
                    qsel()
                if front:
                    causal("S6")
                if back:
                    scores2()
                if front:
                    causal("S7")
                    causal("A0")
                if back:
                    mix()
                if front:
                    causal("A1")
                    causal("A2")
                if back:
                    transposes2()
                if front:
                    causal("B0")
                if back:
                    context2()
                if front:
                    causal("A3")
                    causal("B1")
                if back:
                    context2_cols()
                if front:
                    causal("A4")
                if back:
                    attn_out()
                if front:
                    causal("A5")
                if back:
                    scatter()
                if front:
                    causal("B2")
                    attention()
                if back:
                    mlp_cols()
                if front:
                    projection()
                if back:
                    up()
                    down(0)
                    down(1)
                if head:
                    attention_cols()
                if back:
                    down(2)
            steps(pe, step)

        @block.vector
        def _(ve):
            ve.wait_ge(one["w_in"], all_loaded)
            ve.wait_ge(one["consts_made"], 1)
            for q in range(QH):
                ve.tensor_scalar(tokw[0:KX, q, 0:D], tokraw[:, q], tok_g[:, q:q + 1], None, ALU.mult)
            ve.tensor_copy(tok_brep[:], tok_bb[:].unsqueeze(2).broadcast_to([KX, QH, HT]))
            ve.tensor_copy(bvrep[:], bv[:].unsqueeze(2).broadcast_to([128, NG, HT]))
            for chunk, (lo, hi) in enumerate(KC):
                size = hi - lo
                ve.tensor_scalar(fbqs[0:size, chunk:chunk + 1], fbq[0:size, chunk:chunk + 1], QSCALE,
                                 None, ALU.mult)
            ve.tensor_copy(raw["wr"][:], wr[:].unsqueeze(2).broadcast_to([128, 2, 128]))
            ve.tensor_scalar(raw["wq"], raw["wq"], QSCALE, None, ALU.mult)
            ve.tensor_scalar(bqrow, bqrow, QSCALE, None, ALU.mult)
            ve.tensor_copy(identr[:], ident[:])
            ve.tensor_copy(onesr[:], ones[0:64, 0:1].broadcast_to([64, T]))
            for g in range(NG):
                ve.tensor_copy(relb[:, g], bk[:, g:g + 1].broadcast_to([128, T]))
            ve.tensor_reduce(hi_half[:], stack32[:, 0:DH], AX.X, ALU.add)
            ve.drain().then_inc(one["w_scaled"], 1)
            ve.tensor_scalar(lo_rows[:], hi_half[:], 1.0, None, ALU.subtract)
            for name, w in raw.items():
                ve.tensor_copy(split[name][:, 0::2], w[:])
            ve.tensor_copy(bqparts[:], bqrow)
            ve.drain()
            ve.tensor_tensor(bqparts[32:64], bqrow[32:64], bqparts[32:64].bitcast(F32),
                             ALU.subtract)
            for name, w in raw.items():
                ve.tensor_tensor(split[name][:, 1::2], w[:], split[name][:, 0::2].bitcast(F32),
                                 ALU.subtract)
            ve.wait_ge(one["w_sums"], 1)
            for q in range(QH):
                ve.scalar_tensor_tensor(tokw[0:KX, q, 0:D], bank[0][0:KX, 0:D], -1.0 / PD,
                                        tokw[0:KX, q, 0:D], ALU.mult, ALU.add)
            ve.tensor_tensor(tok_bias[:], bank[1][0:HT, 0:D], tok_brow[:], ALU.add)
            ve.tensor_tensor(bp[:], bank[2][0:HT, 0:D], bprow[:], ALU.add)
            for g in range(NG):
                ve.tensor_tensor(relb[:, g], bank[3][:, 0:T], relb[:, g], ALU.add)
            ve.drain()
            ve.tensor_copy(relk[:, 0], relb)
            ve.drain()
            ve.tensor_tensor(relk[:, 1], relb, relk[:, 0].bitcast(F32), ALU.subtract)
            ve.drain().then_inc(one["w_ready"], 1)

            def stats(src, bn, mv, name):
                for t in range(2):
                    ve.bn_stats(bn[:, t], src[:, t])
                ve.drain()
                for t in range(2):
                    last = ve.bn_aggr(mv[:, t], bn[:, t])
                last.then_inc(sem[name], 1)

            def normalise(dst, src, mv, r, name):
                for t in range(2):
                    last = ve.tensor_scalar(dst[:, t], src[:, t], mv[:, t, 0:1], r[:, t:t + 1],
                                            ALU.subtract, ALU.mult)
                last.then_inc(sem[name], 1)

            def split_cols(dst, src, name):
                ve.tensor_copy(dst[:, 0], src[:, 0])
                ve.tensor_copy(dst[0:64, 2], src[0:64, 1])
                ve.drain()
                ve.tensor_tensor(dst[:, 1], src[:, 0], dst[:, 0].bitcast(F32), ALU.subtract)
                ve.tensor_tensor(dst[64:128, 2], src[0:64, 1], dst[0:64, 2].bitcast(F32),
                                 ALU.subtract).then_inc(sem[name], 1)

            def rows(b):
                return bank[b][0:HT, 0:2 * D].rearrange("p (t d) -> p t d", t=2)

            def step(m, n, l, head, front, back, again):
                def attention_cols_lo():
                    ve.wait_ge(sem["aT_sb"], after("aT_sb", l))
                    ve.tensor_tensor(aT[:, 1], bank[4][:, 0:T], aT[:, 0].bitcast(F32), ALU.subtract)
                    ve.tensor_tensor(aT[64:128, 2], bank[4][0:64, T:2 * T],
                                     aT[0:64, 2].bitcast(F32),
                                     ALU.subtract).then_inc(sem["aTs_sb"], 1)

                def routed_cols():
                    ve.wait_ge(sem["nT_sb"], after("nT_sb", m))
                    split_cols(nTs, nT, "nTs_sb")

                def query_parts():
                    ve.wait_ge(sem["qhi_sb"], after("qhi_sb", n))
                    for b, g0, gn in ((0, 0, 2), (1, 2, 1)):
                        last = ve.scalar_tensor_tensor(
                            qparts[:, g0:g0 + gn].rearrange("p g t -> p (g t)"),
                            qhi[:, g0:g0 + gn].rearrange("p g t -> p (g t)").bitcast(F32),
                            lo_rows[:], bank[b][:, 0:gn * T], ALU.mult, ALU.add)
                    last.then_inc(sem["qparts_sb"], 1)
                    ve.drain()

                def slot_queries(s):
                    at = slice(32 * s, 32 * s + 32)
                    ve.tensor_copy(qz[at, s], qparts[at].bitcast(F32)).then_inc(sem["qz_sb"], 1)

                def keys():
                    ve.wait_ge(sem["khi_sb"], after("khi_sb", n))
                    for b, g0, gn in ((2, 0, 2), (3, 2, 1)):
                        last = ve.tensor_tensor(
                            klo[:, g0:g0 + gn].rearrange("p g t -> p (g t)"), bank[b][:, 0:gn * T],
                            khi[:, g0:g0 + gn].rearrange("p g t -> p (g t)").bitcast(F32),
                            ALU.subtract)
                    last.then_inc(sem["klo_sb"], 1)

                def maxima(k):
                    ve.wait_ge(sem["s_mm"], after("s_mm", n, k + 1))
                    b, s = RING[f"S{k}"], k // 2
                    parts = ([(1, 0, 2, 0, T)] if k % 2 else
                             [(0, 0, 3, 0, HT), (1, 2, 1, 3 * HT, T)])
                    for t, g, gn, c0, w in parts:
                        last = ve.tensor_reduce(
                            negmax[:, s, t, g:g + gn],
                            bank[b][0:HT, c0:c0 + w * gn].rearrange("p (h w) -> p h w", w=w),
                            AX.X, ALU.max, negate=True)
                    last.then_inc(sem["rowmax"], 1)

                def transposed(name):
                    ve.wait_ge(sem["p_T"], after("p_T", n, PT.index(name) + 1))
                    ve.tensor_copy(pt_dst(name[0], int(name[1:])),
                                   bank[RING[name]][0:HT, 0:4 * HT]).then_inc(sem["pT_dve"], 1)

                def inverse_sums(s):
                    ve.wait_ge(sem["probs"], after("probs", n, 2 * s + 2))
                    ve.reciprocal(rden[:, s], den[:, s]).then_inc(sem["rden_sb"], 1)

                tok_bank = RING["T0"]
                tok = bank[tok_bank][0:HT, 0:2 * (D + 1)].rearrange("p (t d) -> p t d", t=2)

                def patch_variance():
                    ve.wait_ge(sem["tok_mm"], after("tok_mm", l))
                    ve.tensor_scalar(mean1[:], tok[:, :, D], 1.0 / PD, None, ALU.mult)
                    ve.drain()
                    ve.tensor_tensor(msq1[:], mean1[:], mean1[:], ALU.mult)
                    ve.drain()
                    ve.scalar_tensor_tensor(var1[:], bank[tok_bank][0:HT, 2 * D + 2:2 * D + 4],
                                            1.0 / PD, msq1[:], ALU.mult,
                                            ALU.subtract).then_inc(sem["tok_var"], 1)

                def embedding():
                    ve.wait_ge(sem["tok_rstd"], after("tok_rstd", l))
                    for t in range(2):
                        last = ve.scalar_tensor_tensor(y_row[:, t], tok[:, t, 0:D],
                                                       rstd1[:, t:t + 1], tok_bias[:], ALU.mult,
                                                       ALU.add)
                    last.then_inc(sem["tok_y"], 1)
                    ve.drain()
                    stats(y_row, bn_y, mv_y, "y_stat")

                def embedding_normalised():
                    ve.wait_ge(sem["y_rstd"], after("y_rstd", l))
                    normalise(y_row, y_row, mv_y, rstd2, "y_norm")

                def h1_stats():
                    ve.wait_ge(sem["h1_sb"], after("h1_sb", l))
                    stats(h1, bn_a, mv_a, "h1_stat")

                def attention_input():
                    ve.wait_ge(sem["h1_rstd"], after("h1_rstd", l))
                    normalise(a_row, h1, mv_a, rstd3, "a_sb")

                def routing_scores():
                    ve.wait_ge(sem["score_mm"], after("score_mm", m))
                    ve.tensor_scalar(zrow[:], bank[6][:, 0:T], br[:], None,
                                     ALU.add).then_inc(sem["z_sb"], 1)

                def rank_tokens():
                    ve.drain()
                    ve.tensor_scalar(zclip[:], zrow[:], TOPZ, -88.0, ALU.min, ALU.max)
                    ve.drain()
                    for t in range(2):
                        ve.tensor_tensor_reduce(scr[:, t, 0:HT], zclip[0:HT, HT * t:HT * t + HT],
                                                ident[0:HT, 0:HT], 1.0, 0.0, ALU.mult, ALU.add,
                                                zi[:, t:t + 1])
                    ve.drain()
                    for t in range(2):
                        ve.scalar_tensor_tensor(scr[:, t], zclip[0:HT], zi[:, t:t + 1],
                                                before[:, t], ALU.is_le, ALU.mult,
                                                accum_out=cnt[:, 0, t:t + 1])
                        ve.scalar_tensor_tensor(scr[:, 2 + t], zclip[0:HT], zi[:, t:t + 1],
                                                notbefore[:, t], ALU.is_lt, ALU.mult,
                                                accum_out=cnt[:, 1, t:t + 1])
                    ve.drain()
                    ve.tensor_tensor(rank[:], cnt[:, 0], cnt[:, 1], ALU.add)
                    ve.drain()
                    ve.tensor_scalar(keep[:], rank[:], NSEL - 0.5, None, ALU.is_ge)
                    for t in range(2):
                        last = ve.tensor_scalar(sel[:, t], iota32[:], rank[:, t:t + 1], None,
                                                ALU.is_equal)
                    last.then_inc(sem["sel_sb"], 1)

                def sigmoid():
                    ve.wait_ge(sem["expz"], after("expz", m))
                    ve.tensor_scalar(ez[:], ez[:], 1.0, None, ALU.add)
                    ve.drain()
                    ve.reciprocal(sig[:], ez[:])

                def pool_tokens():
                    ve.drain()
                    ve.tensor_scalar(scr2[:, 2], sig[:], 1.0, None, ALU.mult, ALU.add,
                                     accum_out=ssum[:])
                    for chunk, (lo, hi) in enumerate(KC):
                        size = hi - lo
                        ve.tensor_tensor_reduce(scr2[0:size, chunk], nT[0:size, chunk], sig[0:size], 1.0,
                                                0.0, ALU.mult, ALU.add,
                                                pool_raw[0:size, chunk:chunk + 1])
                    ve.drain()
                    ve.tensor_scalar(sse[:], ssum[:], 1e-6, None, ALU.add)
                    ve.drain()
                    ve.reciprocal(rss[:], sse[:])
                    ve.drain()
                    for chunk, (lo, hi) in enumerate(KC):
                        size = hi - lo
                        ve.tensor_scalar(pooled[0:size, chunk:chunk + 1],
                                         pool_raw[0:size, chunk:chunk + 1], rss[0:size], None, ALU.mult)
                    ve.drain()
                    for chunk, (lo, hi) in enumerate(KC):
                        size = hi - lo
                        last = ve.scalar_tensor_tensor(mT[0:size, chunk], sig[0:size],
                                                       pooled[0:size, chunk:chunk + 1],
                                                       nT[0:size, chunk], ALU.mult, ALU.add)
                    last.then_inc(sem["mT_sb"], 1)

                def q_blocks():
                    ve.wait_ge(sem["qs_sb"], after("qs_sb", m))
                    ve.tensor_tensor(qb0[:], qs[:, 0:1].broadcast_to([128, 8, SELP]),
                                     slot_of[:].unsqueeze(2).broadcast_to([128, 8, SELP]),
                                     ALU.mult)
                    ve.tensor_tensor(qb1[:], qs[0:64, 1:2].broadcast_to([64, 4, SELP]),
                                     slot_of[0:64, 0:4].unsqueeze(2).broadcast_to([64, 4, SELP]),
                                     ALU.mult).then_inc(sem["qb_sb"], 1)

                def max2():
                    ve.wait_ge(sem["s2_mm"], after("s2_mm", m))
                    ve.tensor_reduce(negmax2[:, 0:2],
                                     bank[5][:, 0:2 * T].rearrange("p (g t) -> p g t", g=2), AX.X,
                                     ALU.max, negate=True)
                    ve.tensor_reduce(negmax2[:, 2:3], bank[4][:, 0:T], AX.X, ALU.max,
                                     negate=True).then_inc(sem["max2"], 1)

                def context2():
                    ve.wait_ge(sem["probs2"], after("probs2", m))
                    ve.reciprocal(rden2[:], den2[:])
                    ve.drain()
                    ve.wait_ge(sem["ctx_mm"], after("ctx_mm", m))
                    for g in range(NG):
                        last = ve.scalar_tensor_tensor(
                            ctxm[:, g], bank[5][:, 64 * g:64 * g + 64], rden2[:, g:g + 1],
                            diag_of[:].rearrange("p h e -> p (h e)"), ALU.mult, ALU.mult)
                    last.then_inc(sem["ctx_sb"], 1)

                def context2_cols():
                    ve.wait_ge(sem["ctxT_mm"], after("ctxT_mm", m))
                    for chunk, (lo, hi) in enumerate(KC):
                        size = hi - lo
                        last = ve.tensor_scalar(ctxT[0:size, chunk],
                                                bank[4][0:size, SELP * chunk:SELP * (chunk + 1)],
                                                fbv[0:size, chunk:chunk + 1], None, ALU.add)
                    last.then_inc(sem["ctxT_sb"], 1)

                def attn_out():
                    ve.wait_ge(sem["ao_mm"], after("ao_mm", m))
                    ve.tensor_tensor(ao[:], bank[6][0:SELP, 0:D], fbo[:],
                                     ALU.add).then_inc(sem["ao_sb"], 1)

                def mix():
                    ve.wait_ge(sem["mix_mm"], after("mix_mm", m))
                    ve.tensor_tensor(f1[:], rows(7), fbm[:].unsqueeze(1).broadcast_to([HT, 2, D]),
                                     ALU.add)
                    ve.drain()
                    for t in range(2):
                        last = ve.scalar_tensor_tensor(f1[:, t], f1[:, t], keep[:, t:t + 1],
                                                       f0[:, t], ALU.mult, ALU.add)
                    last.then_inc(sem["f1_sb"], 1)

                def merge():
                    ve.drain()
                    ve.wait_ge(sem["scat_mm"], after("scat_mm", m))
                    ve.tensor_tensor(h3[:], rows(5), f1[:], ALU.add).then_inc(sem["h3_sb"], 1)
                    ve.drain()
                    stats(h3, bn_3, mv_3, "h3_stat")

                def mlp_input():
                    ve.wait_ge(sem["h3_rstd"], after("h3_rstd", m))
                    normalise(z3, h3, mv_3, rstd5, "z3_sb")

                def mlp_cols():
                    ve.wait_ge(sem["n2T_sb"], after("n2T_sb", m))
                    split_cols(n2Ts, n2T, "n2Ts_sb")

                def residual():
                    ve.wait_ge(sem["proj_mm"], after("proj_mm", n))
                    ve.wait_ge(sem["h1b_sb"], after("h1b_sb", n))
                    if back:
                        ve.wait_ge(sem["res_sb"], all_before("res_sb", n))
                    ve.tensor_tensor(h2[:], rows(0), h1b[:], ALU.add).then_inc(sem["h2_sb"], 1)
                    ve.drain()
                    stats(h2, bn_f, mv_f, "h2_stat")

                def routed_input():
                    ve.wait_ge(sem["h2_rstd"], after("h2_rstd", n))
                    normalise(z0, h2, mv_f, vf[:, 5], "z0_sb")
                    normalise(f0, h2, mv_f, vf[:, 1], "f0_sb")

                def output():
                    ve.wait_ge(sem["down_mm"], after("down_mm", m))
                    ve.wait_ge(sem["res_sb"], after("res_sb", m))
                    if again:
                        ve.wait_ge(sem["out_done"], all_before("out_done", m))
                    ve.tensor_tensor(out_row[:], rows(6), res[:], ALU.add).then_inc(sem["out_sb"], 1)

                if back:
                    routed_cols()
                if front:
                    query_parts()
                    slot_queries(0)
                    slot_queries(1)
                    keys()
                if back:
                    routing_scores()
                    sigmoid()
                if front:
                    maxima(0)
                    maxima(1)
                if back:
                    rank_tokens()
                if front:
                    maxima(2)
                    inverse_sums(0)
                    maxima(3)
                    maxima(4)
                    maxima(5)
                    inverse_sums(1)
                if back:
                    pool_tokens()
                if head:
                    patch_variance()
                if back:
                    q_blocks()
                if front:
                    maxima(6)
                if head:
                    embedding()
                if front:
                    inverse_sums(2)
                if back:
                    max2()
                if front:
                    maxima(7)
                    transposed("A0")
                if head:
                    embedding_normalised()
                if back:
                    mix()
                if front:
                    inverse_sums(3)
                    transposed("A2")
                if head:
                    h1_stats()
                if back:
                    context2()
                if front:
                    transposed("A3")
                if back:
                    context2_cols()
                if front:
                    transposed("A4")
                if back:
                    attn_out()
                if head:
                    attention_input()
                if back:
                    merge()
                    mlp_input()
                    mlp_cols()
                if front:
                    residual()
                    routed_input()
                if head:
                    attention_cols_lo()
                if back:
                    output()
            steps(ve, step)

        @block.scalar
        def _(sc):
            sc.wait_ge(one["p1_zeroed"], 1)

            def affine_cols(dst, b, name, scale, bias, width=T):
                for chunk, (lo, hi) in enumerate(KC):
                    size = hi - lo
                    last = sc.activation(
                        dst[0:size, chunk], bank[b][0:size, chunk * width:(chunk + 1) * width],
                        ACT.Identity, bias=bias[0:size, chunk:chunk + 1],
                        scale=scale[0:size, chunk:chunk + 1] if not isinstance(scale, float)
                        else scale)
                if name:
                    last.then_inc(sem[name], 1)

            def step(m, n, l, head, front, back, again):
                def attention_cols_hi():
                    sc.wait_ge(sem["aT_mm"], after("aT_mm", l))
                    sc.copy(aT[:, 0], bank[4][:, 0:T])
                    sc.copy(aT[0:64, 2], bank[4][0:64, T:2 * T]).then_inc(sem["aT_sb"], 1)

                def routed_cols():
                    sc.wait_ge(sem["zT_mm"], after("zT_mm", m))
                    affine_cols(nT, 5, "nT_sb", g1, b1)

                def group_hi(dst, b0, made, name):
                    sc.wait_ge(sem[made], after(made, n))
                    for b, g0, gn in ((b0, 0, 2), (b0 + 1, 2, 1)):
                        last = sc.copy(dst[:, g0:g0 + gn].rearrange("p g t -> p (g t)"),
                                       bank[b][:, 0:gn * T])
                    last.then_inc(sem[name], 1)

                def queries():
                    group_hi(qhi, 0, "q_mm", "qhi_sb")

                def keys():
                    group_hi(khi, 2, "k_mm", "khi_sb")

                def load_table(function):
                    sc.activation(table_out[:], ones[0:1, 0:1], function)

                def squares():
                    sc.wait_ge(sem["x_in"], after("x_in", l))
                    if front:
                        sc.wait_ge(sem["sqsum_sb"], all_before("sqsum_sb", l))
                    xv = x_sb[0:KX].rearrange("p h (w q) -> p (h w) q", q=PS)
                    sc.activation(x_sq[:], xv[:, :, 0:QH], ACT.Square).then_inc(sem["sq_sb"], 1)

                def values():
                    sc.wait_ge(sem["v_mm"], after("v_mm", n))
                    sc.copy(v_sb[0:HT, :, :, 0:DH].rearrange("p t h e -> p (t h) e"),
                            bank[4][0:HT, 0:2 * D].rearrange("p (h e) -> p h e", e=DH)
                            ).then_inc(sem["v_sb"], 1)

                def softmax(k):
                    sc.wait_ge(sem["rowmax"], after("rowmax", n, k + 1))
                    b = RING[f"S{k}"]
                    s, heads = s_unit(k)
                    for g, t, c0 in heads:
                        sc.activation((p1 if t else p0)[0:HT, 3 * s + g],
                                      bank[b][0:HT, c0:c0 + (T if t else HT)],
                                      ACT.Exp, bias=negmax[:, s, t, g:g + 1],
                                      accum_out=den[:, s, t, g:g + 1])
                    sc.drain().then_inc(sem["probs"], 1)

                def transposed(name):
                    sc.wait_ge(sem["p_T"], after("p_T", n, PT.index(name) + 1))
                    sc.copy(pt_dst(name[0], int(name[1:])),
                            bank[RING[name]][0:HT, 0:4 * HT]).then_inc(sem["pT_act"], 1)

                def exp_scores():
                    sc.wait_ge(sem["z_sb"], after("z_sb", m))
                    sc.activation(ez[:], zrow[:], ACT.Exp, scale=-1.0).then_inc(sem["expz"], 1)

                def keys_values2():
                    sc.wait_ge(sem["kk_mm"], after("kk_mm", m))
                    affine_cols(kk, 7, "kk_sb", 1.0, fbk)
                    sc.wait_ge(sem["vv_mm"], after("vv_mm", m))
                    sc.copy(vv[:].rearrange("p t d -> p (t d)"),
                            bank[5][0:HT, 0:2 * D]).then_inc(sem["vv_sb"], 1)

                def gathered():
                    sc.wait_ge(sem["gather_mm"], after("gather_mm", m))
                    affine_cols(nsel, 6, None, g1, b1, SELP)
                    sc.copy(selT[:], bank[6][0:SELP, 64:64 + T]).then_inc(sem["nsel_sb"], 1)

                def queries2():
                    sc.wait_ge(sem["qsel_mm"], after("qsel_mm", m))
                    affine_cols(qs, 7, "qs_sb", QSCALE, fbqs, SELP)

                def softmax2():
                    sc.wait_ge(sem["max2"], after("max2", m))
                    for g in range(NG):
                        src = bank[5][:, T * g:T * g + T] if g < 2 else bank[4][:, 0:T]
                        sc.activation(probs2[:, g], src, ACT.Exp, bias=negmax2[:, g:g + 1],
                                      accum_out=den2[:, g:g + 1])
                    sc.drain().then_inc(sem["probs2"], 1)

                def transposed2():
                    sc.wait_ge(sem["p2_T"], after("p2_T", m))
                    for t in range(2):
                        last = sc.copy(p2T[:, t], bank[6 + t][0:HT, 0:NG * 128])
                    last.then_inc(sem["p2T_sb"], 1)

                def attention():
                    sc.wait_ge(sem["y_mm"], after("y_mm", n))
                    sc.copy(yT[:, 0:2].rearrange("p g t -> p (g t)"), bank[2][:, 0:2 * T])
                    sc.copy(yT[:, 2], bank[3][:, 0:T]).then_inc(sem["yT_sb"], 1)

                def mlp_cols():
                    sc.wait_ge(sem["z3_T"], after("z3_T", m))
                    affine_cols(n2T, 6, "n2T_sb", g2, b2)

                def gelu(j):
                    sc.wait_ge(sem["up_mm"], after("up_mm", m, j + 1))
                    for i in range(2):
                        f = 2 * j + i
                        last = sc.activation(gT[:, f], bank[(4, 5, 7)[j]][:, T * i:T * i + T],
                                             ACT.Gelu, bias=bf1[:, f:f + 1])
                    last.then_inc(sem["gelu_sb"], 1)

                if back:
                    routed_cols()
                if front:
                    queries()
                    load_table(ACT.Exp)
                    keys()
                    values()
                if back:
                    exp_scores()
                if head:
                    squares()
                if front:
                    softmax(0)
                if back:
                    keys_values2()
                if front:
                    softmax(1)
                    softmax(2)
                    softmax(3)
                if back:
                    gathered()
                if front:
                    softmax(4)
                if back:
                    queries2()
                if front:
                    softmax(5)
                    softmax(6)
                if back:
                    softmax2()
                if front:
                    softmax(7)
                    transposed("A1")
                if back:
                    transposed2()
                if front:
                    transposed("B0")
                    transposed("B1")
                    transposed("A5")
                    transposed("B2")
                if back:
                    load_table(ACT.Gelu)
                if front:
                    attention()
                if back:
                    mlp_cols()
                    gelu(0)
                    gelu(1)
                    gelu(2)
                if head:
                    attention_cols_hi()
            steps(sc, step)


def kernel(**inputs):
    import numpy as _np
    import concourse.bacc as _bacc
    from concourse import mybir as _mybir
    from concourse.bass_utils import run_bass_kernel_spmd as _run

    nc = _bacc.Bacc("TRN2", target_bir_lowering=False, num_devices=1)
    arrays, args = {}, {}
    for name, a in inputs.items():
        a = _np.ascontiguousarray(a)
        if a.ndim == 0:
            a = a.reshape(1)
        arrays[f"in_{name}"] = a
        args[name] = nc.dram_tensor(f"in_{name}", a.shape, _mybir.dt.from_np(a.dtype),
                                    kind="ExternalInput").ap()
    y = nc.dram_tensor("out_0", (B, T, D), _mybir.dt.float32, kind="ExternalOutput").ap()
    build(nc, args, y)
    r = _run(nc, [arrays], core_ids=[0])
    return r.results[0]["out_0"]
```

```python
from contextlib import ExitStack

import concourse.bass as bass
from concourse import mybir

F32 = mybir.dt.float32
F32R = mybir.dt.float32r
BF16 = mybir.dt.bfloat16
ALU = mybir.AluOpType
ACT = mybir.ActivationFunctionType
AX = mybir.AxisListType

B, C, IMG = 128, 3, 224
PS = 16
GR = IMG // PS
T = GR * GR
HT = T // 2
PD = PS * PS * C
D = 192
NH, DH = 12, 16
F = 768
NSEL = max(1, int(round(0.15 * T)))
SELP = 32
EPS = 1e-5
QH = PS // 2
KX = 2 * C * PS
NEG = -1e30
KC = ((0, 128), (128, 192))
NG = 3
QSCALE = DH ** -0.5
TOPZ = 16.635532
RING = dict(S0=0, S1=1, S2=2, T0=3, S3=0, S4=1, S5=2, S6=0, S7=1, A0=2, A1=0, A2=3, B0=1, A3=2,
            B1=0, A4=1, A5=3, B2=0)
ORDER = list(RING)
PT = [name for name in ORDER if name[0] in "AB"]
PT_ACT = ("A1", "B0", "B1", "A4", "A5", "B2")
PAIRS = ((0, 0), (0, 1), (1, 0), (2, 2), (2, 3))

SEMS = dict(
    x_in=2 * C * 16, out_done=16,
    tok_mm=1, zT_mm=1, score_mm=1, kk_mm=1, vv_mm=1, aT_mm=1, q_mm=1, k_mm=1, v_mm=1,
    s_mm=8, p_T=len(PT), y_mm=2, proj_mm=1,
    gather_mm=1, qsel_mm=1, s2_mm=1, p2_T=1, ctx_mm=1, ctxT_mm=1, ao_mm=1, mix_mm=1,
    scat_mm=1, z3_T=1, up_mm=3, down_mm=1,
    tok_var=1, tok_y=1, y_stat=1, y_norm=1, h1_stat=1, a_sb=1, aTs_sb=1, klo_sb=1,
    qparts_sb=1, qz_sb=2, rowmax=8, rden_sb=4, pT_dve=len(PT) - len(PT_ACT), h2_sb=1,
    h2_stat=1, z0_sb=1, f0_sb=1, nTs_sb=1, z3Ts_sb=1, z_sb=1, sel_sb=1, mTs_sb=1, qb_sb=1,
    max2=1, ctx_sb=1, ctxT_sb=1, ao_sb=1,
    yparts_sb=2, gparts_sb=3, h3_sb=1, h3_stat=1, z3_sb=1, out_sb=1,
    sq_sb=1, aT_sb=1, qhi_sb=1, khi_sb=1, v_sb=1, probs=8, pT_act=len(PT_ACT), yhi_sb=2,
    nT_sb=1, expz=1, kk_sb=1, vv_sb=1, nsel_sb=1, qs_sb=1, probs2=1, p2T_sb=1, z3T_sb=1, gelu_sb=3,
    qz2_sb=2, f1b_sb=1, sqsum_sb=1, tok_rstd=1, y_rstd=1, h1_sb=1, h1b_sb=1, diag_sb=4,
    h1_rstd=1, h2_rstd=1, res_sb=1, h3_rstd=1,
)


def s_unit(u):
    s, second = divmod(u, 2)
    if second:
        return s, [(0, 1, 0), (1, 1, T)]
    return s, [(2, 1, 0), (0, 0, T), (1, 0, T + HT), (2, 0, T + 2 * HT)]


def build(nc, ins, out):
    W = dict(ins)
    with ExitStack() as ctx:
        ctx.enter_context(nc.allow_non_contiguous_dma(reason="small weights, once"))
        def sb(name, shape, dt=F32):
            return ctx.enter_context(nc.sbuf_tensor(name, shape, dt))

        sem = {name: ctx.enter_context(nc.semaphore(name)) for name in SEMS}
        one = {name: ctx.enter_context(nc.semaphore(name)) for name in
               ("w_in", "w_in_act", "w_in_gp", "consts_made", "zeroed", "w_scaled", "w_sums",
                "w_ready", "p1_zeroed")}
        bank = [ctx.enter_context(nc.psum_tensor(f"bank{i}", [128, 512], F32)) for i in range(8)]

        ident = sb("ident", [128, 128])
        identh = sb("identh", [HT, HT], BF16)
        tri = sb("tri", [HT, HT], BF16)
        before = sb("before", [HT, 2, T])
        notbefore = sb("notbefore", [HT, 2, T])
        slot_of = sb("slot_of", [128, 8])
        diag_of = sb("diag_of", [128, 4, DH])
        stack32 = sb("stack32", [128, SELP])
        lo_rows = sb("lo_rows", [128, 1])
        hi_half = sb("hi_half", [128, 1])
        iota32 = sb("iota32", [HT, SELP])
        ones = sb("ones", [128, 128])
        epsc = sb("epsc", [HT, 2])
        nhalf = sb("nhalf", [HT, 2])
        tokw = sb("tokw", [128, QH, D + 1])
        tok_g = sb("tok_g", [KX, QH])
        tok_bb = sb("tok_bb", [KX, QH])
        tok_bias = sb("tok_bias", [HT, D])
        ln2g = sb("ln2g", [HT, D])
        ln2b = sb("ln2b", [HT, D])
        widths = dict(wq=NG * 128, wk=NG * 128, wv=D, fwk=D, fwv=D, fwm=D, wr=128, w1=F)
        split = {name: sb(name + "_split", [128, 4, width], F32R)
                 for name, width in widths.items()}
        bk = sb("bk", [128, NG])
        bv = sb("bv", [128, NG])
        relk = sb("relk", [128, NG, T], F32R)
        add_parts = sb("add_parts", [128, 128], F32R)
        onesr = sb("onesr", [64, T], F32R)
        bqparts = sb("bqparts", [64, NG * 128], F32R)
        wps = sb("wps", [128, 2, NG, D], F32R)
        bp = sb("bp", [HT, D])
        g1 = sb("g1", [128, 2])
        b1 = sb("b1", [128, 2])
        g2 = sb("g2", [128, 2])
        b2 = sb("b2", [128, 2])
        wr = sb("wr", [128, 2])
        br = sb("br", [128, 1])
        fwq = sb("fwq", [128, 2, D])
        fwo = sb("fwo", [128, 2, D])
        fbq = sb("fbq", [128, 2])
        fbqs = sb("fbqs", [128, 2])
        fbk = sb("fbk", [128, 2])
        fbv = sb("fbv", [128, 2])
        fbo = sb("fbo", [SELP, D])
        fbm = sb("fbm", [HT, D])
        bf1 = sb("bf1", [128, F // 128])
        w2 = sb("w2", [128, 2, F // 128, D], F32R)
        bf2 = sb("bf2", [HT, D])
        x_sb = sb("x_sb", [128, GR, IMG])
        x_store = sb("x_store", [128, T * QH])
        x_sq = x_store[0:KX].rearrange("p (t q) -> p t q", q=QH)
        sqsum = sb("sqsum", [KX, T])
        mean1 = sb("mean1", [HT, 2])
        msq1 = sb("msq1", [HT, 2])
        var1 = sb("var1", [HT, 2])
        ve1 = sb("ve1", [HT, 2])
        rstd1 = sb("rstd1", [HT, 2])
        y_row = sb("y_row", [HT, 2, D])
        bn_y = sb("bn_y", [HT, 2, 6])
        mv_y = sb("mv_y", [HT, 2, 2])
        ve2 = sb("ve2", [HT, 2])
        rstd2 = sb("rstd2", [HT, 2])
        h1 = sb("h1", [HT, 2, D])
        h1b = sb("h1b", [HT, 2, D])
        bn_a = sb("bn_a", [HT, 2, 6])
        mv_a = sb("mv_a", [HT, 2, 2])
        ve3 = sb("ve3", [HT, 2])
        rstd3 = sb("rstd3", [HT, 2])
        a_row = sb("a_row", [HT, 2, D])
        aT = sb("aT", [128, 3, T], F32R)
        probs2 = sb("probs2_", [128, NG, T])
        qk_parts = sb("qk_parts", [128, 4, NG, T], F32R)
        khi, klo, qhi, qparts = (qk_parts[:, i] for i in range(4))
        table_out = sb("table_out", [1, 1])
        qz = sb("qz", [128, 4, NG, T], F32R)
        v_sb = sb("v_sb", [128, 2, NH, 32])
        negmax = sb("negmax", [HT, 4, 2, NG])
        den = sb("den", [HT, 4, 2, NG])
        rden = sb("rden", [HT, 4, 2, NG])
        diag = sb("diag", [128, 4, 2, NG, HT])
        p0 = sb("p0", [128, NH, HT])
        p1 = sb("p1", [128, NH, T])
        pT0 = sb("pT0", [128, NH, T])
        pT1 = sb("pT1", [128, NH, HT])
        yhi, yparts = qhi, qparts
        h2 = sb("h2", [HT, 2, D])
        h2b = sb("h2b", [HT, 2, D])
        bn_f = sb("bn_f", [HT, 2, 6])
        mv_f = sb("mv_f", [HT, 2, 2])
        vf = sb("vf", [HT, 6, 2])
        f0 = sb("f0", [HT, 2, D])
        z0 = sb("z0", [HT, 2, D])
        nT = sb("nT", [128, 2, T])
        nTs = sb("nTs", [128, 3, T], F32R)
        zrow = sb("zrow", [128, T])
        zclip = sb("zclip", [128, T])
        zi = sb("zi", [HT, 2])
        scr = sb("scr", [128, 4, T])
        cnt = sb("cnt", [HT, 2, 2])
        rank = sb("rank", [HT, 2])
        keep = sb("keep", [HT, 2])
        sel = sb("sel", [HT, 2, SELP])
        ez = sb("ez", [128, T])
        sig = sb("sig", [128, T])
        ssum = sb("ssum", [128, 1])
        sse = sb("sse", [128, 1])
        rss = sb("rss", [128, 1])
        pool_raw = sb("pool_raw", [128, 2])
        pooled = sb("pooled", [128, 2])
        mT = sb("mT", [128, 2, T])
        kk = sb("kk", [128, 2, T])
        vv = sb("vv", [HT, 2, D])
        nsel = sb("nsel", [128, 2, SELP])
        selT = sb("selT", [SELP, T])
        qs = sb("qs", [128, 2, SELP])
        qb0 = sb("qb0", [128, 8, SELP])
        qb1 = sb("qb1", [64, 4, SELP])
        negmax2 = sb("negmax2", [128, NG])
        den2 = sb("den2", [128, NG])
        rden2 = sb("rden2", [128, NG])
        p2T = sb("p2T", [HT, 2, NG * 128])
        ctxm = sb("ctxm", [128, NG, 64])
        ctxT = sb("ctxT", [128, 2, SELP])
        ao = sb("ao", [SELP, D])
        f1 = sb("f1", [HT, 2, D])
        h3 = sb("h3", [HT, 2, D])
        res = sb("res", [HT, 2, D])
        bn_3 = sb("bn_3", [HT, 2, 6])
        mv_3 = sb("mv_3", [HT, 2, 2])
        ve5 = sb("ve5", [HT, 2])
        rstd5 = sb("rstd5", [HT, 2])
        z3 = f0
        z3Ts = nTs
        gstore = sb("gstore", [128, 2 * F])
        gT = gstore[:, 0:F // 128 * T].rearrange("p (f t) -> p f t", t=T)
        gparts = qk_parts[:].rearrange("p a g t -> p (a g t)").rearrange(
            "p (a f t) -> p a f t", a=2, t=T)
        mTs = aT
        out_row = sb("out_row", [HT, 2, D])

        tokraw = x_store[0:KX, 0:QH * D].rearrange(
            "p (q d) -> p q d", d=D)
        tok_brep = scr[0:KX].rearrange("p a t -> p (a t)").rearrange("p (q i) -> p q i", i=HT)
        flat = p1[:].rearrange("p h t -> p (h t)")
        relb = flat[:, 2 * F:2 * F + NG * T].rearrange("p (g t) -> p g t", g=NG)
        bvrep = pT1[:].rearrange("p h t -> p (h t)")[:, 0:NG * HT].rearrange(
            "p (g i) -> p g i", g=NG)
        wp = probs2[:].rearrange("p g t -> p (g t)")[:, 0:NG * D].rearrange(
            "p (g d) -> p g d", g=NG)
        tok_brow, bprow = h3[:, 0], h3[:, 1]
        same_dim = ctxm[:].rearrange("p g e -> p (g e)")[:, 0:128]
        rel4 = out_row[:, :, 0:128]
        bqrow = p0[0:64].rearrange("p h t -> p (h t)")[:, 0:NG * 128]
        raw = dict(w1=gstore[:].rearrange("p (c w) -> p c w", c=2),
                   wr=qb0[:].rearrange("p h i -> p (h i)").rearrange("p (c w) -> p c w", c=2))
        for i, name in enumerate(("wq", "wk")):
            size = 2 * widths[name]
            raw[name] = flat[:, i * size:(i + 1) * size].rearrange("p (c w) -> p c w", c=2)
        flat = diag[:].rearrange("p s t g i -> p (s t g i)")
        size = F // 128 * D
        w2raw = flat[:, 0:size].rearrange("p (f d) -> p f d", d=D)
        raw["fwm"] = flat[:, size:size + 2 * D].rearrange("p (c w) -> p c w", c=2)
        for name, place in (("wv", nT), ("fwk", mT), ("fwv", kk)):
            raw[name] = place[:].rearrange("p c t -> p (c t)")[:, 0:2 * D].rearrange(
                "p (c w) -> p c w", c=2)

        def cols(t, chunk):
            lo, hi = KC[chunk]
            return t[0:hi - lo, chunk]

        def after(name, image, j=None):
            k = SEMS[name]
            return image * k + (k if j is None else j)

        def all_before(name, image):
            return image * SEMS[name]

        def steps(eng, step):
            step(-2, -1, 0, True, False, False, False)
            step(-1, 0, 1, True, True, False, False)
            step(0, 1, 2, True, True, True, False)
            with eng.Fori(1, B - 2) as m:
                step(m, m + 1, m + 2, True, True, True, True)
            step(B - 2, B - 1, B, False, True, True, True)
            step(B - 1, B, B + 1, False, False, True, True)

        def evacuation(name):
            act = name in PT_ACT
            return ("pT_act" if act else "pT_dve",
                    sum((o in PT_ACT) == act for o in PT[:PT.index(name) + 1]))

        def pt_dst(kind, k):
            if kind == "A":
                return pT0[0:HT, 2 * k:2 * k + 2].rearrange("p h t -> p (h t)")
            return pT1[0:HT, 4 * k:4 * k + 4].rearrange("p h t -> p (h t)")

        block = ctx.enter_context(nc.Block())

        loads = []

        def load(dst, src):
            loads.append((dst, src))

        xh = W["x"].rearrange("b c (h p) w -> b c p h w", p=PS)

        def load_x(eng, image):
            for s in range(2):
                for c in range(C):
                    part = (s * C + c) * PS
                    eng.dma_start(x_sb[part:part + PS, :, 0:IMG - QH * s],
                                  xh[image, c, :, :, QH * s:IMG]).then_inc(sem["x_in"], 16)

        tw = W["L0_tok_W"].rearrange("(p s q c) m -> s c p q m", p=PS, s=2, q=QH)
        tg = W["L0_tok_ln1_g"].rearrange("(p s q c) -> s c p q", p=PS, s=2, q=QH)
        tb = W["L0_tok_ln1_b"].rearrange("(p s q c) -> s c p q", p=PS, s=2, q=QH)
        for s in range(2):
            for c in range(C):
                part = (s * C + c) * PS
                load(tokraw[part:part + PS], tw[s, c])
                load(tok_g[part:part + PS], tg[s, c])
                load(tok_bb[part:part + PS], tb[s, c])
        for dst, name, n in ((tok_brow, "L0_tok_b", HT), (ln2g, "L0_tok_ln2_g", HT),
                             (ln2b, "L0_tok_ln2_b", HT), (bprow, "L0_attn_b_proj", HT),
                             (fbo, "L0_ffn_bo", SELP), (fbm, "L0_ffn_bm", HT),
                             (bf2, "L0_ffn_bf2", HT)):
            load(dst[:], W[name].partition_broadcast(n))
        wa = W["L0_attn_w_attn"]
        for chunk, (lo, hi) in enumerate(KC):
            size = hi - lo
            for p in (0,) if chunk == 0 else (0, 64):
                for j, name in enumerate(("wq", "wk")):
                    for r in (0, DH):
                        load(raw[name][p:p + size, chunk].rearrange(
                                 "p (h e) -> p h e", e=32)[:, :, r:r + DH],
                             wa[lo:hi, j * D:(j + 1) * D].rearrange("p (h e) -> p h e", e=DH))
                load(raw["wv"][p:p + size, chunk], wa[lo:hi, 2 * D:3 * D])
                for dst, name in (("fwk", "Wk"), ("fwv", "Wv"), ("fwm", "Wm"),
                                  ("w1", "W1")):
                    load(raw[dst][p:p + size, chunk], W["L0_ffn_" + name][lo:hi])
                load(wr[p:p + size, chunk:chunk + 1], W["L0_ffn_Wr"][lo:hi].unsqueeze(1))
                load(g2[p:p + size, chunk:chunk + 1], W["L0_ffn_g2"][lo:hi].unsqueeze(1))
            for dst, name in ((fwq, "Wq"), (fwo, "Wo")):
                load(dst[0:size, chunk], W["L0_ffn_" + name][lo:hi])
            for dst, name in ((g1, "g1"), (b1, "b1"), (b2, "b2"), (fbq, "bq"),
                              (fbk, "bk"), (fbv, "bv")):
                load(dst[0:size, chunk:chunk + 1], W["L0_ffn_" + name][lo:hi].unsqueeze(1))
        ba = W["L0_attn_b_attn"].rearrange("(j g s e) -> j s e g", j=3, g=NG, s=4)
        wpr = W["L0_attn_w_proj"].rearrange("(g s e) m -> s e g m", g=NG, s=4)
        rel = W["L0_attn_rel_emb"]
        for s in range(4):
            for r in (0, DH):
                at = 32 * s + r
                load(bk[at:at + DH], ba[1, s])
                load(wp[at:at + DH], wpr[s])
            load(bv[32 * s:32 * s + DH], ba[2, s])
        for row in (0, 32):
            for r in (0, DH):
                load(bqrow[row:row + 1].rearrange("p (h e) -> p h e", e=32)[:, :, r:r + DH],
                     W["L0_attn_b_attn"][0:D].rearrange("(o h e) -> o h e", o=1, e=DH))
        for t, (first, r0) in enumerate(((1, 0), (0, HT - 1))):
            rows_in = HT - first
            load(rel4[first:HT, t].rearrange("p (x e) -> p x e", e=DH),
                 rel[r0:r0 + rows_in].unsqueeze(1).broadcast_to([rows_in, 8, DH]))
        load(br[:], W["L0_ffn_br"].unsqueeze(0).partition_broadcast(128))
        load(bf1[:], W["L0_ffn_bf1"].rearrange("(k p) -> p k", p=128))
        load(w2raw, W["L0_ffn_W2"].rearrange("(k p) m -> p k m", p=128))
        by_sp, by_act, by_gp = loads[0::3], loads[1::3], loads[2::3]

        @block.sync
        def _(sp):
            load_x(sp, 0)
            sp.wait_ge(one["zeroed"], 1)
            for dst, src in by_sp:
                sp.dma_start(dst, src).then_inc(one["w_in"], 16)

            def prefetch(j, image):
                sp.wait_ge(sem["tok_mm"], after("tok_mm", j))
                sp.wait_ge(sem["sq_sb"], after("sq_sb", j))
                load_x(sp, image)

            def store(j):
                sp.wait_ge(sem["out_sb"], after("out_sb", j))
                sp.dma_start(out[j].rearrange("(t p) d -> p t d", p=HT),
                             out_row[:]).then_inc(sem["out_done"], 16)

            prefetch(0, 1)
            prefetch(1, 2)
            with sp.Fori(0, B - 3) as j:
                prefetch(j + 2, j + 3)
                store(j)
            for j in range(B - 3, B):
                store(j)
            sp.wait_ge(sem["out_done"], 16 * B)

        @block.gpsimd
        def _(gp):
            for t in (bv, out_row, p0):
                gp.memset(t[:], 0.0)
            gp.drain().then_inc(one["zeroed"], 1)
            for dst, src in by_gp:
                gp.dma_start(dst, src).then_inc(one["w_in_gp"], 16)
            gp.memset(ident[:], 0.0)
            gp.memset(identh[:], 0.0)
            gp.memset(tri[:], 0.0)
            gp.memset(before[:], 1.0)
            gp.memset(notbefore[:], 1.0)
            gp.memset(slot_of[:], 1.0)
            gp.memset(diag_of[:], 1.0)
            gp.memset(stack32[:], 0.0)
            gp.memset(same_dim, 0.0)
            gp.memset(qz[:].bitcast(F32), 0.0)
            gp.memset(ones[:], 1.0)
            gp.memset(epsc[:], EPS)
            gp.memset(nhalf[:], -0.5)
            gp.memset(v_sb[:], 0.0)
            for t in (pT0, pT1, tokw):
                gp.memset(t[:], 0.0)
            gp.drain()
            gp.memset(tokw[0:KX], 1.0)
            gp.drain()
            gp.memset(x_sb[KX:128], 0.0)
            gp.drain()
            gp.iota(iota32[:], [[1, SELP]], base=0, channel_multiplier=0,
                    allow_small_or_imprecise_dtypes=True)
            gp.drain()

            def select(t, op, fill, base, mult, pattern):
                gp.affine_select(out=t, in_=t, compare_op=op, fill=fill, base=base,
                                 pattern=pattern, channel_multiplier=mult)

            select(ident[:], ALU.not_equal, 1.0, 0, 1, [[-1, 128]])
            select(identh[:], ALU.not_equal, 1.0, 0, 1, [[-1, HT]])
            select(tri[:], ALU.is_ge, NEG, 0, 1, [[-1, HT]])
            for t in range(2):
                select(before[:, t], ALU.is_ge, 0.0, HT * t - 1, 1, [[-1, T]])
                select(notbefore[:, t], ALU.is_ge, 0.0, -HT * t, -1, [[1, T]])
            select(slot_of[:], ALU.is_ge, 0.0, 0, 1, [[-DH, 8]])
            select(diag_of[:], ALU.is_ge, 0.0, 0, 1, [[-32, 4], [0, DH]])
            for r in range(4):
                gp.drain()
                select(stack32[:], ALU.not_equal, 1.0, -32 * r, 1, [[-1, SELP]])
                if r < 2:
                    select(same_dim.rearrange("p (s r e) -> p s r e", r=2, e=DH), ALU.not_equal,
                           1.0, -DH * r, 1, [[-32, 4], [0, 2], [-1, DH]])
            select(slot_of[:], ALU.is_ge, 0.0, DH - 1, -1, [[DH, 8]])
            select(diag_of[:], ALU.is_ge, 0.0, 31, -1, [[32, 4], [0, DH]])
            gp.drain().then_inc(one["consts_made"], 1)
            gp.wait_ge(one["w_ready"], 1)
            for t in (p1, diag):
                gp.memset(t[:], 0.0)
            gp.drain().then_inc(one["p1_zeroed"], 1)

            def rstd(var, ve, r, name):
                gp.tensor_tensor(ve, var, epsc[:], ALU.add)
                gp.drain()
                gp.tensor_tensor(r, ve, nhalf[:], ALU.pow).then_inc(sem[name], 1)

            def both(t):
                return t[:].unsqueeze(1).broadcast_to([HT, 2, D])

            def step(m, n, l, head, front, back, again):
                def h1_with_bias():
                    if back:
                        gp.wait_ge(sem["h2_sb"], all_before("h2_sb", n))
                    gp.tensor_tensor(h1b[:], h1[:], both(bp), ALU.add).then_inc(sem["h1b_sb"], 1)

                def diagonals(s):
                    gp.wait_ge(sem["rden_sb"], after("rden_sb", n, s + 1))
                    gp.tensor_tensor(
                        diag[0:HT, s].rearrange("p t g i -> p (t g) i"),
                        ident[0:HT, 0:HT].unsqueeze(1).broadcast_to([HT, 2 * NG, HT]),
                        rden[:, s].rearrange("p t g -> p (t g)").unsqueeze(2).broadcast_to(
                            [HT, 2 * NG, HT]), ALU.mult).then_inc(sem["diag_sb"], 1)

                if front:
                    h1_with_bias()
                if back:
                    gp.tensor_tensor(h2b[:], h2[:], both(bf2), ALU.add)
                if front:
                    for i in (2, 3):
                        at = slice(32 * i, 32 * i + 32)
                        gp.drain()
                        if i == 2:
                            gp.wait_ge(sem["qparts_sb"], after("qparts_sb", n))
                        gp.tensor_tensor(qz[at, i], qparts[at].bitcast(F32),
                                         ones[at, 0:1].unsqueeze(2).broadcast_to([32, NG, T]),
                                         ALU.mult).then_inc(sem["qz2_sb"], 1)
                    gp.drain()
                if head:
                    gp.wait_ge(sem["sq_sb"], after("sq_sb", l))
                    gp.tensor_tensor(x_sq[:, :, 0:4], x_sq[:, :, 0:4], x_sq[:, :, 4:8], ALU.add)
                    gp.drain()
                    gp.tensor_tensor(x_sq[:, :, 0:2], x_sq[:, :, 0:2], x_sq[:, :, 2:4], ALU.add)
                    gp.drain()
                    gp.tensor_tensor(sqsum[:].unsqueeze(2), x_sq[:, :, 0:1], x_sq[:, :, 1:2],
                                     ALU.add).then_inc(sem["sqsum_sb"], 1)
                if front:
                    diagonals(0)
                if back:
                    gp.wait_ge(sem["sel_sb"], after("sel_sb", m))
                    gp.tensor_tensor(f1[:], both(fbm), keep[:].unsqueeze(2).broadcast_to(
                        [HT, 2, D]), ALU.mult)
                    gp.drain()
                    gp.tensor_tensor(f1[:], f1[:], f0[:], ALU.add).then_inc(sem["f1b_sb"], 1)
                if front:
                    diagonals(1)
                if head:
                    gp.wait_ge(sem["tok_var"], after("tok_var", l))
                    rstd(var1[:], ve1[:], rstd1[:], "tok_rstd")
                if head:
                    gp.wait_ge(sem["y_stat"], after("y_stat", l))
                    rstd(mv_y[:, :, 1], ve2[:], rstd2[:], "y_rstd")
                if front:
                    diagonals(2)
                    diagonals(3)
                if head:
                    gp.wait_ge(sem["y_norm"], after("y_norm", l))
                    gp.tensor_tensor(y_row[:], y_row[:], both(ln2g), ALU.mult)
                    gp.drain()
                    gp.tensor_tensor(h1[:], y_row[:], both(ln2b), ALU.add).then_inc(sem["h1_sb"], 1)
                if head:
                    gp.wait_ge(sem["h1_stat"], after("h1_stat", l))
                    rstd(mv_a[:, :, 1], ve3[:], rstd3[:], "h1_rstd")
                if back:
                    gp.wait_ge(sem["h3_stat"], after("h3_stat", m))
                    rstd(mv_3[:, :, 1], ve5[:], rstd5[:], "h3_rstd")
                if back:
                    gp.tensor_tensor(res[:], h2b[:], h3[:], ALU.add).then_inc(sem["res_sb"], 1)
                if front:
                    gp.wait_ge(sem["h2_stat"], after("h2_stat", n))
                    v = mv_f[:, :, 1]
                    ve, r, rr, vr, vn, r2 = (vf[:, i, :] for i in range(6))
                    gp.tensor_tensor(ve, v, epsc[:], ALU.add)
                    gp.drain()
                    gp.tensor_tensor(r, ve, nhalf[:], ALU.pow)
                    gp.drain()
                    gp.tensor_tensor(rr, r, r, ALU.mult)
                    gp.drain()
                    gp.tensor_tensor(vr, rr, v, ALU.mult)
                    gp.drain()
                    gp.tensor_tensor(vn, vr, epsc[:], ALU.add)
                    gp.drain()
                    gp.tensor_tensor(vr, vn, nhalf[:], ALU.pow)
                    gp.drain()
                    gp.tensor_tensor(r2, r, vr, ALU.mult).then_inc(sem["h2_rstd"], 1)

            steps(gp, step)

        @block.tensor
        def _(pe):
            mm = pe.matmul
            pe.wait_ge(one["w_in"], 16 * len(by_sp))
            pe.wait_ge(one["w_in_act"], 16 * len(by_act))
            pe.wait_ge(one["w_in_gp"], 16 * len(by_gp))
            pe.wait_ge(one["consts_made"], 1)
            pe.wait_ge(one["w_scaled"], 1)
            for q in range(QH):
                mm(bank[0][0:KX, 0:D], ones[0:KX, 0:KX], tokw[0:KX, q, 0:D], start=q == 0,
                   stop=q == QH - 1)
            for q in range(QH):
                mm(bank[1][0:HT, 0:D], tok_brep[:, q], tokraw[:, q], start=q == 0, stop=q == QH - 1)
            for g in range(NG):
                mm(bank[2][0:HT, 0:D], bvrep[:, g], wp[:, g], start=g == 0, stop=g == NG - 1)
            for t in range(2):
                last = pe.transpose(bank[3][0:128, HT * t:HT * t + HT], rel4[:, t],
                                    ident[0:HT, 0:HT])
            for f in range(F // 128):
                for chunk, (lo, hi) in enumerate(KC):
                    last = mm(bank[4][:, f:f + 1], raw["w1"][0:hi - lo, chunk, 128 * f:128 * f + 128],
                              b2[0:hi - lo, chunk:chunk + 1], start=chunk == 0, stop=chunk == 1)
            last.then_inc(one["w_sums"], 1)
            pe.wait_ge(one["w_ready"], 1)

            def rows_to_cols(b, src, name):
                for chunk, (lo, hi) in enumerate(KC):
                    for t in range(2):
                        c0 = chunk * T + t * HT
                        last = pe.transpose(bank[b][0:hi - lo, c0:c0 + HT], src[:, t, lo:hi],
                                            ident[0:HT, 0:HT])
                last.then_inc(sem[name], 1)

            def cols_to_rows(b, src, w, name):
                for t in range(2):
                    for i, (p, wpart) in enumerate(PAIRS):
                        last = mm(bank[b][0:HT, t * D:(t + 1) * D],
                                  src[:, p, HT * t:HT * t + HT], w[:, wpart],
                                  start=i == 0, stop=i == len(PAIRS) - 1)
                last.then_inc(sem[name], 1)

            def cols_to_cols(o, src, w, lo, hi):
                for i, (p, wpart) in enumerate(PAIRS):
                    last = mm(o, w[:, wpart, lo:hi], src[:, p], start=i == 0,
                              stop=i == len(PAIRS) - 1)
                return last

            def group_cols(b0, w, name):
                for g in range(NG):
                    o = bank[b0 + g // 2][:, (g % 2) * T:(g % 2) * T + T]
                    for i, (p, wpart) in enumerate(PAIRS):
                        mm(o, w[:, wpart, 128 * g:128 * g + 128], aT[:, p], start=i == 0,
                           stop=False)
                    if name == "q_mm":
                        last = mm(o, bqparts[:, 128 * g:128 * g + 128], onesr[:], start=False,
                                  stop=True)
                    else:
                        last = mm(o, add_parts[:], relk[:, g], start=False, stop=True)
                last.then_inc(sem[name], 1)

            def step(m, n, l, head, front, back, again):
                def routed_cols():
                    pe.wait_ge(sem["z0_sb"], after("z0_sb", m))
                    rows_to_cols(5, z0, "zT_mm")

                def queries_keys_values():
                    pe.wait_ge(sem["aTs_sb"], after("aTs_sb", n))
                    if back:
                        pe.wait_ge(sem["h2_sb"], all_before("h2_sb", n))
                    group_cols(0, split["wq"], "q_mm")
                    group_cols(2, split["wk"], "k_mm")
                    cols_to_rows(4, aT, split["wv"], "v_mm")

                def scores(u, b):
                    s, heads = s_unit(u)
                    if u % 2:
                        masked = bank[b][0:HT, 0:2 * T].rearrange("p (h w) -> p h w", w=T)[:, :, HT:T]
                    else:
                        masked = bank[b][0:HT, HT:5 * HT].rearrange("p (h w) -> p h w", w=HT)
                    blocks = 2 if u % 2 else 4
                    mm(masked, identh[:], tri[:].unsqueeze(1).broadcast_to([HT, blocks, HT]),
                       start=True, stop=False, skip_group_check=True)
                    for i, (g, t, c0) in enumerate(heads):
                        w = T if t else HT
                        for part in (khi, klo):
                            last = mm(bank[b][0:HT, c0:c0 + w],
                                      qz[:, s, g, HT * t:HT * t + HT], part[:, g, 0:w],
                                      start=False, stop=i == len(heads) - 1 and part is klo,
                                      skip_group_check=True)
                    last.then_inc(sem["s_mm"], 1)

                def patches(b, t, q0, q1):
                    xf = x_sb[:].rearrange("p h w -> p (h w)")
                    for q in range(q0, q1):
                        a = t * HT * PS + q
                        mm(bank[b][0:HT, t * (D + 1):(t + 1) * (D + 1)],
                           xf[:, a:a + (HT - 1) * PS + 1:PS], tokw[:, q],
                           start=t == 0 and q == 0, stop=q == QH - 1, skip_group_check=True)

                def square_sums(b):
                    pe.wait_ge(sem["sqsum_sb"], after("sqsum_sb", l))
                    for t in range(2):
                        last = mm(bank[b][0:HT, 2 * D + 2 + t:2 * D + 3 + t],
                                  sqsum[:, HT * t:HT * t + HT], ones[0:KX, 0:1], start=False,
                                  stop=True, skip_group_check=True)
                    last.then_inc(sem["tok_mm"], 1)

                def transposes(kind, k, b):
                    if kind == "A":
                        blocks = [(2 * k + i, t, 0) for i in range(2) for t in range(2)]
                    else:
                        blocks = [(4 * k + i, 1, 1) for i in range(4)]
                    for i, (h, t, u) in enumerate(blocks):
                        src = p1[:, h, HT * u:HT * u + HT] if t else p0[:, h]
                        last = mm(bank[b][0:HT, HT * i:HT * i + HT], src, diag[:, h // 3, t, h % 3],
                                  start=True, stop=True)
                    last.then_inc(sem["p_T"], 1)

                def bank_free(name):
                    i = ORDER.index(name)
                    before_it = [o for o in ORDER[:i] if RING[o] == RING[name]]
                    if not before_it:
                        return
                    o = before_it[-1]
                    if o[0] == "S" and front:
                        pe.wait_ge(sem["probs"], after("probs", n, int(o[1:]) + 1))
                    elif o[0] == "T" and head:
                        pe.wait_ge(sem["tok_y"], after("tok_y", l))
                    elif o[0] in "AB":
                        engine, count = evacuation(o)
                        pe.wait_ge(sem[engine], after(engine, n, count))

                def causal(name):
                    kind, k = name[0], int(name[1:])
                    bank_free(name)
                    if kind == "S":
                        if k == 0:
                            pe.wait_ge(sem["klo_sb"], after("klo_sb", n))
                        if k % 2 == 0:
                            by = "qz_sb" if k < 4 else "qz2_sb"
                            pe.wait_ge(sem[by], after(by, n, k // 2 % 2 + 1))
                        scores(k, RING[name])
                    else:
                        s = (2 * k + 1 if kind == "A" else 4 * k + 3) // 3
                        pe.wait_ge(sem["diag_sb"], after("diag_sb", n, s + 1))
                        transposes(kind, k, RING[name])

                def embed(t, q0, q1):
                    if t == 0 and q0 == 0:
                        bank_free("T0")
                        pe.wait_ge(sem["x_in"], after("x_in", l))
                    patches(RING["T0"], t, q0, q1)
                    if t == 1 and q1 == QH:
                        square_sums(RING["T0"])

                def score():
                    pe.wait_ge(sem["nTs_sb"], after("nTs_sb", m))
                    if again:
                        pe.wait_ge(sem["out_sb"], all_before("out_sb", m))
                    cols_to_cols(bank[6][:, 0:T], nTs, split["wr"], 0, 128).then_inc(
                        sem["score_mm"], 1)

                def keys_values2():
                    for mt, (mlo, mhi) in enumerate(KC):
                        last = cols_to_cols(bank[7][0:mhi - mlo, mt * T:mt * T + T], nTs,
                                            split["fwk"], mlo, mhi)
                    last.then_inc(sem["kk_mm"], 1)
                    cols_to_rows(5, nTs, split["fwv"], "vv_mm")

                def gather():
                    pe.wait_ge(sem["sel_sb"], after("sel_sb", m))
                    for chunk, (lo, hi) in enumerate(KC):
                        for t in range(2):
                            mm(bank[6][0:hi - lo, chunk * SELP:(chunk + 1) * SELP],
                               z0[:, t, lo:hi], sel[:, t], start=t == 0, stop=t == 1)
                    for t in range(2):
                        last = pe.transpose(bank[6][0:SELP, 64 + HT * t:64 + HT * t + HT],
                                            sel[:, t], ident[0:HT, 0:HT])
                    last.then_inc(sem["gather_mm"], 1)

                def qsel():
                    pe.wait_ge(sem["nsel_sb"], after("nsel_sb", m))
                    for mt, (mlo, mhi) in enumerate(KC):
                        for chunk, (lo, hi) in enumerate(KC):
                            last = mm(bank[7][0:mhi - mlo, mt * SELP:(mt + 1) * SELP],
                                      fwq[0:hi - lo, chunk, mlo:mhi], cols(nsel, chunk),
                                      start=chunk == 0, stop=chunk == 1)
                    last.then_inc(sem["qsel_mm"], 1)

                def scores2():
                    pe.wait_ge(sem["qb_sb"], after("qb_sb", m))
                    if front:
                        pe.wait_ge(sem["v_sb"], after("v_sb", n))
                    mm(bank[5][:, 0:T], qb0[:, 0:4], kk[:, 0], start=True, stop=True)
                    mm(bank[5][:, T:2 * T], qb0[:, 4:8], kk[:, 0], start=True, stop=True)
                    mm(bank[4][:, 0:T], qb1[:], kk[0:64, 1], start=True,
                       stop=True).then_inc(sem["s2_mm"], 1)

                def transposes2():
                    pe.wait_ge(sem["probs2"], after("probs2", m))
                    for t in range(2):
                        for g in range(NG):
                            last = pe.transpose(bank[6 + t][0:HT, 128 * g:128 * g + 128],
                                                probs2[:, g, HT * t:HT * t + HT], ident[:])
                    last.then_inc(sem["p2_T"], 1)

                def context2():
                    pe.wait_ge(sem["p2T_sb"], after("p2T_sb", m))
                    for g in range(NG):
                        for t in range(2):
                            last = mm(bank[5][:, 64 * g:64 * g + 64],
                                      p2T[:, t, 128 * g:128 * g + 128],
                                      vv[:, t, 64 * g:64 * g + 64], start=t == 0, stop=t == 1)
                    last.then_inc(sem["ctx_mm"], 1)

                def mix():
                    pe.wait_ge(sem["mTs_sb"], after("mTs_sb", m))
                    cols_to_rows(7, mTs, split["fwm"], "mix_mm")

                def context2_cols():
                    pe.wait_ge(sem["ctx_sb"], after("ctx_sb", m))
                    mm(bank[4][:, 0:SELP], ctxm[:, 0:2], stack32[:], start=True, stop=True)
                    last = mm(bank[4][0:64, SELP:2 * SELP], ctxm[:, 2], stack32[:], start=True,
                              stop=True)
                    last.then_inc(sem["ctxT_mm"], 1)

                def attn_out():
                    pe.wait_ge(sem["ctxT_sb"], after("ctxT_sb", m))
                    for chunk in range(2):
                        last = mm(bank[6][0:SELP, 0:D], cols(ctxT, chunk), cols(fwo, chunk),
                                  start=chunk == 0, stop=chunk == 1)
                    last.then_inc(sem["ao_mm"], 1)

                def scatter():
                    pe.wait_ge(sem["ao_sb"], after("ao_sb", m))
                    for t in range(2):
                        last = mm(bank[5][0:HT, t * D:(t + 1) * D],
                                  selT[0:NSEL, HT * t:HT * t + HT], ao[0:NSEL], start=True,
                                  stop=True)
                    last.then_inc(sem["scat_mm"], 1)

                def attention():
                    out_of = [bank[2 + g // 2][:, (g % 2) * T:(g % 2) * T + T] for g in range(NG)]
                    pe.wait_ge(sem["pT_dve"], after("pT_dve", n))
                    pe.wait_ge(sem["pT_act"], after("pT_act", n, SEMS["pT_act"] - 1))
                    for groups in ((0, 1), (2,)):
                        for g in groups:
                            for s in range(4):
                                mm(out_of[g][32 * s:32 * s + 32], v_sb[:, 0, 4 * g + s],
                                   pT0[:, 3 * s + g], start=g != 1, stop=False,
                                   skip_group_check=True)
                        for g in groups:
                            if g == 0:
                                pe.wait_ge(sem["pT_act"], after("pT_act", n))
                            for s in range(4):
                                last = mm(out_of[g][32 * s:32 * s + 32, HT:T],
                                          v_sb[:, 1, 4 * g + s], pT1[:, 3 * s + g],
                                          start=False, stop=True, skip_group_check=True)
                        last.then_inc(sem["y_mm"], 1)

                def projection():
                    for t in range(2):
                        for g in range(NG):
                            if t == 0 and g != 1:
                                pe.wait_ge(sem["yparts_sb"], after("yparts_sb", n, g // 2 + 1))
                            for part in range(2):
                                last = mm(bank[0][0:HT, t * D:(t + 1) * D],
                                          yparts[:, g, HT * t:HT * t + HT], wps[:, part, g],
                                          start=g == 0 and part == 0,
                                          stop=g == NG - 1 and part == 1)
                    last.then_inc(sem["proj_mm"], 1)

                def mlp_cols():
                    pe.wait_ge(sem["z3_sb"], after("z3_sb", m))
                    rows_to_cols(6, z3, "z3_T")

                def up(j):
                    if j == 0:
                        pe.wait_ge(sem["z3Ts_sb"], after("z3Ts_sb", m))
                    for f in (2 * j, 2 * j + 1):
                        last = cols_to_cols(bank[(4, 5, 7)[j]][:, T * (f % 2):T * (f % 2) + T],
                                            z3Ts, split["w1"], 128 * f, 128 * f + 128)
                    last.then_inc(sem["up_mm"], 1)

                def down(j):
                    pe.wait_ge(sem["gparts_sb"], after("gparts_sb", m, j + 1))
                    for f in (2 * j, 2 * j + 1):
                        for t in range(2):
                            for i, (part, wpart) in enumerate(((0, 0), (0, 1), (1, 0))):
                                last = mm(bank[6][0:HT, t * D:(t + 1) * D],
                                          gparts[:, part, f, HT * t:HT * t + HT], w2[:, wpart, f],
                                          start=f == 0 and t == 0 and i == 0,
                                          stop=f == F // 128 - 1 and i == 2, skip_group_check=True)
                    if j == 2:
                        last.then_inc(sem["down_mm"], 1)

                def attention_cols():
                    pe.wait_ge(sem["a_sb"], after("a_sb", l))
                    rows_to_cols(1, a_row, "aT_mm")

                if back:
                    routed_cols()
                if front:
                    queries_keys_values()
                if back:
                    score()
                    keys_values2()
                if front:
                    causal("S0")
                    causal("S1")
                    causal("S2")
                if back:
                    gather()
                if head:
                    embed(0, 0, QH)
                if front:
                    causal("S3")
                if back:
                    qsel()
                if front:
                    causal("S4")
                    causal("S5")
                if head:
                    embed(1, 0, 4)
                if front:
                    causal("S6")
                if back:
                    scores2()
                if head:
                    embed(1, 4, QH)
                if front:
                    causal("S7")
                    causal("A0")
                    causal("A1")
                if back:
                    transposes2()
                if front:
                    causal("A2")
                    causal("B0")
                if back:
                    context2()
                    mix()
                    context2_cols()
                if front:
                    causal("A3")
                if back:
                    attn_out()
                if front:
                    causal("B1")
                if back:
                    scatter()
                if front:
                    causal("A4")
                    causal("A5")
                    causal("B2")
                    attention()
                if back:
                    mlp_cols()
                if head:
                    attention_cols()
                if front:
                    projection()
                if back:
                    up(0)
                    up(1)
                    up(2)
                    down(0)
                    down(1)
                    down(2)
            steps(pe, step)

        @block.vector
        def _(ve):
            ve.wait_ge(one["w_in"], 16 * len(by_sp))
            ve.wait_ge(one["w_in_act"], 16 * len(by_act))
            ve.wait_ge(one["w_in_gp"], 16 * len(by_gp))
            ve.wait_ge(one["consts_made"], 1)
            for q in range(QH):
                ve.tensor_scalar(tokw[0:KX, q, 0:D], tokraw[:, q], tok_g[:, q:q + 1], None, ALU.mult)
            ve.tensor_copy(tok_brep[:], tok_bb[:].unsqueeze(2).broadcast_to([KX, QH, HT]))
            ve.tensor_copy(bvrep[:], bv[:].unsqueeze(2).broadcast_to([128, NG, HT]))
            for chunk, (lo, hi) in enumerate(KC):
                size = hi - lo
                ve.tensor_scalar(fbqs[0:size, chunk:chunk + 1], fbq[0:size, chunk:chunk + 1], QSCALE,
                                 None, ALU.mult)
            ve.tensor_copy(raw["wr"][:], wr[:].unsqueeze(2).broadcast_to([128, 2, 128]))
            ve.tensor_scalar(raw["wq"], raw["wq"], QSCALE, None, ALU.mult)
            ve.tensor_scalar(bqrow, bqrow, QSCALE, None, ALU.mult)
            ve.tensor_copy(add_parts[:], same_dim)
            ve.tensor_copy(onesr[:], ones[0:64, 0:1].broadcast_to([64, T]))
            for g in range(NG):
                ve.tensor_copy(relb[:, g], bk[:, g:g + 1].broadcast_to([128, T]))
            ve.tensor_reduce(hi_half[:], stack32[:, 0:DH], AX.X, ALU.add)
            ve.drain().then_inc(one["w_scaled"], 1)
            ve.tensor_scalar(lo_rows[:], hi_half[:], 1.0, None, ALU.subtract)
            others = [name for name in raw if name != "w1"]
            for name in others:
                ve.tensor_copy(split[name][:, 0::2], raw[name][:])
            ve.tensor_copy(wps[:, 0], wp)
            ve.tensor_copy(w2[:, 0], w2raw)
            ve.tensor_copy(bqparts[:], bqrow)
            ve.drain()
            ve.tensor_tensor(wps[:, 1], wp, wps[:, 0].bitcast(F32), ALU.subtract)
            ve.tensor_tensor(w2[:, 1], w2raw, w2[:, 0].bitcast(F32), ALU.subtract)
            ve.tensor_tensor(bqparts[32:64], bqrow[32:64], bqparts[32:64].bitcast(F32),
                             ALU.subtract)
            for name in others:
                ve.tensor_tensor(split[name][:, 1::2], raw[name][:],
                                 split[name][:, 0::2].bitcast(F32), ALU.subtract)
            ve.wait_ge(one["w_sums"], 1)
            for chunk in range(2):
                ve.tensor_scalar(raw["w1"][:, chunk], raw["w1"][:, chunk], g2[:, chunk:chunk + 1],
                                 None, ALU.mult)
            ve.tensor_tensor(bf1[:], bf1[:], bank[4][:, 0:F // 128], ALU.add)
            ve.drain()
            ve.tensor_copy(split["w1"][:, 0::2], raw["w1"][:])
            ve.drain()
            ve.tensor_tensor(split["w1"][:, 1::2], raw["w1"][:],
                             split["w1"][:, 0::2].bitcast(F32), ALU.subtract)
            for q in range(QH):
                ve.scalar_tensor_tensor(tokw[0:KX, q, 0:D], bank[0][0:KX, 0:D], -1.0 / PD,
                                        tokw[0:KX, q, 0:D], ALU.mult, ALU.add)
            ve.tensor_tensor(tok_bias[:], bank[1][0:HT, 0:D], tok_brow[:], ALU.add)
            ve.tensor_tensor(bp[:], bank[2][0:HT, 0:D], bprow[:], ALU.add)
            for g in range(NG):
                ve.tensor_tensor(relb[:, g], bank[3][:, 0:T], relb[:, g], ALU.add)
            ve.drain()
            ve.tensor_copy(khi, relb)
            ve.drain()
            ve.scalar_tensor_tensor(relk[:], khi.bitcast(F32), lo_rows[:], relb, ALU.mult,
                                    ALU.add)
            ve.drain().then_inc(one["w_ready"], 1)

            def stats(src, bn, mv, name):
                for t in range(2):
                    ve.bn_stats(bn[:, t], src[:, t])
                ve.drain()
                for t in range(2):
                    last = ve.bn_aggr(mv[:, t], bn[:, t])
                last.then_inc(sem[name], 1)

            def normalise(dst, src, mv, r, name):
                for t in range(2):
                    last = ve.tensor_scalar(dst[:, t], src[:, t], mv[:, t, 0:1], r[:, t:t + 1],
                                            ALU.subtract, ALU.mult)
                last.then_inc(sem[name], 1)

            def split_cols(dst, src, name):
                ve.tensor_copy(dst[:, 0], src[:, 0])
                ve.tensor_copy(dst[0:64, 2], src[0:64, 1])
                ve.drain()
                ve.tensor_tensor(dst[:, 1], src[:, 0], dst[:, 0].bitcast(F32), ALU.subtract)
                ve.tensor_tensor(dst[64:128, 2], src[0:64, 1], dst[0:64, 2].bitcast(F32),
                                 ALU.subtract).then_inc(sem[name], 1)

            def rows(b):
                return bank[b][0:HT, 0:2 * D].rearrange("p (t d) -> p t d", t=2)

            def step(m, n, l, head, front, back, again):
                def cols_lo(dst, b, made, image, name):
                    ve.wait_ge(sem[made], after(made, image))
                    ve.tensor_tensor(dst[:, 1], bank[b][:, 0:T], dst[:, 0].bitcast(F32),
                                     ALU.subtract)
                    ve.tensor_tensor(dst[64:128, 2], bank[b][0:64, T:2 * T],
                                     dst[0:64, 2].bitcast(F32),
                                     ALU.subtract).then_inc(sem[name], 1)

                def attention_cols_lo():
                    cols_lo(aT, 1, "aT_sb", l, "aTs_sb")

                def routed_cols():
                    ve.wait_ge(sem["nT_sb"], after("nT_sb", m))
                    split_cols(nTs, nT, "nTs_sb")

                def query_parts():
                    ve.wait_ge(sem["qhi_sb"], after("qhi_sb", n))
                    for b, g0, gn in ((0, 0, 2), (1, 2, 1)):
                        last = ve.scalar_tensor_tensor(
                            qparts[:, g0:g0 + gn].rearrange("p g t -> p (g t)"),
                            qhi[:, g0:g0 + gn].rearrange("p g t -> p (g t)").bitcast(F32),
                            lo_rows[:], bank[b][:, 0:gn * T], ALU.mult, ALU.add)
                    last.then_inc(sem["qparts_sb"], 1)
                    ve.drain()

                def slot_queries(s):
                    at = slice(32 * s, 32 * s + 32)
                    ve.tensor_copy(qz[at, s], qparts[at].bitcast(F32)).then_inc(sem["qz_sb"], 1)

                def keys():
                    ve.wait_ge(sem["khi_sb"], after("khi_sb", n))
                    for b, g0, gn in ((2, 0, 2), (3, 2, 1)):
                        last = ve.tensor_tensor(
                            klo[:, g0:g0 + gn].rearrange("p g t -> p (g t)"), bank[b][:, 0:gn * T],
                            khi[:, g0:g0 + gn].rearrange("p g t -> p (g t)").bitcast(F32),
                            ALU.subtract)
                    last.then_inc(sem["klo_sb"], 1)

                def maxima(k):
                    ve.wait_ge(sem["s_mm"], after("s_mm", n, k + 1))
                    b, s = RING[f"S{k}"], k // 2
                    parts = ([(1, 0, 2, 0, T)] if k % 2 else
                             [(1, 2, 1, 0, T), (0, 0, 3, T, HT)])
                    for t, g, gn, c0, w in parts:
                        last = ve.tensor_reduce(
                            negmax[:, s, t, g:g + gn],
                            bank[b][0:HT, c0:c0 + w * gn].rearrange("p (h w) -> p h w", w=w),
                            AX.X, ALU.max, negate=True)
                    last.then_inc(sem["rowmax"], 1)

                def transposed(name):
                    ve.wait_ge(sem["p_T"], after("p_T", n, PT.index(name) + 1))
                    ve.tensor_copy(pt_dst(name[0], int(name[1:])),
                                   bank[RING[name]][0:HT, 0:4 * HT]).then_inc(sem["pT_dve"], 1)

                def inverse_sums(s):
                    ve.wait_ge(sem["probs"], after("probs", n, 2 * s + 2))
                    ve.reciprocal(rden[:, s], den[:, s]).then_inc(sem["rden_sb"], 1)

                tok_bank = RING["T0"]
                tok = bank[tok_bank][0:HT, 0:2 * (D + 1)].rearrange("p (t d) -> p t d", t=2)

                def patch_variance():
                    ve.wait_ge(sem["tok_mm"], after("tok_mm", l))
                    ve.tensor_scalar(mean1[:], tok[:, :, D], 1.0 / PD, None, ALU.mult)
                    ve.drain()
                    ve.tensor_tensor(msq1[:], mean1[:], mean1[:], ALU.mult)
                    ve.drain()
                    ve.scalar_tensor_tensor(var1[:], bank[tok_bank][0:HT, 2 * D + 2:2 * D + 4],
                                            1.0 / PD, msq1[:], ALU.mult,
                                            ALU.subtract).then_inc(sem["tok_var"], 1)

                def embedding():
                    ve.wait_ge(sem["tok_rstd"], after("tok_rstd", l))
                    for t in range(2):
                        last = ve.scalar_tensor_tensor(y_row[:, t], tok[:, t, 0:D],
                                                       rstd1[:, t:t + 1], tok_bias[:], ALU.mult,
                                                       ALU.add)
                    last.then_inc(sem["tok_y"], 1)
                    ve.drain()
                    stats(y_row, bn_y, mv_y, "y_stat")

                def embedding_normalised():
                    ve.wait_ge(sem["y_rstd"], after("y_rstd", l))
                    normalise(y_row, y_row, mv_y, rstd2, "y_norm")

                def h1_stats():
                    ve.wait_ge(sem["h1_sb"], after("h1_sb", l))
                    stats(h1, bn_a, mv_a, "h1_stat")

                def attention_input():
                    ve.wait_ge(sem["h1_rstd"], after("h1_rstd", l))
                    normalise(a_row, h1, mv_a, rstd3, "a_sb")

                def routing_scores():
                    ve.wait_ge(sem["score_mm"], after("score_mm", m))
                    ve.tensor_scalar(zrow[:], bank[6][:, 0:T], br[:], None,
                                     ALU.add).then_inc(sem["z_sb"], 1)

                def rank_tokens():
                    ve.drain()
                    ve.tensor_scalar(zclip[:], zrow[:], TOPZ, -88.0, ALU.min, ALU.max)
                    ve.drain()
                    for t in range(2):
                        ve.tensor_tensor_reduce(scr[0:HT, t, 0:HT], zclip[0:HT, HT * t:HT * t + HT],
                                                ident[0:HT, 0:HT], 1.0, 0.0, ALU.mult, ALU.add,
                                                zi[:, t:t + 1])
                    ve.drain()
                    for t in range(2):
                        hi, lo = (t + 1) * HT, t * HT
                        ve.scalar_tensor_tensor(scr[0:HT, t, 0:hi], zclip[0:HT, 0:hi],
                                                zi[:, t:t + 1], before[:, t, 0:hi], ALU.is_le,
                                                ALU.mult, accum_out=cnt[:, 0, t:t + 1])
                        ve.scalar_tensor_tensor(scr[0:HT, 2 + t, lo:T], zclip[0:HT, lo:T],
                                                zi[:, t:t + 1], notbefore[:, t, lo:T], ALU.is_lt,
                                                ALU.mult, accum_out=cnt[:, 1, t:t + 1])
                    ve.drain()
                    ve.tensor_tensor(rank[:], cnt[:, 0], cnt[:, 1], ALU.add)
                    ve.drain()
                    ve.tensor_scalar(keep[:], rank[:], NSEL - 0.5, None, ALU.is_ge)
                    for t in range(2):
                        last = ve.tensor_scalar(sel[:, t], iota32[:], rank[:, t:t + 1], None,
                                                ALU.is_equal)
                    last.then_inc(sem["sel_sb"], 1)

                def sigmoid():
                    ve.wait_ge(sem["expz"], after("expz", m))
                    ve.tensor_scalar(ez[:], ez[:], 1.0, None, ALU.add)
                    ve.drain()
                    ve.reciprocal(sig[:], ez[:])

                def pool_tokens():
                    ve.drain()
                    ve.tensor_scalar(scr[:, 2], sig[:], 1.0, None, ALU.mult, ALU.add,
                                     accum_out=ssum[:])
                    for chunk, (lo, hi) in enumerate(KC):
                        size = hi - lo
                        ve.tensor_tensor_reduce(scr[0:size, chunk], nT[0:size, chunk], sig[0:size], 1.0,
                                                0.0, ALU.mult, ALU.add,
                                                pool_raw[0:size, chunk:chunk + 1])
                    ve.drain()
                    ve.tensor_scalar(sse[:], ssum[:], 1e-6, None, ALU.add)
                    ve.drain()
                    ve.reciprocal(rss[:], sse[:])

                def mix_pooled():
                    ve.drain()
                    for chunk, (lo, hi) in enumerate(KC):
                        size = hi - lo
                        ve.tensor_scalar(pooled[0:size, chunk:chunk + 1],
                                         pool_raw[0:size, chunk:chunk + 1], rss[0:size], None, ALU.mult)
                    ve.drain()
                    for chunk, (lo, hi) in enumerate(KC):
                        size = hi - lo
                        ve.scalar_tensor_tensor(mT[0:size, chunk], sig[0:size],
                                                pooled[0:size, chunk:chunk + 1],
                                                nT[0:size, chunk], ALU.mult, ALU.add)

                def mix_cols():
                    ve.drain()
                    split_cols(mTs, mT, "mTs_sb")

                def q_blocks():
                    ve.wait_ge(sem["qs_sb"], after("qs_sb", m))
                    ve.tensor_tensor(qb0[:], qs[:, 0:1].broadcast_to([128, 8, SELP]),
                                     slot_of[:].unsqueeze(2).broadcast_to([128, 8, SELP]),
                                     ALU.mult)
                    ve.tensor_tensor(qb1[:], qs[0:64, 1:2].broadcast_to([64, 4, SELP]),
                                     slot_of[0:64, 0:4].unsqueeze(2).broadcast_to([64, 4, SELP]),
                                     ALU.mult).then_inc(sem["qb_sb"], 1)

                def max2():
                    ve.wait_ge(sem["s2_mm"], after("s2_mm", m))
                    ve.tensor_reduce(negmax2[:, 0:2],
                                     bank[5][:, 0:2 * T].rearrange("p (g t) -> p g t", g=2), AX.X,
                                     ALU.max, negate=True)
                    ve.tensor_reduce(negmax2[:, 2:3], bank[4][:, 0:T], AX.X, ALU.max,
                                     negate=True).then_inc(sem["max2"], 1)

                def context2():
                    ve.wait_ge(sem["probs2"], after("probs2", m))
                    ve.reciprocal(rden2[:], den2[:])
                    ve.drain()
                    ve.wait_ge(sem["ctx_mm"], after("ctx_mm", m))
                    for g in range(NG):
                        last = ve.scalar_tensor_tensor(
                            ctxm[:, g], bank[5][:, 64 * g:64 * g + 64], rden2[:, g:g + 1],
                            diag_of[:].rearrange("p h e -> p (h e)"), ALU.mult, ALU.mult)
                    last.then_inc(sem["ctx_sb"], 1)

                def context2_cols():
                    ve.wait_ge(sem["ctxT_mm"], after("ctxT_mm", m))
                    for chunk, (lo, hi) in enumerate(KC):
                        size = hi - lo
                        last = ve.tensor_scalar(ctxT[0:size, chunk],
                                                bank[4][0:size, SELP * chunk:SELP * (chunk + 1)],
                                                fbv[0:size, chunk:chunk + 1], None, ALU.add)
                    last.then_inc(sem["ctxT_sb"], 1)

                def attn_out():
                    ve.wait_ge(sem["ao_mm"], after("ao_mm", m))
                    ve.tensor_tensor(ao[:], bank[6][0:SELP, 0:D], fbo[:],
                                     ALU.add).then_inc(sem["ao_sb"], 1)

                def mix():
                    ve.wait_ge(sem["mix_mm"], after("mix_mm", m))
                    ve.wait_ge(sem["f1b_sb"], after("f1b_sb", m))
                    for t in range(2):
                        ve.scalar_tensor_tensor(f1[:, t], rows(7)[:, t], keep[:, t:t + 1],
                                                f1[:, t], ALU.mult, ALU.add)

                def merge():
                    ve.drain()
                    ve.wait_ge(sem["scat_mm"], after("scat_mm", m))
                    ve.tensor_tensor(h3[:], rows(5), f1[:], ALU.add).then_inc(sem["h3_sb"], 1)
                    ve.drain()
                    stats(h3, bn_3, mv_3, "h3_stat")

                def attention():
                    for i, (g0, gn) in enumerate(((0, 2), (2, 1))):
                        ve.wait_ge(sem["yhi_sb"], after("yhi_sb", n, i + 1))
                        ve.scalar_tensor_tensor(
                            yparts[:, g0:g0 + gn].rearrange("p g t -> p (g t)"),
                            yhi[:, g0:g0 + gn].rearrange("p g t -> p (g t)").bitcast(F32),
                            lo_rows[:], bank[2 + i][:, 0:gn * T], ALU.mult,
                            ALU.add).then_inc(sem["yparts_sb"], 1)

                def mlp_input():
                    ve.wait_ge(sem["h3_rstd"], after("h3_rstd", m))
                    normalise(z3, h3, mv_3, rstd5, "z3_sb")

                def mlp_cols_lo():
                    cols_lo(z3Ts, 6, "z3T_sb", m, "z3Ts_sb")

                def gelu_parts(j):
                    ve.wait_ge(sem["gelu_sb"], after("gelu_sb", m, j + 1))
                    at = slice(2 * j, 2 * j + 2)
                    ve.tensor_copy(gparts[:, 0, at], gT[:, at])
                    ve.drain()
                    ve.tensor_tensor(gparts[:, 1, at], gT[:, at], gparts[:, 0, at].bitcast(F32),
                                     ALU.subtract).then_inc(sem["gparts_sb"], 1)

                def residual():
                    ve.wait_ge(sem["proj_mm"], after("proj_mm", n))
                    ve.wait_ge(sem["h1b_sb"], after("h1b_sb", n))
                    if back:
                        ve.wait_ge(sem["res_sb"], all_before("res_sb", n))
                    ve.tensor_tensor(h2[:], rows(0), h1b[:], ALU.add).then_inc(sem["h2_sb"], 1)
                    ve.drain()
                    stats(h2, bn_f, mv_f, "h2_stat")

                def routed_input():
                    ve.wait_ge(sem["h2_rstd"], after("h2_rstd", n))
                    normalise(z0, h2, mv_f, vf[:, 5], "z0_sb")
                    normalise(f0, h2, mv_f, vf[:, 1], "f0_sb")

                def output():
                    ve.wait_ge(sem["down_mm"], after("down_mm", m))
                    ve.wait_ge(sem["res_sb"], after("res_sb", m))
                    if again:
                        ve.wait_ge(sem["out_done"], all_before("out_done", m))
                    ve.tensor_tensor(out_row[:], rows(6), res[:], ALU.add).then_inc(sem["out_sb"], 1)

                if back:
                    routed_cols()
                if front:
                    query_parts()
                    slot_queries(0)
                    slot_queries(1)
                    keys()
                if back:
                    routing_scores()
                    rank_tokens()
                if front:
                    maxima(0)
                    maxima(1)
                    maxima(2)
                if back:
                    sigmoid()
                    pool_tokens()
                if front:
                    inverse_sums(0)
                    maxima(3)
                    maxima(4)
                    maxima(5)
                if back:
                    q_blocks()
                    mix_pooled()
                if front:
                    maxima(6)
                    inverse_sums(1)
                if back:
                    max2()
                if head:
                    patch_variance()
                if front:
                    maxima(7)
                    inverse_sums(2)
                if head:
                    embedding()
                if front:
                    transposed("A0")
                    inverse_sums(3)
                if back:
                    mix_cols()
                    context2()
                if head:
                    embedding_normalised()
                if back:
                    context2_cols()
                if front:
                    transposed("A2")
                if back:
                    mix()
                    attn_out()
                if front:
                    transposed("A3")
                if head:
                    h1_stats()
                if back:
                    merge()
                if head:
                    attention_input()
                if back:
                    mlp_input()
                if front:
                    attention()
                if back:
                    mlp_cols_lo()
                if front:
                    residual()
                if back:
                    gelu_parts(0)
                    gelu_parts(1)
                if head:
                    attention_cols_lo()
                if back:
                    gelu_parts(2)
                if front:
                    routed_input()
                if back:
                    output()
            steps(ve, step)

        @block.scalar
        def _(sc):
            sc.wait_ge(one["zeroed"], 1)
            for dst, src in by_act:
                sc.dma_start(dst, src).then_inc(one["w_in_act"], 16)
            sc.wait_ge(one["p1_zeroed"], 1)

            def affine_cols(dst, b, name, scale, bias, width=T):
                for chunk, (lo, hi) in enumerate(KC):
                    size = hi - lo
                    last = sc.activation(
                        dst[0:size, chunk], bank[b][0:size, chunk * width:(chunk + 1) * width],
                        ACT.Identity, bias=bias[0:size, chunk:chunk + 1],
                        scale=scale[0:size, chunk:chunk + 1] if not isinstance(scale, float)
                        else scale)
                if name:
                    last.then_inc(sem[name], 1)

            def step(m, n, l, head, front, back, again):
                def cols_hi(dst, b, made, image, name):
                    sc.wait_ge(sem[made], after(made, image))
                    sc.copy(dst[:, 0], bank[b][:, 0:T])
                    sc.copy(dst[0:64, 2], bank[b][0:64, T:2 * T]).then_inc(sem[name], 1)

                def attention_cols_hi():
                    cols_hi(aT, 1, "aT_mm", l, "aT_sb")

                def routed_cols():
                    sc.wait_ge(sem["zT_mm"], after("zT_mm", m))
                    affine_cols(nT, 5, "nT_sb", g1, b1)

                def group_hi(dst, b0, made, name):
                    sc.wait_ge(sem[made], after(made, n))
                    for b, g0, gn in ((b0, 0, 2), (b0 + 1, 2, 1)):
                        last = sc.copy(dst[:, g0:g0 + gn].rearrange("p g t -> p (g t)"),
                                       bank[b][:, 0:gn * T])
                    last.then_inc(sem[name], 1)

                def queries():
                    group_hi(qhi, 0, "q_mm", "qhi_sb")

                def keys():
                    group_hi(khi, 2, "k_mm", "khi_sb")

                def load_table(function):
                    sc.activation(table_out[:], ones[0:1, 0:1], function)

                def squares():
                    sc.wait_ge(sem["x_in"], after("x_in", l))
                    if front:
                        sc.wait_ge(sem["sqsum_sb"], all_before("sqsum_sb", l))
                    xv = x_sb[0:KX].rearrange("p h (w q) -> p (h w) q", q=PS)
                    sc.activation(x_sq[:], xv[:, :, 0:QH], ACT.Square).then_inc(sem["sq_sb"], 1)

                def values():
                    sc.wait_ge(sem["v_mm"], after("v_mm", n))
                    sc.copy(v_sb[0:HT].rearrange("p t h (r e) -> p (t h) r e", e=DH),
                            bank[4][0:HT, 0:2 * D].rearrange("p (h e) -> p h e", e=DH).unsqueeze(
                                2).broadcast_to([HT, 2 * NH, 2, DH])
                            ).then_inc(sem["v_sb"], 1)

                def softmax(k):
                    sc.wait_ge(sem["rowmax"], after("rowmax", n, k + 1))
                    b = RING[f"S{k}"]
                    s, heads = s_unit(k)
                    for g, t, c0 in heads:
                        sc.activation((p1 if t else p0)[0:HT, 3 * s + g],
                                      bank[b][0:HT, c0:c0 + (T if t else HT)],
                                      ACT.Exp, bias=negmax[:, s, t, g:g + 1],
                                      accum_out=den[:, s, t, g:g + 1])
                    sc.drain().then_inc(sem["probs"], 1)

                def transposed(name):
                    sc.wait_ge(sem["p_T"], after("p_T", n, PT.index(name) + 1))
                    sc.copy(pt_dst(name[0], int(name[1:])),
                            bank[RING[name]][0:HT, 0:4 * HT]).then_inc(sem["pT_act"], 1)

                def exp_scores():
                    sc.wait_ge(sem["z_sb"], after("z_sb", m))
                    sc.activation(ez[:], zrow[:], ACT.Exp, scale=-1.0).then_inc(sem["expz"], 1)

                def keys_values2():
                    sc.wait_ge(sem["kk_mm"], after("kk_mm", m))
                    affine_cols(kk, 7, "kk_sb", 1.0, fbk)
                    sc.wait_ge(sem["vv_mm"], after("vv_mm", m))
                    sc.copy(vv[:].rearrange("p t d -> p (t d)"),
                            bank[5][0:HT, 0:2 * D]).then_inc(sem["vv_sb"], 1)

                def gathered():
                    sc.wait_ge(sem["gather_mm"], after("gather_mm", m))
                    affine_cols(nsel, 6, None, g1, b1, SELP)
                    sc.copy(selT[:], bank[6][0:SELP, 64:64 + T]).then_inc(sem["nsel_sb"], 1)

                def queries2():
                    sc.wait_ge(sem["qsel_mm"], after("qsel_mm", m))
                    affine_cols(qs, 7, "qs_sb", QSCALE, fbqs, SELP)

                def softmax2():
                    sc.wait_ge(sem["max2"], after("max2", m))
                    for g in range(NG):
                        src = bank[5][:, T * g:T * g + T] if g < 2 else bank[4][:, 0:T]
                        sc.activation(probs2[:, g], src, ACT.Exp, bias=negmax2[:, g:g + 1],
                                      accum_out=den2[:, g:g + 1])
                    sc.drain().then_inc(sem["probs2"], 1)

                def transposed2():
                    sc.wait_ge(sem["p2_T"], after("p2_T", m))
                    for t in range(2):
                        last = sc.copy(p2T[:, t], bank[6 + t][0:HT, 0:NG * 128])
                    last.then_inc(sem["p2T_sb"], 1)

                def attention():
                    for i, (g0, gn) in enumerate(((0, 2), (2, 1))):
                        sc.wait_ge(sem["y_mm"], after("y_mm", n, i + 1))
                        sc.copy(yhi[:, g0:g0 + gn].rearrange("p g t -> p (g t)"),
                                bank[2 + i][:, 0:gn * T]).then_inc(sem["yhi_sb"], 1)

                def mlp_cols_hi():
                    cols_hi(z3Ts, 6, "z3_T", m, "z3T_sb")

                def gelu(j):
                    sc.wait_ge(sem["up_mm"], after("up_mm", m, j + 1))
                    for i in range(2):
                        f = 2 * j + i
                        last = sc.activation(gT[:, f], bank[(4, 5, 7)[j]][:, T * i:T * i + T],
                                             ACT.Gelu, bias=bf1[:, f:f + 1])
                    last.then_inc(sem["gelu_sb"], 1)

                if back:
                    routed_cols()
                if front:
                    queries()
                    load_table(ACT.Exp)
                    keys()
                    values()
                if back:
                    exp_scores()
                    keys_values2()
                if head:
                    squares()
                if front:
                    softmax(0)
                    softmax(1)
                if back:
                    gathered()
                if front:
                    softmax(2)
                if back:
                    queries2()
                if front:
                    softmax(3)
                    softmax(4)
                    softmax(5)
                    softmax(6)
                if back:
                    softmax2()
                if front:
                    softmax(7)
                if back:
                    transposed2()
                if front:
                    transposed("A1")
                    transposed("B0")
                    transposed("B1")
                    transposed("A4")
                    transposed("A5")
                    transposed("B2")
                    attention()
                if back:
                    mlp_cols_hi()
                    load_table(ACT.Gelu)
                if head:
                    attention_cols_hi()
                if back:
                    gelu(0)
                    gelu(1)
                    gelu(2)
            steps(sc, step)


def kernel(**inputs):
    import numpy as _np
    import concourse.bacc as _bacc
    from concourse import mybir as _mybir
    from concourse.bass_utils import run_bass_kernel_spmd as _run

    nc = _bacc.Bacc("TRN2", target_bir_lowering=False, num_devices=1)
    arrays, args = {}, {}
    for name, a in inputs.items():
        a = _np.ascontiguousarray(a)
        if a.ndim == 0:
            a = a.reshape(1)
        arrays[f"in_{name}"] = a
        args[name] = nc.dram_tensor(f"in_{name}", a.shape, _mybir.dt.from_np(a.dtype),
                                    kind="ExternalInput").ap()
    y = nc.dram_tensor("out_0", (B, T, D), _mybir.dt.float32, kind="ExternalOutput").ap()
    build(nc, args, y)
    r = _run(nc, [arrays], core_ids=[0])
    return r.results[0]["out_0"]
```
